# Optimizing a Trainium2 kernel written in Bass

```python
import numpy as np
import jax
import jax.numpy as jnp

def _softmax(x, axis=-1):
    return jax.nn.softmax(x, axis=axis)

def _gelu(x):
    return jax.nn.gelu(x, approximate=True)

def _silu(x):
    return jax.nn.silu(x)

def _sigmoid(x):
    return jax.nn.sigmoid(x)

def _layernorm(x, axis=-1, eps=1e-05):
    m = jnp.mean(x, axis=axis, keepdims=True)
    v = jnp.var(x, axis=axis, keepdims=True)
    return (x - m) / jnp.sqrt(v + eps)

def _scatter_add(tgt, idx, src, axis=0):
    return tgt.at[idx].add(src)

def _segment_sum(src, seg, n):
    return jax.ops.segment_sum(src, seg, n)
kernel_name = 'mk_gnn_preln_d4_gnn_r16_2e2a41'

def setup_inputs(seed: int=0):
    np.random.seed(seed)
    _w = jnp.asarray

    def _rec_inputs():
        import jax
        import jax.numpy as jnp
        _gk = jax.random.key(seed)
        x = -0.0001126 + 1 * jax.random.normal(jax.random.fold_in(_gk, 1), (625, 768), jnp.float32)
        src = jax.random.randint(jax.random.fold_in(_gk, 2), (10000,), 0, 625, jnp.int32)
        dst = jax.random.randint(jax.random.fold_in(_gk, 3), (10000,), 0, 625, jnp.int32)
        _o = jnp.argsort(dst, stable=True)
        src = src[_o]
        dst = dst[_o]
        edge_type_3 = jax.random.randint(jax.random.fold_in(_gk, 12), (10000,), 0, 3, jnp.int32)
        node_type_3 = jax.random.randint(jax.random.fold_in(_gk, 13), (625,), 0, 3, jnp.int32)
        return (x, src, dst, edge_type_3, node_type_3)
    x, src, dst, edge_type_3, node_type_3 = _rec_inputs()

    def _L0_gnn_setup():
        import jax, jax.numpy as jnp
        import numpy as np
        N_NODES = 625
        N_EDGES = 5000
        IN_DIM, HID, OUT_DIM, HEADS = (768, 512, 768, 4)
        NEG_SLOPE = 0.2

        def _gat_layer(x, src, dst, W, a_src, a_dst, b, heads, d_out, concat):
            N = x.shape[0]
            h = (x @ W).reshape(N, heads, d_out)
            as_n = jnp.einsum('nhd,hd->nh', h, a_src)
            ad_n = jnp.einsum('nhd,hd->nh', h, a_dst)
            e = jax.nn.leaky_relu(as_n[src] + ad_n[dst], NEG_SLOPE)
            e_max = jax.lax.stop_gradient(jax.ops.segment_max(e, dst, num_segments=N))
            ex = jnp.exp(e - e_max[dst])
            denom = jax.ops.segment_sum(ex, dst, num_segments=N)
            alpha = ex / (denom[dst] + 1e-16)
            msg = alpha[:, :, None] * h[src]
            out = jax.ops.segment_sum(msg, dst, num_segments=N)
            out = out.reshape(N, heads * d_out) if concat else out.mean(axis=1)
            return out + b
        key = jax.random.key(seed)
        ks = jax.random.split(key, 10)
        g = 0.05
        return {'x': jax.random.normal(ks[0], (N_NODES, IN_DIM), jnp.float32), 'edge_index': jax.random.randint(ks[1], (2, N_EDGES), 0, N_NODES, jnp.int64), 'W1': jax.random.normal(ks[2], (IN_DIM, HEADS * HID), jnp.float32) * g, 'a1_src': jax.random.normal(ks[3], (HEADS, HID), jnp.float32) * g, 'a1_dst': jax.random.normal(ks[4], (HEADS, HID), jnp.float32) * g, 'b1': jnp.zeros((HEADS * HID,), jnp.float32), 'W2': jax.random.normal(ks[5], (HEADS * HID, OUT_DIM), jnp.float32) * g, 'a2_src': jax.random.normal(ks[6], (1, OUT_DIM), jnp.float32) * g, 'a2_dst': jax.random.normal(ks[7], (1, OUT_DIM), jnp.float32) * g, 'b2': jnp.zeros((OUT_DIM,), jnp.float32)}
    _L0_gnn_all = _L0_gnn_setup()
    _L0_gnn_in = {k: v for k, v in _L0_gnn_all.items() if k in ('W1', 'a1_src', 'a1_dst', 'b1', 'W2', 'a2_src', 'a2_dst', 'b2')}
    del _L0_gnn_all

    def _L1_gnn_setup():
        import jax, jax.numpy as jnp
        import numpy as np
        N_NODES = 625
        N_EDGES = 10000
        NEG_SLOPE = 0.2

        def _gat_layer(x, src, dst, W, a_src, a_dst, bias, concat):
            N = x.shape[0]
            H, C = a_src.shape
            h = (x @ W).reshape(N, H, C)
            al_s = jnp.einsum('nhc,hc->nh', h, a_src)
            al_d = jnp.einsum('nhc,hc->nh', h, a_dst)
            e = jax.nn.leaky_relu(al_s[src] + al_d[dst], NEG_SLOPE)
            m = jax.ops.segment_max(e, dst, num_segments=N)
            ex = jnp.exp(e - m[dst])
            denom = jax.ops.segment_sum(ex, dst, num_segments=N)
            alpha = ex / (denom[dst] + 1e-16)
            msg = h[src] * alpha[:, :, None]
            out = jax.ops.segment_sum(msg, dst, num_segments=N)
            out = out.reshape(N, H * C) if concat else out.mean(axis=1)
            return out + bias
        key = jax.random.key(seed)
        ks = jax.random.split(key, 10)
        in_dim, hid, out_dim, heads = (768, 512, 768, 4)
        x = jax.random.normal(ks[0], (N_NODES, in_dim), dtype=jnp.float32)
        edge_index = jax.random.randint(ks[1], (2, N_EDGES), 0, N_NODES, dtype=jnp.int64)
        g = lambda k, shape, fan: jax.random.normal(k, shape, jnp.float32) / np.sqrt(fan)
        return {'x': x, 'edge_index': edge_index, 'W1': g(ks[2], (in_dim, heads * hid), in_dim), 'att_src1': g(ks[3], (heads, hid), hid), 'att_dst1': g(ks[4], (heads, hid), hid), 'b1': jnp.zeros((heads * hid,), jnp.float32), 'W2': g(ks[5], (heads * hid, out_dim), heads * hid), 'att_src2': g(ks[6], (1, out_dim), out_dim), 'att_dst2': g(ks[7], (1, out_dim), out_dim), 'b2': jnp.zeros((out_dim,), jnp.float32)}
    _L1_gnn_all = _L1_gnn_setup()
    _L1_gnn_in = {k: v for k, v in _L1_gnn_all.items() if k in ('W1', 'att_src1', 'att_dst1', 'b1', 'W2', 'att_src2', 'att_dst2', 'b2')}
    del _L1_gnn_all

    def _L2_gnn_setup():
        import jax, jax.numpy as jnp
        import numpy as np
        NUM_NODES = 625
        NUM_EDGES = 10000
        IN_CH = 768
        TYPE_DIM = 128
        HID = 768
        OUT = 768
        NUM_REL = 3
        NUM_NODE_TYPE = 3

        def _glorot(key, shape):
            fan_in, fan_out = (shape[-2], shape[-1])
            lim = (6.0 / (fan_in + fan_out)) ** 0.5
            return jax.random.uniform(key, shape, jnp.float32, -lim, lim)

        def rgcn_conv(h, src, dst, edge_type, w_rel, w_root, bias):
            num_nodes = h.shape[0]
            xw = jnp.einsum('nd,rde->rne', h, w_rel)
            msg = xw[edge_type, src]
            onehot = jax.nn.one_hot(edge_type, NUM_REL, dtype=h.dtype)
            count = jax.ops.segment_sum(onehot, dst, num_segments=num_nodes)
            inv = jnp.where(count > 0, 1.0 / jnp.maximum(count, 1.0), 0.0)
            msg = msg * inv[dst, edge_type][:, None]
            agg = jax.ops.segment_sum(msg, dst, num_segments=num_nodes)
            return agg + h @ w_root + bias
        key = jax.random.key(seed)
        ks = jax.random.split(key, 16)
        d1 = IN_CH + TYPE_DIM
        inp = {'x': jax.random.normal(ks[0], (NUM_NODES, IN_CH), jnp.float32), 'node_type': jax.random.randint(ks[1], (NUM_NODES,), 0, NUM_NODE_TYPE, jnp.int32), 'edge_index': jax.random.randint(ks[2], (2, NUM_EDGES), 0, NUM_NODES, jnp.int32), 'edge_type': jax.random.randint(ks[3], (NUM_EDGES,), 0, NUM_REL, jnp.int32), 'node_emb': jax.random.normal(ks[4], (NUM_NODE_TYPE, TYPE_DIM), jnp.float32), 'w_rel1': _glorot(ks[5], (NUM_REL, d1, d1)), 'w_root1': _glorot(ks[6], (d1, d1)), 'b1': jnp.zeros((d1,), jnp.float32), 'w_rel2': _glorot(ks[7], (NUM_REL, d1, HID)), 'w_root2': _glorot(ks[8], (d1, HID)), 'b2': jnp.zeros((HID,), jnp.float32), 'w_rel3': _glorot(ks[9], (NUM_REL, HID, OUT)), 'w_root3': _glorot(ks[10], (HID, OUT)), 'b3': jnp.zeros((OUT,), jnp.float32)}
        return inp
    _L2_gnn_all = _L2_gnn_setup()
    _L2_gnn_in = {k: v for k, v in _L2_gnn_all.items() if k in ('node_emb', 'w_rel1', 'w_root1', 'b1', 'w_rel2', 'w_root2', 'b2', 'w_rel3', 'w_root3', 'b3')}
    del _L2_gnn_all

    def _L3_gnn_setup():
        import jax, jax.numpy as jnp
        import numpy as np
        N = 1250
        E_RAND = 20000
        NEG_SLOPE = 0.2

        def gat_layer(x, W, a_src, a_dst, bias, src, dst, heads, out_c, concat):
            n = x.shape[0]
            h = (x @ W).reshape(n, heads, out_c)
            al_s = jnp.einsum('nhc,hc->nh', h, a_src)
            al_d = jnp.einsum('nhc,hc->nh', h, a_dst)
            e = jax.nn.leaky_relu(al_s[src] + al_d[dst], NEG_SLOPE)
            m = jax.ops.segment_max(e, dst, num_segments=n)
            ex = jnp.exp(e - m[dst])
            z = jax.ops.segment_sum(ex, dst, num_segments=n)
            alpha = ex / (z[dst] + 1e-16)
            msg = h[src] * alpha[:, :, None]
            out = jax.ops.segment_sum(msg, dst, num_segments=n)
            out = out.reshape(n, heads * out_c) if concat else out.mean(axis=1)
            return out + bias
        key = jax.random.key(seed)
        ks = jax.random.split(key, 10)
        x = jax.random.normal(ks[0], (N, 768), dtype=jnp.float32)
        src = jax.random.randint(ks[1], (E_RAND,), 0, N)
        dst = jax.random.randint(ks[2], (E_RAND,), 0, N)
        loop = jnp.arange(N)
        edge_index = jnp.stack([jnp.concatenate([src, loop]), jnp.concatenate([dst, loop])])
        s = 1.0 / np.sqrt(768.0)
        W1 = jax.random.normal(ks[3], (768, 768), dtype=jnp.float32) * s
        a_src1 = jax.random.normal(ks[4], (8, 96), dtype=jnp.float32) * 0.1
        a_dst1 = jax.random.normal(ks[5], (8, 96), dtype=jnp.float32) * 0.1
        b1 = jnp.zeros((768,), dtype=jnp.float32)
        W2 = jax.random.normal(ks[6], (768, 768), dtype=jnp.float32) * s
        a_src2 = jax.random.normal(ks[7], (1, 768), dtype=jnp.float32) * 0.1
        a_dst2 = jax.random.normal(ks[8], (1, 768), dtype=jnp.float32) * 0.1
        b2 = jnp.zeros((768,), dtype=jnp.float32)
        return {'x': x, 'edge_index': edge_index, 'W1': W1, 'a_src1': a_src1, 'a_dst1': a_dst1, 'b1': b1, 'W2': W2, 'a_src2': a_src2, 'a_dst2': a_dst2, 'b2': b2}
    _L3_gnn_all = _L3_gnn_setup()
    _L3_gnn_in = {k: v for k, v in _L3_gnn_all.items() if k in ('W1', 'a_src1', 'a_dst1', 'b1', 'W2', 'a_src2', 'a_dst2', 'b2')}
    del _L3_gnn_all
    return {'x': x, 'src': src, 'dst': dst, 'edge_type_3': edge_type_3, 'node_type_3': node_type_3, 'L0_gnn_W1': _L0_gnn_in['W1'], 'L0_gnn_a1_src': _L0_gnn_in['a1_src'], 'L0_gnn_a1_dst': _L0_gnn_in['a1_dst'], 'L0_gnn_b1': _L0_gnn_in['b1'], 'L0_gnn_W2': _L0_gnn_in['W2'], 'L0_gnn_a2_src': _L0_gnn_in['a2_src'], 'L0_gnn_a2_dst': _L0_gnn_in['a2_dst'], 'L0_gnn_b2': _L0_gnn_in['b2'], 'L1_gnn_W1': _L1_gnn_in['W1'], 'L1_gnn_att_src1': _L1_gnn_in['att_src1'], 'L1_gnn_att_dst1': _L1_gnn_in['att_dst1'], 'L1_gnn_b1': _L1_gnn_in['b1'], 'L1_gnn_W2': _L1_gnn_in['W2'], 'L1_gnn_att_src2': _L1_gnn_in['att_src2'], 'L1_gnn_att_dst2': _L1_gnn_in['att_dst2'], 'L1_gnn_b2': _L1_gnn_in['b2'], 'L2_gnn_node_emb': _L2_gnn_in['node_emb'], 'L2_gnn_w_rel1': _L2_gnn_in['w_rel1'], 'L2_gnn_w_root1': _L2_gnn_in['w_root1'], 'L2_gnn_b1': _L2_gnn_in['b1'], 'L2_gnn_w_rel2': _L2_gnn_in['w_rel2'], 'L2_gnn_w_root2': _L2_gnn_in['w_root2'], 'L2_gnn_b2': _L2_gnn_in['b2'], 'L2_gnn_w_rel3': _L2_gnn_in['w_rel3'], 'L2_gnn_w_root3': _L2_gnn_in['w_root3'], 'L2_gnn_b3': _L2_gnn_in['b3'], 'L3_gnn_W1': _L3_gnn_in['W1'], 'L3_gnn_a_src1': _L3_gnn_in['a_src1'], 'L3_gnn_a_dst1': _L3_gnn_in['a_dst1'], 'L3_gnn_b1': _L3_gnn_in['b1'], 'L3_gnn_W2': _L3_gnn_in['W2'], 'L3_gnn_a_src2': _L3_gnn_in['a_src2'], 'L3_gnn_a_dst2': _L3_gnn_in['a_dst2'], 'L3_gnn_b2': _L3_gnn_in['b2']}

def reference(x, src, dst, edge_type_3, node_type_3, L0_gnn_W1, L0_gnn_a1_src, L0_gnn_a1_dst, L0_gnn_b1, L0_gnn_W2, L0_gnn_a2_src, L0_gnn_a2_dst, L0_gnn_b2, L1_gnn_W1, L1_gnn_att_src1, L1_gnn_att_dst1, L1_gnn_b1, L1_gnn_W2, L1_gnn_att_src2, L1_gnn_att_dst2, L1_gnn_b2, L2_gnn_node_emb, L2_gnn_w_rel1, L2_gnn_w_root1, L2_gnn_b1, L2_gnn_w_rel2, L2_gnn_w_root2, L2_gnn_b2, L2_gnn_w_rel3, L2_gnn_w_root3, L2_gnn_b3, L3_gnn_W1, L3_gnn_a_src1, L3_gnn_a_dst1, L3_gnn_b1, L3_gnn_W2, L3_gnn_a_src2, L3_gnn_a_dst2, L3_gnn_b2):
    import jax
    import jax.numpy as jnp

    def _L0_gnn_ref(x, edge_index, W1, a1_src, a1_dst, b1, W2, a2_src, a2_dst, b2):
        import jax, jax.numpy as jnp
        import numpy as np
        N_NODES = 625
        N_EDGES = 5000
        IN_DIM, HID, OUT_DIM, HEADS = (768, 512, 768, 4)
        NEG_SLOPE = 0.2

        def _gat_layer(x, src, dst, W, a_src, a_dst, b, heads, d_out, concat):
            N = x.shape[0]
            h = (x @ W).reshape(N, heads, d_out)
            as_n = jnp.einsum('nhd,hd->nh', h, a_src)
            ad_n = jnp.einsum('nhd,hd->nh', h, a_dst)
            e = jax.nn.leaky_relu(as_n[src] + ad_n[dst], NEG_SLOPE)
            e_max = jax.lax.stop_gradient(jax.ops.segment_max(e, dst, num_segments=N))
            ex = jnp.exp(e - e_max[dst])
            denom = jax.ops.segment_sum(ex, dst, num_segments=N)
            alpha = ex / (denom[dst] + 1e-16)
            msg = alpha[:, :, None] * h[src]
            out = jax.ops.segment_sum(msg, dst, num_segments=N)
            out = out.reshape(N, heads * d_out) if concat else out.mean(axis=1)
            return out + b
        N = x.shape[0]
        loops = jnp.arange(N, dtype=edge_index.dtype)
        src = jnp.concatenate([edge_index[0], loops])
        dst = jnp.concatenate([edge_index[1], loops])
        h = _gat_layer(x, src, dst, W1, a1_src, a1_dst, b1, HEADS, HID, True)
        h = jax.nn.elu(h)
        out = _gat_layer(h, src, dst, W2, a2_src, a2_dst, b2, 1, OUT_DIM, False)
        return out

    def _L1_gnn_ref(x, edge_index, W1, att_src1, att_dst1, b1, W2, att_src2, att_dst2, b2):
        import jax, jax.numpy as jnp
        import numpy as np
        N_NODES = 625
        N_EDGES = 10000
        NEG_SLOPE = 0.2

        def _gat_layer(x, src, dst, W, a_src, a_dst, bias, concat):
            N = x.shape[0]
            H, C = a_src.shape
            h = (x @ W).reshape(N, H, C)
            al_s = jnp.einsum('nhc,hc->nh', h, a_src)
            al_d = jnp.einsum('nhc,hc->nh', h, a_dst)
            e = jax.nn.leaky_relu(al_s[src] + al_d[dst], NEG_SLOPE)
            m = jax.ops.segment_max(e, dst, num_segments=N)
            ex = jnp.exp(e - m[dst])
            denom = jax.ops.segment_sum(ex, dst, num_segments=N)
            alpha = ex / (denom[dst] + 1e-16)
            msg = h[src] * alpha[:, :, None]
            out = jax.ops.segment_sum(msg, dst, num_segments=N)
            out = out.reshape(N, H * C) if concat else out.mean(axis=1)
            return out + bias
        N = x.shape[0]
        loops = jnp.arange(N, dtype=edge_index.dtype)
        src = jnp.concatenate([edge_index[0], loops])
        dst = jnp.concatenate([edge_index[1], loops])
        h = jax.nn.elu(_gat_layer(x, src, dst, W1, att_src1, att_dst1, b1, concat=True))
        out = _gat_layer(h, src, dst, W2, att_src2, att_dst2, b2, concat=False)
        return out

    def _L2_gnn_ref(x, node_type, edge_index, edge_type, node_emb, w_rel1, w_root1, b1, w_rel2, w_root2, b2, w_rel3, w_root3, b3):
        import jax, jax.numpy as jnp
        import numpy as np
        NUM_NODES = 625
        NUM_EDGES = 10000
        IN_CH = 768
        TYPE_DIM = 128
        HID = 768
        OUT = 768
        NUM_REL = 3
        NUM_NODE_TYPE = 3

        def _glorot(key, shape):
            fan_in, fan_out = (shape[-2], shape[-1])
            lim = (6.0 / (fan_in + fan_out)) ** 0.5
            return jax.random.uniform(key, shape, jnp.float32, -lim, lim)

        def rgcn_conv(h, src, dst, edge_type, w_rel, w_root, bias):
            num_nodes = h.shape[0]
            xw = jnp.einsum('nd,rde->rne', h, w_rel)
            msg = xw[edge_type, src]
            onehot = jax.nn.one_hot(edge_type, NUM_REL, dtype=h.dtype)
            count = jax.ops.segment_sum(onehot, dst, num_segments=num_nodes)
            inv = jnp.where(count > 0, 1.0 / jnp.maximum(count, 1.0), 0.0)
            msg = msg * inv[dst, edge_type][:, None]
            agg = jax.ops.segment_sum(msg, dst, num_segments=num_nodes)
            return agg + h @ w_root + bias
        src, dst = (edge_index[0], edge_index[1])
        h = jnp.concatenate([x, node_emb[node_type]], axis=-1)
        h = jax.nn.relu(rgcn_conv(h, src, dst, edge_type, w_rel1, w_root1, b1))
        h = jax.nn.relu(rgcn_conv(h, src, dst, edge_type, w_rel2, w_root2, b2))
        h = jax.nn.relu(rgcn_conv(h, src, dst, edge_type, w_rel3, w_root3, b3))
        return h

    def _L3_gnn_ref(x, edge_index, W1, a_src1, a_dst1, b1, W2, a_src2, a_dst2, b2):
        import jax, jax.numpy as jnp
        import numpy as np
        N = 1250
        E_RAND = 20000
        NEG_SLOPE = 0.2

        def gat_layer(x, W, a_src, a_dst, bias, src, dst, heads, out_c, concat):
            n = x.shape[0]
            h = (x @ W).reshape(n, heads, out_c)
            al_s = jnp.einsum('nhc,hc->nh', h, a_src)
            al_d = jnp.einsum('nhc,hc->nh', h, a_dst)
            e = jax.nn.leaky_relu(al_s[src] + al_d[dst], NEG_SLOPE)
            m = jax.ops.segment_max(e, dst, num_segments=n)
            ex = jnp.exp(e - m[dst])
            z = jax.ops.segment_sum(ex, dst, num_segments=n)
            alpha = ex / (z[dst] + 1e-16)
            msg = h[src] * alpha[:, :, None]
            out = jax.ops.segment_sum(msg, dst, num_segments=n)
            out = out.reshape(n, heads * out_c) if concat else out.mean(axis=1)
            return out + bias
        src, dst = (edge_index[0], edge_index[1])
        h = gat_layer(x, W1, a_src1, a_dst1, b1, src, dst, heads=8, out_c=96, concat=True)
        h = jax.nn.elu(h)
        out = gat_layer(h, W2, a_src2, a_dst2, b2, src, dst, heads=1, out_c=768, concat=False)
        return out
    edge_index = jnp.stack([src, dst])
    h = jnp.maximum(_layernorm(x, axis=-1), 0.0)
    x = x + _L0_gnn_ref(h, edge_index, L0_gnn_W1, L0_gnn_a1_src, L0_gnn_a1_dst, L0_gnn_b1, L0_gnn_W2, L0_gnn_a2_src, L0_gnn_a2_dst, L0_gnn_b2)
    h = jnp.maximum(_layernorm(x, axis=-1), 0.0)
    x = x + _L1_gnn_ref(h, edge_index, L1_gnn_W1, L1_gnn_att_src1, L1_gnn_att_dst1, L1_gnn_b1, L1_gnn_W2, L1_gnn_att_src2, L1_gnn_att_dst2, L1_gnn_b2)
    h = jnp.maximum(_layernorm(x, axis=-1), 0.0)
    x = x + _L2_gnn_ref(h, node_type_3, edge_index, edge_type_3, L2_gnn_node_emb, L2_gnn_w_rel1, L2_gnn_w_root1, L2_gnn_b1, L2_gnn_w_rel2, L2_gnn_w_root2, L2_gnn_b2, L2_gnn_w_rel3, L2_gnn_w_root3, L2_gnn_b3)
    h = jnp.maximum(_layernorm(x, axis=-1), 0.0)
    x = x + _L3_gnn_ref(h, edge_index, L3_gnn_W1, L3_gnn_a_src1, L3_gnn_a_dst1, L3_gnn_b1, L3_gnn_W2, L3_gnn_a_src2, L3_gnn_a_dst2, L3_gnn_b2)
    return x

_drawn_inputs = setup_inputs


def setup_inputs(seed=0):
    import zlib

    import numpy as np

    out = dict(_drawn_inputs(seed))
    spreads = {'L0_gnn_b1': (0.0, 0.1),
     'L0_gnn_b2': (0.0, 0.1),
     'L1_gnn_b1': (0.0, 0.1),
     'L1_gnn_b2': (0.0, 0.1),
     'L2_gnn_b1': (0.0, 0.1),
     'L2_gnn_b2': (0.0, 0.1),
     'L2_gnn_b3': (0.0, 0.295),
     'L3_gnn_b1': (0.0, 0.1),
     'L3_gnn_b2': (0.0, 0.1)}
    factors = {'L0_gnn_a1_dst': 9.276,
     'L0_gnn_a2_dst': 84.308,
     'L1_gnn_att_src1': 8.0,
     'L1_gnn_att_dst1': 126.082,
     'L1_gnn_att_src2': 23.805,
     'L1_gnn_att_dst2': 8.0,
     'L3_gnn_a_src1': 8.0,
     'L3_gnn_a_dst1': 68.123,
     'L3_gnn_a_src2': 28.951,
     'L3_gnn_a_dst2': 200.0}
    for name, (base, spread) in spreads.items():
        noise = np.random.default_rng([zlib.crc32(name.encode()), seed]).standard_normal(out[name].shape)
        drawn = base * np.exp(spread * noise) if base else spread * noise
        out[name] = jnp.asarray(drawn.astype(out[name].dtype))
    for name, factor in factors.items():
        out[name] = (out[name] * factor).astype(out[name].dtype)
    return out
```

```python
import numpy as np
import concourse.bass as bass
from concourse import mybir
from contextlib import ExitStack

F32, F32R, F16, BF16 = mybir.dt.float32, mybir.dt.float32r, mybir.dt.float16, mybir.dt.bfloat16
U16, I32 = mybir.dt.uint16, mybir.dt.int32
ALU, ACT, AX = mybir.AluOpType, mybir.ActivationFunctionType, mybir.AxisListType

N, D, E, R, TD = 625, 768, 10000, 3, 128
NT = 5
P = N // NT
NP = 628
HC = NP // 2
ET = E // P
EG = 4
NG = ET // EG
BANK = 512
SLOTS = 4
STAGES, PAIRS = 3, 5
AHEAD = PAIRS - 1
WMAX = 384
SLOPE, EPS, ABSENT, FLOOR = 0.2, 1e-5, -1e37, -1e30
PASSES = ((0, 0), (0, 1), (1, 0))
GAT_HEADS = {0: (4, 512), 1: (4, 512), 3: (8, 96)}
RGCN_IN = {1: 7, 2: 7, 3: 6}
RGCN_CHUNKS = {1: ((0, 384), (384, 256), (640, 256)), 2: ((0, 384), (384, 384)), 3: ((0, 384), (384, 384))}
SCRATCH = 512


class Signals:

    def __init__(self, sems, known):
        self.sems, self.known, self.counts, self.seen = sems, known, dict.fromkeys(sems, 0), {}

    def up(self, name, *key, by=1):
        self.counts[name] += by
        self.seen[key] = (name, self.counts[name])
        return self.sems[name], by

    def same(self, key, *other):
        self.seen[other] = self.seen[key]

    def at(self, *key):
        name, value = self.known.get(key, (next(iter(self.sems)), 1))
        return self.sems[name], value


def groups(w):
    return ((0, 4, 256), (4, 1, 256)) if w <= 256 else ((0, 2, BANK), (2, 2, BANK), (4, 1, BANK))


def gat_steps(l):
    heads, dh = GAT_HEADS[l]
    if l == 3:
        yield ("project", l, 0, 384)
        yield ("project", l, 1, 384)
        for h in range(heads + 1):
            if h:
                yield ("attention_T", l, h - 1)
            if h < heads:
                yield ("scores", l, h)
            if h:
                yield ("aggregate", l, h - 1, 0)
            if h < heads:
                for d in range(NT):
                    yield ("softmax", l, h, d)
                yield ("normalise", l, h)
    else:
        for h in range(heads + 1):
            if h < heads:
                yield ("project", l, 2 * h, 256)
            if h:
                yield ("attention_T", l, h - 1)
            if h < heads:
                yield ("project", l, 2 * h + 1, 256)
                yield ("scores", l, h)
            for f in range(4):
                if h:
                    yield ("aggregate", l, h - 1, f)
                if h < heads:
                    yield ("softmax", l, h, f)
            if h < heads:
                yield ("softmax", l, h, 4)
                yield ("normalise", l, h)
    h = heads
    for c in range(3):
        yield ("project2", l, c, 256)
    yield ("scores", l, h)
    for d in range(NT):
        yield ("softmax", l, h, d)
    yield ("normalise", l, h)
    yield ("attention_T", l, h)
    for d in range(NT):
        yield ("output", l, d)
        if d and l != 3:
            yield ("norm_T", l + 1, d - 1)
    if l != 3:
        yield ("norm_T", l + 1, NT - 1)


def rgcn_steps():
    yield ("embed",)
    for i in (1, 2, 3):
        for c, (f0, w) in enumerate(RGCN_CHUNKS[i]):
            for r in range(R):
                yield ("relation", i, c, r, w)
                if i == 1 and c == 0:
                    yield ("mean_T", r)
            if i < 3:
                for f in range(w // 128):
                    yield ("combine", i, c, f)
            else:
                yield ("combine_rows", c)
                for d in range(NT):
                    yield ("row_part", c, d)
                    if d and c:
                        yield ("norm_T", 3, d - 1)
    yield ("norm_T", 3, NT - 1)


def steps():
    yield ("bounds",)
    for d in range(NT):
        yield ("load_x", d)
        if d:
            yield ("norm_T", 0, d - 1)
    yield ("norm_T", 0, NT - 1)
    for d in range(NT):
        yield ("count", d)
    yield from gat_steps(0)
    yield from gat_steps(1)
    yield from rgcn_steps()
    yield ("graph_again",)
    yield from gat_steps(3)


def weight_tiles(I):
    out = {}
    for l, (heads, dh) in GAT_HEADS.items():
        w1, w2 = I[f"W1_{l}"], I[f"W2_{l}"]
        rows = 128 if l < 3 else 96
        for s in gat_steps(l):
            if s[0] == "project":
                c, w = s[2:]
                out[s] = [(w1[128 * k:128 * k + 128, c * w:c * w + w], 128, w) for k in range(6)]
            if s[0] == "project2":
                c, w = s[2:]
                out[s] = [(w2[rows * k:rows * k + rows, c * w:c * w + w], rows, w)
                          for k in range(heads * dh // rows)]
    for s in rgcn_steps():
        if s[0] == "relation":
            _, i, c, r, w = s
            f0 = RGCN_CHUNKS[i][c][0]
            out[s] = [(I[f"rel_{i}"][r, 128 * k:128 * k + 128, f0:f0 + w], 128, w) for k in range(RGCN_IN[i])]
        if s[0] == "combine":
            _, i, c, f = s
            f0 = RGCN_CHUNKS[i][c][0] + 128 * f
            out[s] = [(I[f"root_{i}"][128 * k:128 * k + 128, f0:f0 + 128], 128, 128) for k in range(RGCN_IN[i])]
        if s[0] == "combine_rows":
            f0, w = RGCN_CHUNKS[3][s[1]]
            out[s] = [(I["root_3"][128 * k:128 * k + 128, f0:f0 + w], 128, w) for k in range(RGCN_IN[3])]
    return out


def build(nc, I, out, known):
    ctx = ExitStack()
    with ctx:
        STEPS = list(steps())
        tiles_of = weight_tiles(I)
        first_tile, W = {}, []
        for s in STEPS:
            first_tile[s] = len(W)
            W += tiles_of.get(s, [])
        wend = {s: first_tile[s] + len(tiles_of.get(s, [])) for s in STEPS}

        names = ["psum_filled", "psum_free_dve", "psum_free_act", "weights_used", "weights_hi", "weights_lo",
                 "hi_ready", "lo_ready", "rows_used", "norm_stats", "norm_rows", "norm_scale", "input_hi",
                 "input_lo", "scores_step", "score_rows", "exp_ready", "prob_step", "prob_ready",
                 "att_hi", "att_lo", "elu_step", "elu_relu", "elu_exp", "x2_hi", "x2_lo", "dve_step",
                 "count_step", "bounds_step", "bounds", "bounds_rows", "count_rows", "edge_sums", "graph", "pool_const", "pool_step", "x_added", "embed", "embed_hi", "mean_step"]
        names += [f"onehot{i}" for i in range(EG)] + [f"onehot_used{i}" for i in range(EG)]
        dmas = ([f"weight_in{i}" for i in range(STAGES)] + [f"x_in{i}" for i in range(2)]
                + [f"x_out{i}" for i in range(2)] + [f"att_vec{i}" for i in range(2)]
                + ["edges_in", "bias_in", "bias2_in", "small_in", "counts_out0", "counts_out1", "counts_in", "graph_out0",
                   "graph_out1", "graph_in"])
        sems = {n: ctx.enter_context(nc.semaphore(n)) for n in names + dmas}
        G = Signals(sems, known)
        up, at = G.up, G.at

        base = -(-nc.sbuf_base // 32) * 32
        def sb(name, shape, dt, off):
            off = -(-off // 32) * 32
            return nc.alloc_sbuf_tensor_at(name, shape, dt, offset=base + off)
        tile_b = 2 * NP * 4
        XB = sb("XB", [128, 7, 2, NP], F32R, 0)
        o1 = 7 * tile_b
        XA = sb("XA", [128, 9, 2, NP], F32R, o1)
        og = o1 + 9 * tile_b
        def sg(name, shape, dt, size):
            nonlocal og
            t = sb(name, shape, dt, og)
            og += -(-size // 32) * 32
            return t
        Hg = sg("Hg", [P, NT, 2, 1024], F32R, NT * 2 * 1024 * 4)
        AT = sg("AT", [P, NT, 2, NP], F32R, NT * 2 * NP * 4)
        oprob = og
        prob = sg("prob", [P, NT, NP], F32, NT * NP * 4)
        Cg = sg("Cg", [P, NT, NP], U16, NT * NP * 2)
        negm = sg("negm", [P, NT, NP], BF16, NT * NP * 2)
        asb = sg("asb", [P, NP], F32, NP * 4)
        b2b = sg("b2b", [P, D], F32, D * 4)
        ab = sg("ab", [P, 2, 2, WMAX], F32, 4 * WMAX * 4)
        mx = sg("mx", [P, NT], F32, 32)
        z = sg("z", [P, NT], F32, 32)
        mrow = sg("mrow", [P, NT], F32, 32)
        sh1 = sg("sh1", [P, NT], F32, 32)
        sh2 = sg("sh2", [P, NT], F32, 32)
        den = sg("den", [P, NT], F32, 32)
        dene = sg("dene", [P, NT], F32, 32)
        rden = sg("rden", [P, NT], F32, 32)
        asp = sg("asp", [P, 2, 8, NT], F32, 2 * 8 * NT * 4)
        asq = sg("asq", [P, 2, NT], F32, 2 * NT * 4)
        asad = sg("asad", [P, 2, 2, NT], F32, 4 * NT * 4)
        junk = sg("junk", [P, 2, WMAX], BF16, 4 * WMAX)
        ol = o1 + 7 * tile_b
        MT = sb("MT", [P, R, NT, 2, NP], F32R, ol); ol += R * NT * 2 * NP * 4
        Hl = sb("Hl", [P, NT, R, 2, WMAX], F32R, ol); ol += NT * R * 2 * WMAX * 4
        cr_in = sb("cr_in", [P, NT, R * N], U16, 0)
        mean = sb("mean", [P, NT, N], F32, NT * R * N * 2)
        b3b = sb("b3b", [P, D], F32, 6 * tile_b)
        oc = o1
        def sc(name, shape, dt, size):
            nonlocal oc
            t = sb(name, shape, dt, oc)
            oc += -(-size // 32) * 32
            return t
        CW = R * N + 1
        iota32 = sc("iota32", [P, CW], I32, CW * 4)
        iota16 = sc("iota16", [P, CW], F16, CW * 2)
        srcs = sc("srcs", [P, EG, CW], F16, EG * CW * 2)
        dsts = sc("dsts", [P, EG, 128], F16, EG * 256)
        zero16 = sc("zero16", [1, BANK], F16, BANK * 2)
        gdst32 = sc("gdst32", [NG, EG * P], I32, EG * P * 4)
        gspan = sc("gspan", [NG, 2], F32, 8)
        gid32 = sc("gid32", [NG, 1], I32, 4)
        gid = sc("gid", [NG, 2], F32, 8)
        first32 = sc("first32", [NG, NT], I32, 4 * NT)
        first = sc("first", [NG, 2, NT], F32, 8 * NT)
        touch = sc("touch", [NG, 3, NT], F32, 12 * NT)
        reach = sc("reach", [1, 2, NT], F32, 8 * NT)
        span = sc("span", [1, 4, NT + 1], F32, 16 * NT + 16)
        bounds = sc("bounds", [1, 2, NT + 1], I32, 8 * NT + 8)
        cr = sc("cr", [P, 2, CW], U16, 2 * CW * 2)
        cn = sc("cn", [P, 2, NP], U16, 2 * NP * 2)
        edge32 = sc("edge32", [P, 3, ET], I32, 3 * ET * 4)
        edgef = sc("edgef", [P, 3, ET], F32, 3 * ET * 4)
        cnt = sc("cnt", [P, NT, R], F32, 60)
        cnt1 = sc("cnt1", [P, NT, R], F32, 60)
        got = sc("got", [P, NT, R], F32, 60)
        oa = -(-max(og, ol) // 32) * 32
        def sa(name, shape, dt, size):
            nonlocal oa
            t = sb(name, shape, dt, oa)
            oa += -(-size // 32) * 32
            return t
        stage = sa("stage", [128, STAGES, WMAX], F32, STAGES * WMAX * 4)
        pairs = sa("pairs", [128, PAIRS, 2, WMAX], F32R, PAIRS * 2 * WMAX * 4)
        ort = oa
        mn = sa("mn", [128, NP], F32, NP * 4)
        rl = sa("rl", [128, 2, NP], F32, 2 * NP * 4)
        e2 = sa("e2", [P, 2, NP], F32, 2 * NP * 4)
        xl = sb("xl", [P, 2, D], F32, ort)
        xo = sb("xo", [P, 2, D], F32, ort + 2 * D * 4)
        assert 4 * D * 4 <= 5 * NP * 4
        hn = sa("hn", [P, D], F32, D * 4)
        ident = sa("ident", [128, 128], F32, 512)
        b1t = sa("b1t", [128, 16], F32, 64)
        bns = sa("bns", [P, 2, 2, 6], F32, 96)
        mv = sa("mv", [P, 2, 2], F32, 16)
        ve = sa("ve", [P, 2, 1], F32, 8)
        rstd = sa("rstd", [P, 2, 1], F32, 8)
        nb = sa("nb", [P, 2, 1], F32, 8)
        mhalf = sa("mhalf", [P, 1], F32, 4)
        inv = sa("inv", [P, NT, R], F32, 60)
        nti = sb("nti", [R, N], I32, oprob)
        ntf = sb("ntf", [R, N], F32, oprob + tile_b)
        nth = sb("nth", [R, NP], F32R, oprob + 2 * tile_b)
        emf = sb("emf", [R, TD], F32, oprob + 3 * tile_b)
        emh = sb("emh", [R, 2, TD], F32R, oprob + 3 * tile_b + 512)
        rid = sb("rid", [R, 1], F32, oprob + 3 * tile_b + 1536)
        rii = sb("rii", [R, 1], I32, oprob + 3 * tile_b + 1568)
        assert base + oa <= nc.sbuf_usable_end, (base + oa, nc.sbuf_usable_end)

        x_scr = nc.dram_tensor("x_scratch", [3, N, D], F32).ap()
        cr_scr = nc.dram_tensor("relation_counts", [N, CW], U16).ap()
        cn_scr = nc.dram_tensor("edge_counts", [N, NP], U16).ap()

        ps = ctx.enter_context(nc.psum_tensor("ps", [128, SLOTS * 2 * BANK], F32))

        fill_of, seq, user = {}, [0], {}

        def slot(q):
            s0 = q % SLOTS * 2 * BANK
            return ps[:, s0:s0 + 2 * BANK]

        def halves(q, rows, n=HC):
            return slot(q).rearrange("p (c n) -> p c n", c=2)[:rows, :, :n]

        def h2(ap):
            return ap.rearrange("p (c n) -> p c n", c=2)

        def source(s):
            if s[0] == "project":
                return [(XB, k, 128) for k in range(6)]
            if s[0] == "project2":
                if s[1] == 3:
                    return [(XA, k, 96) for k in range(8)]
                return [(XA, k, 128) if k < 9 else (XB, k - 9, 128) for k in range(16)]
            return [((XB if s[1] == 2 else XA), k, 128) for k in range(RGCN_IN[s[1]])]

        def source_ready(s, k):
            if s[0] == "project":
                return ("input lo", s[1], NT - 1)
            if s[0] == "project2":
                return ("x2 lo", s[1], k) if s[1] == 3 else ("x2 lo", s[1], k // 4, k % 4)
            if s[1] == 1:
                return ("embed lo",) if k == 6 else ("input lo", 2, NT - 1)
            c = next(c for c, (f0, w) in enumerate(RGCN_CHUNKS[s[1] - 1]) if f0 <= 128 * k < f0 + w)
            return ("stage lo", s[1] - 1, c, k - RGCN_CHUNKS[s[1] - 1][c][0] // 128)

        def row_dest(s, s0, n, part, w):
            if s[0] == "project":
                c0 = s[2] * w % 1024
                return Hg[:, s0:s0 + n, part, c0:c0 + w]
            if s[0] == "project2":
                return Hg[:, s0:s0 + n, part, s[2] * w:s[2] * w + w]
            return Hl[:, s0:s0 + n, s[3], part, :w]

        def psum_rows(q, n, pitch, w):
            return slot(q)[:P, :n * pitch].rearrange("p (n c) -> p n c", n=n)[:, :, :w]

        gat_projects = [s for s in STEPS if s[0] in ("project", "project2")]
        loads_x = [s for s in STEPS if s[0] in ("load_x", "output", "combine_rows")]

        def pieces(s):
            if s[0] == "project" and s[1] == 3:
                return [(4 * s[2] + i, 96 * i, 96) for i in range(4)]
            return [(s[2] if s[0] == "project2" else s[2] % 2, 0, s[3])]

        def last_piece(s):
            _, l, h = s
            heads = GAT_HEADS[l][0]
            if h == heads:
                return ("project2", l, 2, 256)
            return ("project", l, 2 * h + 1, 256) if l < 3 else ("project", l, h // 4, 384)

        heads_order = {s[1:]: i for i, s in enumerate(x for x in STEPS if x[0] == "scores")}
        soft_order = {s[1:]: i for i, s in enumerate(x for x in STEPS if x[0] == "softmax")}
        agg_order = {s[1:]: i for i, s in enumerate(x for x in STEPS if x[0] == "aggregate")}
        agg_list = list(agg_order)
        norm_order = {s[1:]: i for i, s in enumerate(x for x in STEPS if x[0] == "norm_T")}
        norm_list = list(norm_order)
        norm_of = {("load_x", d): (0, d) for d in range(NT)}
        norm_of.update({("output", l, d): (l + 1, d) for l in (0, 1) for d in range(NT)})
        norm_of.update({("row_part", 1, d): (3, d) for d in range(NT)})
        xr_keys = ([("load_x", d) for d in range(NT)] + [("output", 0, d) for d in range(NT)]
                   + [("output", 1, d) for d in range(NT)] + [("row_part", c, d) for c in range(2) for d in range(NT)]
                   + [("output", 3, d) for d in range(NT)])
        xr = {k: i for i, k in enumerate(xr_keys)}
        combine_order = {s: i for i, s in enumerate(x for x in STEPS if x[0] == "combine")}
        combine_list = list(combine_order)

        def agg_key(l, h, f):
            return (l, h, f) if l < 3 else (l, h)

        def x2_place(l, h, f):
            if l == 3:
                return XA, h
            i = 4 * h + f
            return (XA, i) if i < 9 else (XB, i - 9)

        block = ctx.enter_context(nc.Block())

        @block.tensor
        def _(pe):
            mm = nc.tensor.matmul

            def acquire(*key):
                q = seq[0]
                seq[0] += 1
                fill_of[key] = q
                if q % SLOTS in user:
                    pe.wait_ge(*at("free", user[q % SLOTS]))
                user[q % SLOTS] = q
                return q

            pe.wait_ge(*at("ident",))
            for s in STEPS:
                kind = s[0]
                if kind in ("project", "project2", "relation"):
                    w = s[-1]
                    src = source(s)
                    gs = groups(w)
                    qs = [acquire("rows", s, g) for g in range(len(gs))]
                    waited = None
                    for k, (X, xi, rows) in enumerate(src):
                        n = first_tile[s] + k
                        if source_ready(s, k) != waited:
                            waited = source_ready(s, k)
                            pe.wait_ge(*at(*waited))
                        pe.wait_ge(*at("weights lo", n))
                        for g, (s0, ns, pitch) in enumerate(gs):
                            for t in range(ns):
                                o = slot(qs[g])[:P, t * pitch:t * pitch + w]
                                for i, (a, b) in enumerate(PASSES):
                                    last = mm(o, X[:rows, xi, a, P * (s0 + t):P * (s0 + t + 1)],
                                              pairs[:rows, n % PAIRS, b, :w],
                                              start=k == 0 and i == 0 and t * pitch % BANK == 0,
                                              stop=k == len(src) - 1 and i == 2, skip_group_check=True)
                            if k == len(src) - 1:
                                last.then_inc(*up("psum_filled", "filled", "rows", s, g))
                        if k == len(src) - 1:
                            G.same(("filled", "rows", s, len(gs) - 1), "weights used", n)
                        else:
                            last.then_inc(*up("weights_used", "weights used", n))
                elif kind == "scores":
                    q = acquire(*s)
                    pe.wait_ge(*at("scores col", *s[1:]))
                    hb = heads_order[s[1:]] % 2
                    for j in range(NT):
                        c0 = j * P if j < 3 else BANK + (j - 3) * P
                        last = nc.tensor.transpose(slot(q)[:P, c0:c0 + P],
                                                   asad[:, hb, 0, j:j + 1].to_broadcast([P, P]), ident[:P, :P])
                    last.then_inc(*up("psum_filled", "filled", *s))
                elif kind in ("attention_T", "mean_T"):
                    M = prob if kind == "attention_T" else mean
                    for j in range(NT):
                        q = acquire(*s, j)
                        for d in range(NT):
                            if j == 0:
                                pe.wait_ge(*at("rows ready", *s, d))
                            c0 = d * P if d < 3 else BANK + (d - 3) * P
                            last = nc.tensor.transpose(slot(q)[:P, c0:c0 + P], M[:, d, P * j:P * j + P], ident[:P, :P])
                        last.then_inc(*up("psum_filled", "filled", *s, j))
                elif kind == "aggregate":
                    _, l, h, f = s
                    heads, dh = GAT_HEADS[l]
                    q = acquire(*s)
                    if f == 0:
                        pe.wait_ge(*at("att lo", l, h, NT - 1))
                    m = 128 if l < 3 else 96
                    c0 = h % 2 * 512 + 128 * f if l < 3 else 96 * h
                    for c in range(2):
                        for t in range(NT):
                            for i, (a, b) in enumerate(PASSES):
                                last = mm(halves(q, m)[:, c, :], Hg[:, t, a, c0:c0 + m],
                                          AT[:, t, b, HC * c:HC * c + HC],
                                          start=t == 0 and i == 0, stop=t == NT - 1 and i == 2)
                    last.then_inc(*up("psum_filled", "filled", *s))
                elif kind == "output":
                    _, l, d = s
                    q = acquire(*s)
                    if d == 0:
                        pe.wait_ge(*at("att lo", l, GAT_HEADS[l][0], NT - 1))
                    for c in range(2):
                        for t in range(NT):
                            for i, (a, b) in enumerate(PASSES):
                                last = mm(halves(q, P, 384)[:, c, :], AT[:, t, a, P * d:P * d + P],
                                          Hg[:, t, b, 384 * c:384 * c + 384],
                                          start=t == 0 and i == 0, stop=t == NT - 1 and i == 2)
                    last.then_inc(*up("psum_filled", "filled", *s))
                elif kind == "norm_T":
                    q = acquire(*s)
                    pe.wait_ge(*at("norm rows", *s[1:]))
                    for k in range(6):
                        c0 = k * P if k < 3 else BANK + (k - 3) * P
                        last = nc.tensor.transpose(slot(q)[:, c0:c0 + P], hn[:, 128 * k:128 * k + 128], ident[:P, :P])
                    last.then_inc(*up("psum_filled", "filled", *s))
                elif kind == "bounds":
                    q = acquire(*s)
                    pe.wait_ge(*at("touched"))
                    for side in range(2):
                        for d in range(NT):
                            c0 = side * BANK + NG * d
                            last = nc.tensor.transpose(slot(q)[:1, c0:c0 + NG], touch[:, 1 + side, d:d + 1],
                                                       ident[:NG, :NG])
                    last.then_inc(*up("psum_filled", "filled", *s))
                elif kind == "count":
                    d = s[1]
                    if d == 0:
                        seq[0] += seq[0] % 2
                        pe.wait_ge(*at("bounds"))
                        passes = [pe.value_load(bounds[0:1, 0, i:i + 1], min_val=0, max_val=NT * NG)
                                  for i in range(NT + 1)]
                    q = acquire(*s, 0)
                    acquire(*s, 1)
                    o = ps[:P, q % SLOTS * 2 * BANK:q % SLOTS * 2 * BANK + 4 * BANK]
                    for c in range(4):
                        last = mm(o[:, BANK * c:BANK * c + BANK], zero16[:, :P], zero16[:, :], start=True,
                                  stop=True, skip_group_check=True)
                        if d == 0:
                            last.then_inc(sems[f"onehot_used{c}"], 1)
                    with pe.Fori(passes[d], passes[d + 1]) as g:
                        for i in range(EG):
                            pe.wait_ge(sems[f"onehot{i}"], g + 1)
                            for c in range(4):
                                c1 = min(BANK * c + BANK, R * N)
                                last = mm(o[:, BANK * c:c1], dsts[:, i, :P], srcs[:, i, BANK * c:c1],
                                          start=False, stop=True, skip_group_check=True)
                            last.then_inc(sems[f"onehot_used{i}"], 1)
                    mm(o[:, :2], zero16[:, :P], zero16[:, :2], start=False, stop=True,
                       skip_group_check=True).then_inc(*up("psum_filled", "filled", *s))
                elif kind == "embed":
                    q = acquire(*s)
                    pe.wait_ge(*at("embed operands",))
                    for c in range(2):
                        for a in range(2):
                            last = mm(halves(q, TD)[:, c, :], emh[:, a, :], nth[:, HC * c:HC * c + HC],
                                      start=a == 0, stop=a == 1)
                    last.then_inc(*up("psum_filled", "filled", *s))
                elif kind == "combine":
                    _, i, c, f = s
                    q = acquire(*s)
                    src = source(("relation", i))
                    for k, (X, xi, rows) in enumerate(src):
                        n = first_tile[s] + k
                        pe.wait_ge(*at("weights lo", n))
                        for half in range(2):
                            for j, (a, b) in enumerate(PASSES):
                                last = mm(halves(q, 128)[:, half, :], pairs[:, n % PAIRS, a, :128],
                                          X[:, xi, b, HC * half:HC * half + HC],
                                          start=k == 0 and j == 0, stop=False)
                        last.then_inc(*up("weights_used", "weights used", n))
                    for r in range(R):
                        if f == 0:
                            g = len(groups(RGCN_CHUNKS[i][c][1])) - 1
                            pe.wait_ge(*at("rows lo", ("relation", i, c, r, RGCN_CHUNKS[i][c][1]), g))
                        if i == 1 and c == 0 and f == 0:
                            pe.wait_ge(*at("mean lo", r, NT - 1))
                        for half in range(2):
                            for t in range(NT):
                                for j, (a, b) in enumerate(PASSES):
                                    last = mm(halves(q, 128)[:, half, :], Hl[:, t, r, a, 128 * f:128 * f + 128],
                                              MT[:, r, t, b, HC * half:HC * half + HC],
                                              start=False, stop=r == R - 1 and t == NT - 1 and j == 2)
                    last.then_inc(*up("psum_filled", "filled", *s))
                elif kind == "combine_rows":
                    c = s[1]
                    gs = groups(384)
                    qs = [acquire("rows", s, g) for g in range(len(gs))]
                    src = source(("relation", 3))
                    for k, (X, xi, rows) in enumerate(src):
                        n = first_tile[s] + k
                        pe.wait_ge(*at("weights lo", n))
                        for g, (s0, ns, pitch) in enumerate(gs):
                            for t in range(ns):
                                for j, (a, b) in enumerate(PASSES):
                                    last = mm(slot(qs[g])[:P, t * pitch:t * pitch + 384],
                                              X[:, xi, a, P * (s0 + t):P * (s0 + t + 1)],
                                              pairs[:, n % PAIRS, b, :384], start=k == 0 and j == 0, stop=False)
                        last.then_inc(*up("weights_used", "weights used", n))
                    for r in range(R):
                        pe.wait_ge(*at("rows lo", ("relation", 3, c, r, 384), len(gs) - 1))
                    for g, (s0, ns, pitch) in enumerate(gs):
                        for t in range(ns):
                            for r in range(R):
                                for u in range(NT):
                                    for j, (a, b) in enumerate(PASSES):
                                        last = mm(slot(qs[g])[:P, t * pitch:t * pitch + 384],
                                                  MT[:, r, u, a, P * (s0 + t):P * (s0 + t + 1)],
                                                  Hl[:, u, r, b, :384], start=False,
                                                  stop=r == R - 1 and u == NT - 1 and j == 2)
                        last.then_inc(*up("psum_filled", "filled", "rows", s, g))

        @block.sync
        def _(sp):
            loaded = [0]

            def load_weights(upto):
                while loaded[0] < min(upto, len(W)):
                    n = loaded[0]
                    ap, rows, w = W[n]
                    if n >= STAGES:
                        sp.wait_ge(*at("weights lo", n - STAGES))
                    sp.dma_start(stage[:rows, n % STAGES, :w], ap).then_inc(
                        *up(f"weight_in{n % STAGES}", "weights in", n, by=16))
                    loaded[0] += 1

            sp.dma_start(gdst32[:, :], I["dst"]).then_inc(*up("edges_in", "targets in", by=16))
            sp.dma_start(edge32[:, :, :], I["edges"]).then_inc(*up("edges_in", "edges in", by=16))
            for s in STEPS:
                if s[0] == "count":
                    d = s[1]
                    sp.wait_ge(*at("relation counts", d))
                    sp.dma_start(cr_scr[P * d:P * d + P, :R * N], cr[:, d % 2, :R * N]).then_inc(
                        *up(f"counts_out{d % 2}", "counts out", d, by=16))
                    sp.wait_ge(*at("edge counts", d))
                    sp.dma_start(cn_scr[P * d:P * d + P, :], cn[:, d % 2, :]).then_inc(
                        *up(f"graph_out{d % 2}", "graph out", d, by=16))
                load_weights(wend[s] + AHEAD + STAGES if s in tiles_of else STAGES)
            for d in (NT - 2, NT - 1):
                sp.wait_ge(*at("graph out", d))
                sp.wait_ge(*at("counts out", d))

        @block.gpsimd
        def _(pool):
            split = [0]

            def split_lo(upto):
                while split[0] < min(upto, len(W)):
                    n = split[0]
                    _, rows, w = W[n]
                    pool.wait_ge(*at("weights hi", n))
                    nc.gpsimd.tensor_tensor(pairs[:rows, n % PAIRS, 1, :w], stage[:rows, n % STAGES, :w],
                                            pairs[:rows, n % PAIRS, 0, :w].bitcast(F32), ALU.subtract).then_inc(
                        *up("weights_lo", "weights lo", n))
                    split[0] += 1

            nc.gpsimd.memset(ident[:, :], 0.0).then_inc(*up("pool_const", "zeros"))
            pool.wait_ge(*at("zeros"))
            nc.gpsimd.affine_select(out=ident[:, :], in_=ident[:, :], compare_op=ALU.not_equal, fill=1.0, base=0,
                                    pattern=[[-1, 128]], channel_multiplier=1).then_inc(*up("pool_const", "ident"))
            nc.gpsimd.iota(iota32[:, :], pattern=[[1, CW]], base=0, channel_multiplier=0).then_inc(
                *up("pool_const", "iota32"))
            nc.gpsimd.iota(gid32[:, :], pattern=[[0, 1]], base=0, channel_multiplier=1)
            nc.gpsimd.iota(first32[:, :], pattern=[[P, NT]], base=0, channel_multiplier=0)
            nc.gpsimd.memset(zero16[:, :], 0.0).then_inc(*up("pool_const", "iota"))
            nc.gpsimd.memset(mhalf[:, :], -0.5).then_inc(*up("pool_const", "mhalf"))
            pool.wait_ge(*at("mhalf"))

            def root(n):
                b = n % 2
                pool.wait_ge(*at("norm stats", n))
                nc.gpsimd.tensor_scalar(ve[:, b, :], mv[:, b, 1:2], EPS, 1.0, ALU.add, ALU.mult).then_inc(
                    *up("pool_step", "variance", n))
                pool.wait_ge(*at("variance", n))
                nc.gpsimd.tensor_tensor(rstd[:, b, :], ve[:, b, :], mhalf[:, :], ALU.pow).then_inc(
                    *up("norm_scale", "norm scale", n))

            for s in STEPS:
                if s in norm_of:
                    root(norm_order[norm_of[s]])
                elif s == ("embed",):
                    nc.gpsimd.iota(rii[:, :], pattern=[[0, 1]], base=0, channel_multiplier=1).then_inc(
                        *up("pool_step", "relation ids"))
                elif s in tiles_of:
                    split_lo(wend[s] + AHEAD)

        @block.scalar
        def _(act):
            A = nc.scalar.activation
            split = [0]

            def split_hi(upto):
                while split[0] < min(upto, len(W)):
                    n = split[0]
                    _, rows, w = W[n]
                    act.wait_ge(*at("weights in", n))
                    if n >= PAIRS:
                        act.wait_ge(*at("weights used", n - PAIRS))
                    A(pairs[:rows, n % PAIRS, 0, :w], stage[:rows, n % STAGES, :w], ACT.Copy).then_inc(
                        *up("weights_hi", "weights hi", n))
                    split[0] += 1

            def load_x(i):
                if i >= len(xr_keys):
                    return
                key = xr_keys[i]
                if i >= 2:
                    act.wait_ge(*at("x read", i - 2))
                kept = key[0] != "load_x" and key[:2] != ("output", 0)
                src = (x_scr[2] if key[:2] == ("output", 3) else
                       x_scr[0] if key[0] == "output" else x_scr[1]) if kept else I["x"]
                d = key[-1]
                c0, w = (0, D)
                if key[:2] == ("row_part", 0):
                    w = 384
                if kept:
                    act.wait_ge(*at("x stored", i - 5))
                act.dma_start(xl[:, i % 2, c0:c0 + w], src[P * d:P * d + P, c0:c0 + w]).then_inc(
                    *up(f"x_in{i % 2}", "x in", i, by=16))

            def load_vectors(i):
                s = gat_projects[i]
                if i >= 2:
                    act.wait_ge(*at("vectors read", i - 2))
                w = s[3]
                for v, name in enumerate(("a1", "a2")[s[0] == "project2"] + x for x in ("src", "dst")):
                    src = I[f"{name}_{s[1]}"][s[2] * w:s[2] * w + w]
                    act.dma_start(ab[:, i % 2, v, :w], src.partition_broadcast(P)).then_inc(
                        *up(f"att_vec{i % 2}", "vectors in", i, v, by=16))

            def store_x(i, ap, dst):
                act.dma_start(dst, ap).then_inc(*up(f"x_out{i % 2}", "x stored", i, by=16))

            def norm_rows(n, x_ap):
                b = n % 2
                act.wait_ge(*at("norm shift", n))
                if n:
                    act.wait_ge(*at("filled", "norm_T", *norm_list[n - 1]))
                act.wait_ge(*at("norm scale", n))
                A(hn[:, :], x_ap, ACT.Relu, bias=nb[:, b, :], scale=rstd[:, b, :]).then_inc(
                    *up("norm_rows", "norm rows", *norm_list[n]))

            def row_hi(s, w):
                for g, (s0, ns, pitch) in enumerate(groups(w)):
                    act.wait_ge(*at("filled", "rows", s, g))
                    A(row_dest(s, s0, ns, 0, w), psum_rows(fill_of["rows", s, g], ns, pitch, w), ACT.Copy).then_inc(
                        *up("hi_ready", "rows hi", s, g))

            def transposed_hi(s, j, dest, name):
                q = fill_of[(*s, j)]
                act.wait_ge(*at("filled", *s, j))
                for half, c0, n in ((0, 0, 3 * P), (1, 3 * P, 2 * P)):
                    A(dest[:, c0:c0 + n], slot(q)[:P, half * BANK:half * BANK + n], ACT.Copy).then_inc(
                        *up("att_hi", name + " hi", *s[1:], j, half))

            act.dma_start(b1t[:, :16], I["b1_0"]).then_inc(*up("bias_in", "b1 in", 0, by=16))
            load_x(0)
            for s in STEPS:
                kind = s[0]
                if kind == "load_x":
                    i = xr[s]
                    load_x(i + 1)
                    norm_rows(s[1], xl[:, i % 2, :])
                    G.same(("norm rows", 0, s[1]), "x read", i)
                    if s[1] == NT - 1:
                        load_vectors(0)
                        load_vectors(1)
                elif kind == "count":
                    d = s[1]
                    q = fill_of[(*s, 0)]
                    act.wait_ge(*at("filled", *s))
                    if d >= 2:
                        act.wait_ge(*at("counts out", d - 2))
                        act.wait_ge(*at("edge counts", d - 2))
                    for r in range(R):
                        c0 = q % SLOTS * 2 * BANK + N * r
                        A(cr[:, d % 2, N * r:N * r + N], ps[:P, c0:c0 + N], ACT.Copy,
                          accum_out=cnt[:, d, r:r + 1]).then_inc(*up("count_rows", "relation", d, r))
                    G.same(("relation", d, R - 1), "relation counts", d)
                    G.same(("relation", d, R - 1), "free", q)
                    G.same(("relation", d, R - 1), "free", q + 1)
                elif kind == "norm_T":
                    l, d = s[1:]
                    X = XA if l == 2 else XB
                    act.wait_ge(*at("filled", *s))
                    A(X[:, 0:6, 0, P * d:P * d + P].rearrange("p (b k) c -> p b k c", b=2),
                      halves(fill_of[s], 128, 3 * P).rearrange("p b (k c) -> p b k c", k=3), ACT.Copy).then_inc(
                        *up("input_hi", "input hi", l, d))
                elif kind in ("project", "project2", "relation"):
                    split_hi(wend[s] + AHEAD)
                    if kind == "relation" and s[1:4] == (1, 0, 0):
                        act.wait_ge(*at("filled", "rows", ("project2", 1, 2, 256), 1))
                        act.wait_ge(*at("counts out", NT - 1))
                        act.wait_ge(*at("counts out", NT - 2))
                        act.dma_start(cr_in[:, :, :],
                                      cr_scr[:, :R * N].rearrange("(t p) n -> p t n", p=P)).then_inc(
                            *up("counts_in", "counts in", by=16))
                    row_hi(s, s[-1])
                    if kind != "relation":
                        i = gat_projects.index(s)
                        if i + 2 < len(gat_projects) and (gat_projects[i + 2][1] < 3 or s[1] == 3):
                            load_vectors(i + 2)
                        if kind == "project2" and s[2] == 0 and s[1] < 3:
                            act.wait_ge(*at("elu relu", agg_order[s[1], GAT_HEADS[s[1]][0] - 1, 3]))
                            bias = I[f"b1_{s[1] + 1}"]
                            act.dma_start(b1t[:, :bias.shape[1]], bias).then_inc(
                                *up("bias_in", "b1 in", s[1] + 1, by=16))
                elif kind == "scores":
                    act.wait_ge(*at("filled", *s))
                    q = fill_of[s]
                    h = heads_order[s[1:]]
                    if h:
                        act.wait_ge(*at("scores read", h - 1))
                    A(asb[:, 0:3 * P], slot(q)[:P, 0:3 * P], ACT.Copy).then_inc(*up("score_rows", "score rows", h, 0))
                    A(asb[:, 3 * P:N], slot(q)[:P, BANK:BANK + 2 * P], ACT.Copy).then_inc(
                        *up("score_rows", "score rows", h, 1))
                    G.same(("score rows", h, 1), "free", q)
                elif kind == "softmax":
                    l, h, d = s[1:]
                    n = soft_order[s[1:]]
                    act.wait_ge(*at("shift", l, h))
                    if n >= 2:
                        act.wait_ge(*at("prob max", n - 2))
                    if l and (h, d) == (0, 0):
                        for b in range(2):
                            act.wait_ge(*at("x stored", xr[("output", 0, NT - 1) if l == 1 else
                                                           ("row_part", 1, NT - 1)] - b))
                    A(e2[:, n % 2, :N], prob[:, d, :N], ACT.Exp, bias=sh2[:, d:d + 1], scale=SLOPE).then_inc(
                        *up("exp_ready", "exp slope", n))
                    act.wait_ge(*at("exp slope", n))
                    A(prob[:, d, :N], prob[:, d, :N], ACT.Exp, bias=sh1[:, d:d + 1]).then_inc(
                        *up("exp_ready", "exp", n))
                elif kind == "normalise":
                    l, h = s[1:]
                    act.wait_ge(*at("rden", l, h))
                    for d in range(NT):
                        A(prob[:, d, :N], prob[:, d, :N], ACT.Copy, scale=rden[:, d:d + 1]).then_inc(
                            *up("prob_ready", "rows ready", "attention_T", l, h, d))
                elif kind == "attention_T":
                    l, h = s[1:]
                    if h or l:
                        prev = ("aggregate", l, h - 1, 3 if l < 3 else 0) if h else (
                            ("output", 0, NT - 1) if l == 1 else ("combine_rows", 1))
                        act.wait_ge(*at("filled", *prev)) if l < 3 or h else None
                    for j in range(NT):
                        transposed_hi(s, j, AT[:, j, 0, :], "att")
                    if h == GAT_HEADS[l][0]:
                        act.wait_ge(*at("x2 lo", *agg_key(*[k for k in agg_list if k[0] == l][-1])))
                        act.wait_ge(*at("prob max", soft_order[l, h, NT - 1]))
                        act.dma_start(b2b[:, :], I[f"b2_{l}"].partition_broadcast(P)).then_inc(
                            *up("bias2_in", "b2 in", l, by=16))
                        load_x(xr["output", l, 0])
                    if (l, h) == (1, 4):
                        act.wait_ge(*at("filled", "attention_T", 1, 4, NT - 1))
                        act.dma_start(nti[:, :], I["node_type"].partition_broadcast(R)).then_inc(
                            *up("small_in", "types in", by=16))
                        act.dma_start(emf[:, :], I["emb"]).then_inc(*up("small_in", "emb in", by=16))
                elif kind == "mean_T":
                    for j in range(NT):
                        transposed_hi(s, j, MT[:, s[1], j, 0, :], "mean")
                elif kind == "aggregate":
                    l, h, f = s[1:]
                    n = agg_order[s[1:]]
                    m = 128 if l < 3 else 96
                    q = fill_of[s]
                    act.wait_ge(*at("elu min", n))
                    bcol = 4 * h + f if l < 3 else h
                    if n >= 2:
                        act.wait_ge(*at("x2 lo", *agg_key(*agg_list[n - 2])))
                    A(h2(rl[:m, n % 2, :]), halves(q, m), ACT.Relu, bias=b1t[:m, bcol:bcol + 1]).then_inc(
                        *up("elu_relu", "elu relu", n))
                    G.same(("elu relu", n), "free", q)
                    A(mn[:m, :], mn[:m, :], ACT.Exp).then_inc(*up("elu_exp", "elu exp", n))
                    act.wait_ge(*at("elu sum", n))
                    X, xi = x2_place(l, h, f)
                    A(X[:m, xi, 0, :], rl[:m, n % 2, :], ACT.Copy).then_inc(*up("x2_hi", "x2 hi", n))
                elif kind == "output":
                    l, d = s[1:]
                    i = xr[s]
                    if d + 1 < NT:
                        load_x(i + 1)
                    if l < 3:
                        n = norm_order[norm_of[s]]
                        norm_rows(n, xo[:, i % 2, :])
                        store_x(i, xo[:, i % 2, :], x_scr[l, P * d:P * d + P, :])
                    else:
                        act.wait_ge(*at("x added", i))
                        store_x(i, xo[:, i % 2, :], out[P * d:P * d + P, :])
                elif kind == "embed":
                    act.wait_ge(*at("filled", *s))
                    A(h2(XA[:TD, 6, 0, :]), halves(fill_of[s], TD), ACT.Copy).then_inc(*up("embed_hi", "embed hi"))
                elif kind == "combine":
                    split_hi(wend[s] + AHEAD)
                    _, i, c, f = s
                    act.wait_ge(*at("stage relu", *s[1:]))
                    X, xi = (XB if i == 1 else XA), RGCN_CHUNKS[i][c][0] // 128 + f
                    n = combine_order[s]
                    A(X[:, xi, 0, :], rl[:, n % 2, :], ACT.Copy).then_inc(*up("x2_hi", "stage hi", *s[1:]))
                elif kind == "combine_rows":
                    split_hi(wend[s] + AHEAD)
                    if s[1] == 0:
                        act.wait_ge(*at("stage lo", 2, 1, 2))
                        act.dma_start(b3b[:, :], I["b3_3"].partition_broadcast(P)).then_inc(
                            *up("bias2_in", "b3 in", by=16))
                        load_x(xr["row_part", 0, 0])
                elif kind == "row_part":
                    c, d = s[1:]
                    i = xr[s]
                    if (c, d) != (1, NT - 1):
                        load_x(i + 1)
                    if c == 0:
                        act.wait_ge(*at("x added", i))
                        store_x(i, xo[:, i % 2, :384], x_scr[1, P * d:P * d + P, :384])
                    else:
                        norm_rows(norm_order[(3, d)], xo[:, i % 2, :])
                        store_x(i, xo[:, i % 2, :], x_scr[2, P * d:P * d + P, :])
                elif kind == "graph_again":
                    act.wait_ge(*at("filled", "rows", ("combine_rows", 1), 2))
                    act.wait_ge(*at("graph out", NT - 2))
                    act.wait_ge(*at("graph out", NT - 1))
                    act.dma_start(Cg[:, :, :], cn_scr.rearrange("(t p) n -> p t n", p=P)).then_inc(
                        *up("graph_in", "graph in", by=16))
                    act.dma_start(b1t[:96, :8], I["b1_3"]).then_inc(*up("bias_in", "b1 in", 3, by=16))
                    load_vectors(len(gat_projects) - 5)
                    load_vectors(len(gat_projects) - 4)
            for b in range(2):
                act.wait_ge(*at("x stored", len(xr_keys) - 1 - b))

        @block.vector
        def _(dve):
            V = nc.vector
            last_tile = None
            junks = [0]

            def stats(n, x_ap):
                b = n % 2
                if n >= 2:
                    dve.wait_ge(*at("norm scale", n - 2))
                for i in range(2):
                    V.bn_stats(bns[:, b, i, :], x_ap[:, 384 * i:384 * i + 384]).then_inc(
                        *up("dve_step", "half stats", n, i))
                dve.wait_ge(*at("half stats", n, 1))
                V.bn_aggr(mv[:, b, :], bns[:, b, :, :].rearrange("p a c -> p (a c)")).then_inc(
                    *up("norm_stats", "norm stats", n))

            def shift(n):
                b = n % 2
                dve.wait_ge(*at("norm scale", n))
                if n >= 2:
                    dve.wait_ge(*at("norm rows", *norm_list[n - 2]))
                V.scalar_tensor_tensor(out=nb[:, b, :], in0=mv[:, b, 0:1], scalar=-1.0, in1=rstd[:, b, :],
                                       op0=ALU.mult, op1=ALU.mult).then_inc(*up("norm_stats", "norm shift", n))

            def minus_hi(out_ap, whole, hi_ap):
                return V.tensor_tensor(out_ap, whole, hi_ap.bitcast(F32), ALU.subtract)

            def finish_tile():
                nonlocal last_tile
                if last_tile is not None:
                    X, xi, m, b, hi, lo = last_tile
                    dve.wait_ge(*at(*hi))
                    minus_hi(X[:m, xi, 1, :], rl[:m, b, :], X[:m, xi, 0, :]).then_inc(*up("x2_lo", *lo))
                last_tile = None

            def transposed_lo(s, j, dest, name):
                q = fill_of[(*s, j)]
                for half, c0, n in ((0, 0, 3 * P), (1, 3 * P, 2 * P)):
                    dve.wait_ge(*at(name + " hi", *s[1:], j, half))
                    last = minus_hi(dest[:, 1, c0:c0 + n], slot(q)[:P, half * BANK:half * BANK + n],
                                    dest[:, 0, c0:c0 + n])
                last.then_inc(*up("att_lo", name + " lo", *s[1:], j))
                G.same((name + " lo", *s[1:], j), "free", q)

            def sum_relations(d):
                b = d % 2
                dve.wait_ge(*at("relation counts", d))
                if d >= 2:
                    dve.wait_ge(*at("graph out", d - 2))
                T = V.tensor_tensor
                T(cn[:, b, :N], cr[:, b, :N], cr[:, b, N:2 * N], ALU.add).then_inc(
                    *up("edge_sums", "two relations", d))
                dve.wait_ge(*at("two relations", d))
                T(cn[:, b, :N], cn[:, b, :N], cr[:, b, 2 * N:3 * N], ALU.add).then_inc(
                    *up("edge_sums", "edge counts", d))
                dve.wait_ge(*at("edge counts", d))
                V.tensor_copy(Cg[:, d, :N], cn[:, b, :N]).then_inc(*up("edge_sums", "graph copy", d))
                dve.wait_ge(*at("graph copy", d))
                dve.wait_ge(*at("ident"))
                T(Cg[:, d, P * d:P * d + P], cn[:, b, P * d:P * d + P], ident[:P, :P], ALU.add).then_inc(
                    *up("edge_sums", "graph whole", d))

            def mask():
                for d in range(NT):
                    dve.wait_ge(*at("graph whole", d))
                    V.tensor_scalar(negm[:, d, :N], Cg[:, d, :N], 0.0, ABSENT, ALU.is_equal, ALU.mult).then_inc(
                        *up("graph", "mask", d))

            V.memset(cn[:, :, N:NP], 0).then_inc(*up("graph", "cn pad"))
            V.memset(AT[:, :, :, N:NP].bitcast(F32), 0.0).then_inc(*up("graph", "AT pad"))
            for s in STEPS:
                kind = s[0]
                if kind not in ("softmax", "aggregate", "combine"):
                    finish_tile()
                if kind == "load_x":
                    i = xr[s]
                    dve.wait_ge(*at("x in", i))
                    stats(s[1], xl[:, i % 2, :])
                    shift(s[1])
                elif kind == "norm_T":
                    l, d = s[1:]
                    X = XA if l == 2 else XB
                    dve.wait_ge(*at("input hi", l, d))
                    c = slice(P * d, P * d + P)
                    minus_hi(X[:, 0:6, 1, c].rearrange("p (b k) c -> p b k c", b=2),
                             halves(fill_of[s], 128, 3 * P).rearrange("p b (k c) -> p b k c", k=3),
                             X[:, 0:6, 0, c].rearrange("p (b k) c -> p b k c", b=2)).then_inc(
                        *up("input_lo", "input lo", l, d))
                    G.same(("input lo", l, d), "free", fill_of[s])
                elif kind == "bounds":
                    n = iter(range(30))

                    def step(instruction):
                        key = ("bounds step", next(n))
                        instruction.then_inc(*up("bounds_step", *key))
                        dve.wait_ge(*at(*key))

                    dve.wait_ge(*at("iota"))
                    V.tensor_copy(iota16[:, :], iota32[:, :]).then_inc(*up("count_step", "iota16"))
                    V.tensor_copy(gid[:, 0:1], gid32[:, :])
                    step(V.tensor_copy(first[:, 0, :], first32[:, :]))
                    V.tensor_scalar(gid[:, 1:2], gid[:, 0:1], 1.0, None, ALU.add)
                    V.tensor_scalar(first[:, 1, :], first[:, 0, :], float(P), None, ALU.add)
                    dve.wait_ge(*at("edges in"))
                    V.tensor_reduce(gspan[:, 0:1], gdst32[:, :], AX.X, ALU.min)
                    step(V.tensor_reduce(gspan[:, 1:2], gdst32[:, :], AX.X, ALU.max))
                    step(V.tensor_scalar(touch[:, 0, :], first[:, 0, :], gspan[:, 1:2], None, ALU.is_le))
                    step(V.scalar_tensor_tensor(out=touch[:, 0, :], in0=first[:, 1, :], scalar=gspan[:, 0:1],
                                                in1=touch[:, 0, :], op0=ALU.is_gt, op1=ALU.mult))
                    V.tensor_scalar(touch[:, 2, :], touch[:, 0, :], gid[:, 1:2], None, ALU.mult)
                    step(V.tensor_scalar(touch[:, 1, :], touch[:, 0, :], gid[:, 0:1], None, ALU.mult))
                    V.scalar_tensor_tensor(out=touch[:, 1, :], in0=touch[:, 0, :], scalar=float(NG),
                                           in1=touch[:, 1, :], op0=ALU.mult, op1=ALU.subtract).then_inc(
                        *up("count_step", "touched"))
                    V.tensor_copy(edgef[:, :, :], edge32[:, :, :]).then_inc(*up("count_step", "edges float"))
                    dve.wait_ge(*at("edges float"))
                    V.scalar_tensor_tensor(out=edgef[:, 0, :], in0=edgef[:, 2, :], scalar=float(N),
                                           in1=edgef[:, 0, :], op0=ALU.mult, op1=ALU.add).then_inc(
                        *up("count_step", "edge keys"))
                    dve.wait_ge(*at("filled", *s))
                    step(V.tensor_reduce(reach[:, :, :],
                                         slot(fill_of[s])[:1, :].rearrange("p (c n) -> p c n", c=2)[
                                             :, :, :NT * NG].rearrange("p c (d g) -> p c d g", d=NT),
                                         AX.X, ALU.max))
                    step(V.tensor_scalar(span[:, 0, :NT], reach[:, 0, :], -1.0, float(NG), ALU.mult, ALU.add))
                    step(V.tensor_scalar(span[:, 0, :NT], span[:, 0, :NT], float(NG - 1), None, ALU.min))
                    step(V.scalar_tensor_tensor(out=span[:, 1, :NT], in0=span[:, 0, :NT], scalar=1.0,
                                                in1=reach[:, 1, :], op0=ALU.add, op1=ALU.max))
                    V.memset(span[:, 2, 0:1], 0.0)
                    step(V.tensor_tensor(span[:, 1, :NT], span[:, 1, :NT], span[:, 0, :NT], ALU.subtract))
                    for d in range(NT):
                        step(V.tensor_tensor(span[:, 2, d + 1:d + 2], span[:, 2, d:d + 1], span[:, 1, d:d + 1],
                                             ALU.add))
                    V.tensor_copy(bounds[:, 0, :], span[:, 2, :])
                    step(V.tensor_tensor(span[:, 3, :NT], span[:, 0, :NT], span[:, 2, :NT], ALU.subtract))
                    V.tensor_copy(bounds[:, 1, :NT], span[:, 3, :NT]).then_inc(*up("bounds", "bounds"))
                    G.same(("bounds",), "free", fill_of[s])
                elif kind == "count":
                    d = s[1]
                    if d == 0:
                        dve.wait_ge(*at("bounds"))
                        passes = [dve.value_load(bounds[0:1, 0, i:i + 1], min_val=0, max_val=NT * NG)
                                  for i in range(NT + 1)]
                        shift_of = [dve.value_load(bounds[0:1, 1, i:i + 1], min_val=-NT * NG, max_val=NG - 1)
                                    for i in range(NT)]
                        dve.wait_ge(*at("edge keys"))
                    with dve.Fori(passes[d], passes[d + 1]) as g:
                        group = nc.s_assert_within(g + shift_of[d], 0, NG - 1, skip_runtime_bounds_check_because=
                                                   "a pass's group lies between its tile's first and last")
                        for i in range(EG):
                            dve.wait_ge(sems[f"onehot_used{i}"], g + 1)
                            V.tensor_scalar(srcs[:, i, :], iota16[:, :], edgef[:, 0, bass.ds(group * EG + i, 1)],
                                            None, ALU.is_equal)
                            V.tensor_scalar(dsts[:, i, :P], iota16[:, P * d:P * d + P],
                                            edgef[:, 1, bass.ds(group * EG + i, 1)], None,
                                            ALU.is_equal).then_inc(sems[f"onehot{i}"], 1)
                    if d:
                        sum_relations(d - 1)
                    if d == NT - 1:
                        sum_relations(d)
                        mask()
                        V.tensor_scalar(cnt1[:, :, :], cnt[:, :, :], 1.0, None, ALU.max).then_inc(
                            *up("count_step", "degree floor"))
                        V.tensor_scalar(got[:, :, :], cnt[:, :, :], 1.0, None, ALU.min)
                        dve.wait_ge(*at("degree floor"))
                        V.reciprocal(cnt1[:, :, :], cnt1[:, :, :]).then_inc(*up("count_step", "degree inverse"))
                        dve.wait_ge(*at("degree inverse"))
                        V.tensor_tensor(inv[:, :, :], cnt1[:, :, :], got[:, :, :], ALU.mult).then_inc(
                            *up("count_step", "inverse degrees"))
                elif kind in ("project", "project2", "relation"):
                    w = s[-1]
                    if kind == "relation" and s[1:3] == (1, 0):
                        r = s[3]
                        if r == 0:
                            V.memset(MT[:, :, :, :, N:NP].bitcast(F32), 0.0).then_inc(*up("mean_step", "MT pad"))
                            dve.wait_ge(*at("counts in"))
                        for d in range(NT):
                            if r and d == 0:
                                dve.wait_ge(*at("filled", "mean_T", r - 1, NT - 1))
                            V.tensor_scalar(mean[:, d, :], cr_in[:, d, N * r:N * r + N], inv[:, d, r:r + 1], None,
                                            ALU.mult).then_inc(*up("mean_step", "rows ready", "mean_T", r, d))
                    if kind != "relation":
                        i = gat_projects.index(s)
                        dve.wait_ge(*at("vectors in", i, 1))
                    for g, (s0, ns, pitch) in enumerate(groups(w)):
                        q = fill_of["rows", s, g]
                        dve.wait_ge(*at("rows hi", s, g))
                        last = minus_hi(row_dest(s, s0, ns, 1, w), psum_rows(q, ns, pitch, w),
                                        row_dest(s, s0, ns, 0, w))
                        last.then_inc(*up("lo_ready", "rows lo", s, g))
                        if kind == "relation":
                            G.same(("rows lo", s, g), "free", q)
                            continue
                        for t in range(ns):
                            for part, c0, pw in pieces(s):
                                for v in range(2):
                                    j = junks[0]
                                    junks[0] += 1
                                    if j >= 2:
                                        dve.wait_ge(*at("dot", j - 2))
                                    V.tensor_tensor_reduce(
                                        out=junk[:, j % 2, :pw],
                                        in0=slot(q)[:P, t * pitch + c0:t * pitch + c0 + pw],
                                        in1=ab[:, i % 2, v, c0:c0 + pw], scale=1.0, scalar=0.0, op0=ALU.mult,
                                        op1=ALU.add, accum_out=asp[:, v, part, s0 + t:s0 + t + 1]).then_inc(
                                        *up("rows_used", "dot", j))
                        G.same(("dot", junks[0] - 1), "free", q)
                    if kind != "relation":
                        G.same(("dot", junks[0] - 1), "vectors read", i)
                        G.same(("dot", junks[0] - 1), "dots", s)
                elif kind == "scores":
                    l, h = s[1:]
                    n = heads_order[s[1:]]
                    hb = n % 2
                    heads = GAT_HEADS[l][0]
                    dve.wait_ge(*at("dots", last_piece(s)))
                    if n >= 2:
                        dve.wait_ge(*at("filled", "scores", *list(heads_order)[n - 2]))
                    if h == heads:
                        V.tensor_tensor(asq[:, :, :], asp[:, :, 0, :], asp[:, :, 1, :], ALU.add).then_inc(
                            *up("scores_step", "two parts", l))
                        dve.wait_ge(*at("two parts", l))
                        V.tensor_tensor(asad[:, hb, :, :], asq[:, :, :], asp[:, :, 2, :], ALU.add).then_inc(
                            *up("scores_step", "scores col", l, h))
                    elif l < 3:
                        V.tensor_tensor(asad[:, hb, :, :], asp[:, :, 0, :], asp[:, :, 1, :], ALU.add).then_inc(
                            *up("scores_step", "scores col", l, h))
                    else:
                        V.tensor_copy(asad[:, hb, :, :], asp[:, :, h, :]).then_inc(
                            *up("scores_step", "scores col", l, h))
                    dve.wait_ge(*at("score rows", n, 1))
                    if n:
                        prev = list(heads_order)[n - 1]
                        dve.wait_ge(*at("filled", "attention_T", *prev, NT - 1))
                        dve.wait_ge(*at("exp", soft_order[(*prev, NT - 1)]))
                    for d in range(NT):
                        V.tensor_tensor_reduce(out=prob[:, d, :N], in0=asb[:, :N], in1=negm[:, d, :N], scale=1.0,
                                               scalar=FLOOR, op0=ALU.add, op1=ALU.max,
                                               accum_out=mx[:, d:d + 1]).then_inc(
                            *up("scores_step", "masked", n, d))
                    G.same(("masked", n, NT - 1), "scores read", n)
                    ad = asad[:, hb, 1, :]
                    dve.wait_ge(*at("masked", n, NT - 1))
                    V.tensor_tensor(z[:, :], mx[:, :], ad, ALU.add).then_inc(*up("scores_step", "top score", n))
                    dve.wait_ge(*at("top score", n))
                    V.scalar_tensor_tensor(out=mrow[:, :], in0=z[:, :], scalar=SLOPE, in1=z[:, :], op0=ALU.mult,
                                           op1=ALU.max).then_inc(*up("scores_step", "row max", n))
                    dve.wait_ge(*at("row max", n))
                    V.tensor_tensor(sh1[:, :], ad, mrow[:, :], ALU.subtract).then_inc(
                        *up("scores_step", "shift one", n))
                    V.scalar_tensor_tensor(out=sh2[:, :], in0=ad, scalar=SLOPE, in1=mrow[:, :], op0=ALU.mult,
                                           op1=ALU.subtract).then_inc(*up("scores_step", "shift", l, h))
                elif kind == "softmax":
                    l, h, d = s[1:]
                    n = soft_order[s[1:]]
                    dve.wait_ge(*at("exp", n))
                    V.tensor_tensor(prob[:, d, :N], prob[:, d, :N], e2[:, n % 2, :N], ALU.max).then_inc(
                        *up("prob_step", "prob max", n))
                    dve.wait_ge(*at("prob max", n))
                    V.tensor_tensor_reduce(out=prob[:, d, :N], in0=prob[:, d, :N], in1=Cg[:, d, :N], scale=1.0,
                                           scalar=0.0, op0=ALU.mult, op1=ALU.add,
                                           accum_out=den[:, d:d + 1]).then_inc(*up("prob_step", "prob mass", n))
                elif kind == "normalise":
                    l, h = s[1:]
                    n = heads_order[s[1:]]
                    dve.wait_ge(*at("prob mass", soft_order[l, h, NT - 1]))
                    V.tensor_scalar(dene[:, :], den[:, :], 1e-16, None, ALU.add).then_inc(
                        *up("prob_step", "denominator", n))
                    dve.wait_ge(*at("denominator", n))
                    if n:
                        dve.wait_ge(*at("rows ready", "attention_T", *list(heads_order)[n - 1], NT - 1))
                    V.reciprocal(rden[:, :], dene[:, :]).then_inc(*up("prob_step", "rden", l, h))
                elif kind == "attention_T":
                    for j in range(NT):
                        transposed_lo(s, j, AT[:, j, :, :], "att")
                elif kind == "mean_T":
                    for j in range(NT):
                        transposed_lo(s, j, MT[:, s[1], j, :, :], "mean")
                elif kind == "aggregate":
                    l, h, f = s[1:]
                    n = agg_order[s[1:]]
                    m = 128 if l < 3 else 96
                    q = fill_of[s]
                    bcol = 4 * h + f if l < 3 else h
                    dve.wait_ge(*at("b1 in", l))
                    dve.wait_ge(*at("filled", *s))
                    if n:
                        dve.wait_ge(*at("elu sum", n - 1))
                    if (h, f) == (0, 0) and l:
                        for b in range(2):
                            dve.wait_ge(*at("x stored", xr[("output", 0, NT - 1) if l == 1 else
                                                           ("row_part", 1, NT - 1)] - b))
                    V.tensor_scalar(h2(mn[:m, :]), halves(q, m), b1t[:m, bcol:bcol + 1], 0.0, ALU.add,
                                    ALU.min).then_inc(*up("elu_step", "elu min", n))
                    finish_tile()
                    dve.wait_ge(*at("elu exp", n))
                    V.scalar_tensor_tensor(out=rl[:m, n % 2, :], in0=mn[:m, :], scalar=-1.0, in1=rl[:m, n % 2, :],
                                           op0=ALU.add, op1=ALU.add).then_inc(*up("elu_step", "elu sum", n))
                    last_tile = (*x2_place(l, h, f), m, n % 2, ("x2 hi", n), ("x2 lo", *agg_key(l, h, f)))
                elif kind == "output":
                    l, d = s[1:]
                    i = xr[s]
                    q = fill_of[s]
                    dve.wait_ge(*at("b2 in", l))
                    dve.wait_ge(*at("x in", i))
                    V.tensor_tensor(xl[:, i % 2, :], xl[:, i % 2, :], b2b[:, :], ALU.add).then_inc(
                        *up("dve_step", "x and bias", i))
                    dve.wait_ge(*at("x and bias", i))
                    dve.wait_ge(*at("filled", *s))
                    if d >= 2:
                        dve.wait_ge(*at("x stored", i - 2))
                        if l < 3:
                            dve.wait_ge(*at("norm rows", l + 1, d - 2))
                    V.tensor_tensor(xo[:, i % 2, :].rearrange("p (c n) -> p c n", c=2), halves(q, P, 384),
                                    xl[:, i % 2, :].rearrange("p (c n) -> p c n", c=2), ALU.add).then_inc(
                        *up("x_added", "x added", i))
                    G.same(("x added", i), "free", q)
                    G.same(("x added", i), "x read", i)
                    if l < 3:
                        dve.wait_ge(*at("x added", i))
                        n = norm_order[norm_of[s]]
                        stats(n, xo[:, i % 2, :])
                        shift(n)
                elif kind == "embed":
                    dve.wait_ge(*at("emb in"))
                    V.tensor_copy(ntf[:, :], nti[:, :]).then_inc(*up("embed", "types float"))
                    V.memset(nth[:, N:NP].bitcast(F32), 0.0).then_inc(*up("embed", "types pad"))
                    dve.wait_ge(*at("relation ids"))
                    V.tensor_copy(rid[:, :], rii[:, :]).then_inc(*up("embed", "ids float"))
                    V.tensor_copy(emh[:, 0, :], emf[:, :]).then_inc(*up("embed", "emb hi"))
                    dve.wait_ge(*at("emb hi"))
                    minus_hi(emh[:, 1, :], emf[:, :], emh[:, 0, :])
                    V.tensor_scalar(nth[:, :N], ntf[:, :], rid[:, :], None, ALU.is_equal).then_inc(
                        *up("embed", "embed operands"))
                    V.memset(XA[:, 0:6, :, N:NP].bitcast(F32), 0.0).then_inc(*up("embed", "XA pad"))
                    dve.wait_ge(*at("embed hi"))
                    minus_hi(h2(XA[:TD, 6, 1, :]), halves(fill_of[s], TD), h2(XA[:TD, 6, 0, :])).then_inc(
                        *up("embed", "embed lo"))
                    G.same(("embed lo",), "free", fill_of[s])
                elif kind == "combine":
                    _, i, c, f = s
                    n = combine_order[s]
                    q = fill_of[s]
                    col = RGCN_CHUNKS[i][c][0] // 128 + f
                    bcol = col + (7 if i == 2 else 0)
                    dve.wait_ge(*at("b1 in", 2))
                    dve.wait_ge(*at("filled", *s))
                    if n < 2:
                        dve.wait_ge(*at("x stored", xr["output", 1, NT - 1 - n]))
                    else:
                        dve.wait_ge(*at("stage lo", *combine_list[n - 2][1:]))
                    V.tensor_scalar(h2(rl[:, n % 2, :]), halves(q, 128), b1t[:, bcol:bcol + 1], 0.0, ALU.add,
                                    ALU.max).then_inc(*up("elu_step", "stage relu", *s[1:]))
                    G.same(("stage relu", *s[1:]), "free", q)
                    finish_tile()
                    last_tile = (XB if i == 1 else XA, col, 128, n % 2, ("stage hi", *s[1:]), ("stage lo", *s[1:]))
                elif kind == "row_part":
                    c, d = s[1:]
                    i = xr[s]
                    g, t = d // 2, d % 2
                    q = fill_of["rows", ("combine_rows", c), g]
                    c0 = 384 * c
                    dve.wait_ge(*at("b3 in"))
                    dve.wait_ge(*at("filled", "rows", ("combine_rows", c), g))
                    if d >= 2 or c:
                        dve.wait_ge(*at("x stored", i - 2))
                    if c and d >= 2:
                        dve.wait_ge(*at("norm rows", 3, d - 2))
                    xh = xo[:, i % 2, c0:c0 + 384]
                    V.tensor_tensor(xh, slot(q)[:P, t * BANK:t * BANK + 384], b3b[:, c0:c0 + 384],
                                    ALU.add).then_inc(*up("dve_step", "part and bias", c, d))
                    if t == 1 or d == NT - 1:
                        G.same(("part and bias", c, d), "free", q)
                    dve.wait_ge(*at("part and bias", c, d))
                    dve.wait_ge(*at("x in", i))
                    last = V.scalar_tensor_tensor(out=xh, in0=xh, scalar=0.0, in1=xl[:, i % 2, c0:c0 + 384],
                                                  op0=ALU.max, op1=ALU.add)
                    if c:
                        last = V.tensor_copy(xo[:, i % 2, :384], xl[:, i % 2, :384])
                    last.then_inc(*up("x_added", "x added", i))
                    G.same(("x added", i), "x read", i)
                    if c:
                        dve.wait_ge(*at("x added", i))
                        n = norm_order[(3, d)]
                        stats(n, xo[:, i % 2, :])
                        shift(n)
                elif kind == "graph_again":
                    dve.wait_ge(*at("filled", "rows", ("combine_rows", 1), 2))
                    V.memset(AT[:, :, :, N:NP].bitcast(F32), 0.0).then_inc(*up("graph", "AT pad again"))
                    dve.wait_ge(*at("graph in"))
                    mask()
    return G.seen


def describe(nc, inputs):
    arrays = {}
    for name, a in inputs.items():
        arrays[name] = nc.dram_tensor(f"in_{name}", a.shape, mybir.dt.from_np(a.dtype), kind="ExternalInput").ap()
    return arrays, nc.dram_tensor("out_x", (N, D), F32, kind="ExternalOutput").ap()


def laid_out(k):
    c = np.ascontiguousarray
    edges = np.stack([k["src"], k["dst"], k["edge_type_3"]]).reshape(3, ET, P)
    out = {"x": c(k["x"]), "edges": c(edges.transpose(2, 0, 1)), "dst": c(k["dst"].reshape(NG, EG * P)), "node_type": c(k["node_type_3"]),
           "emb": c(k["L2_gnn_node_emb"])}
    names = {0: ("a1_src", "a1_dst", "a2_src", "a2_dst"), 1: ("att_src1", "att_dst1", "att_src2", "att_dst2"),
             3: ("a_src1", "a_dst1", "a_src2", "a_dst2")}
    for l, (s1, d1, s2, d2) in names.items():
        g = f"L{l}_gnn_"
        rows = 128 if l < 3 else 96
        out[f"W1_{l}"], out[f"W2_{l}"] = c(k[g + "W1"]), c(k[g + "W2"])
        out[f"a1src_{l}"], out[f"a1dst_{l}"] = c(k[g + s1].reshape(-1)), c(k[g + d1].reshape(-1))
        out[f"a2src_{l}"], out[f"a2dst_{l}"] = c(k[g + s2].reshape(-1)), c(k[g + d2].reshape(-1))
        out[f"b1_{l}"] = c(k[g + "b1"].reshape(-1, rows).T)
        out[f"b2_{l}"] = c(k[g + "b2"])
    for i in (1, 2, 3):
        out[f"rel_{i}"], out[f"root_{i}"] = c(k[f"L2_gnn_w_rel{i}"]), c(k[f"L2_gnn_w_root{i}"])
    out["b1_2"] = c(np.concatenate([k["L2_gnn_b1"].reshape(-1, 128).T, k["L2_gnn_b2"].reshape(-1, 128).T], axis=1))
    out["b3_3"] = c(k["L2_gnn_b3"])
    return out


def kernel(**inputs):
    import concourse.bacc as bacc
    from concourse.bass_utils import run_bass_kernel_spmd

    arrays = laid_out({n: np.asarray(a) for n, a in inputs.items()})
    known = {}
    for _ in range(2):
        nc = bacc.Bacc("TRN2", target_bir_lowering=False, num_devices=1, dynamic_dma_scratch_size=SCRATCH)
        I, out = describe(nc, arrays)
        known = build(nc, I, out, known)
    r = run_bass_kernel_spmd(nc, [{f"in_{n}": a for n, a in arrays.items()}], core_ids=[0])
    return r.results[0]["out_x"]
```

```python
import numpy as np
import concourse.bass as bass
from concourse import mybir
from contextlib import ExitStack

F32, F32R, F16, BF16 = mybir.dt.float32, mybir.dt.float32r, mybir.dt.float16, mybir.dt.bfloat16
U16, I32 = mybir.dt.uint16, mybir.dt.int32
ALU, ACT, AX = mybir.AluOpType, mybir.ActivationFunctionType, mybir.AxisListType

N, D, E, R, TD = 625, 768, 10000, 3, 128
NT = 5
P = N // NT
NP = 628
HC = NP // 2
ET = E // P
EG = 4
NG = ET // EG
BANK = 512
BANKS = 8
STAGES, PAIRS = 3, 5
AHEAD = PAIRS - 1
WMAX = 384
SLOPE, EPS, ABSENT, FLOOR = 0.2, 1e-5, -1e37, -1e30
PASSES = ((0, 0), (0, 1), (1, 0))
GAT_HEADS = {0: (4, 512), 1: (4, 512), 3: (8, 96)}
RGCN_IN = {1: 7, 2: 7, 3: 6}
RGCN_CHUNKS = {1: ((0, 384), (384, 256), (640, 256)), 2: ((0, 384), (384, 384)), 3: ((0, 384), (384, 384))}
SCRATCH = 512


class Signals:

    def __init__(self, sems, known):
        self.sems, self.known, self.counts, self.seen = sems, known, dict.fromkeys(sems, 0), {}

    def up(self, name, *key, by=1):
        self.counts[name] += by
        self.seen[key] = (name, self.counts[name])
        return self.sems[name], by

    def same(self, key, *other):
        self.seen[other] = self.seen[key]

    def at(self, *key):
        name, value = self.known.get(key, (next(iter(self.sems)), 1))
        return self.sems[name], value


def groups(w):
    return ((0, 4, 256), (4, 1, 256)) if w <= 256 else ((0, 2, BANK), (2, 2, BANK), (4, 1, BANK))


def tick(l, h, t):
    if 0 <= t < NT:
        yield ("score_rows", l, h, t)
    if 1 <= t <= NT:
        yield ("softmax", l, h, t - 1)
    if 3 <= t < NT + 3:
        yield ("attention_T", l, h, t - 3)


def gat_steps(l):
    heads, dh = GAT_HEADS[l]
    if l == 3:
        yield ("project", l, 0, 384)
        yield ("rows", ("project", l, 0, 384))
        yield ("project", l, 1, 384)
        yield ("rows", ("project", l, 1, 384))
        for t in range(heads * NT + 3):
            h, d = t // NT, t % NT
            if h < heads:
                if d == 0:
                    yield ("scores", l, h)
                yield ("score_rows", l, h, d)
            if h > 1 and d == 2:
                yield ("elu_sum", l, h - 2, 0)
            if 0 < t <= heads * NT:
                yield ("softmax", l, (t - 1) // NT, (t - 1) % NT)
            if h > 1 and d == 2:
                yield ("elu_high", l, h - 2, 0)
            if t >= 3:
                yield ("attention_T", l, (t - 3) // NT, (t - 3) % NT)
            if h and d == 4:
                yield ("aggregate", l, h - 1, 0)
            if h > 1 and d == 1:
                yield ("elu", l, h - 2, 0)
        h = heads - 1
        yield ("aggregate", l, h, 0)
        yield from (("elu", l, h, 0), ("elu_sum", l, h, 0), ("elu_high", l, h, 0))
    else:
        for h in range(heads + 1):
            new = [("project", l, 2 * h + i, 256) for i in range(2)]
            old = h - 1
            if h < heads:
                yield new[0]
            if h:
                yield ("score_rows", l, old, 4)
                if h > 1:
                    yield ("elu_sum", l, h - 2, 3)
                yield ("softmax", l, old, 3)
                if h > 1:
                    yield ("elu_high", l, h - 2, 3)
            if h < heads:
                yield ("split", new[0], 1)
            if h:
                yield ("softmax", l, old, 4)
            if h < heads:
                yield ("rows", new[0])
            if h:
                for d in range(2, NT):
                    yield ("attention_T", l, old, d)
            if h < heads:
                yield new[1]
                yield ("rows", new[1])
            for f in range(4):
                if h:
                    yield ("aggregate", l, old, f)
                if h < heads:
                    if f == 0:
                        yield ("scores", l, h)
                    else:
                        yield ("score_rows", l, h, f)
                if h and f:
                    yield ("elu_sum", l, old, f - 1)
                if h < heads and f:
                    yield ("softmax", l, h, f - 1)
                if h and f:
                    yield ("elu_high", l, old, f - 1)
                if h:
                    yield ("elu", l, old, f)
                if h < heads and f == 0:
                    yield ("score_rows", l, h, f)
            if h < heads:
                yield ("attention_T", l, h, 0)
                yield ("attention_T", l, h, 1)
        yield from (("elu_sum", l, heads - 1, 3), ("elu_high", l, heads - 1, 3))
    h = heads
    for c in range(3):
        yield ("project2", l, c, 256)
        yield ("rows", ("project2", l, c, 256))
    yield ("scores", l, h)
    for t in range(NT + 3):
        yield from tick(l, h, t)
        if t >= 4:
            yield ("output", l, t - 4)
            if t > 4 and l != 3:
                yield ("norm_T", l + 1, t - 5)
    yield ("output", l, NT - 1)
    if l != 3:
        yield ("norm_T", l + 1, NT - 2)
        yield ("norm_T", l + 1, NT - 1)


def rgcn_steps():
    yield ("embed",)
    for i in (1, 2, 3):
        for c, (f0, w) in enumerate(RGCN_CHUNKS[i]):
            for r in range(R):
                yield ("relation", i, c, r, w)
                yield ("rows", ("relation", i, c, r, w))
                if i == 1 and c == 0:
                    for d in range(NT):
                        yield ("mean_T", r, d)
            if i < 3:
                for f in range(w // 128):
                    yield ("combine", i, c, f)
            else:
                yield ("combine_rows", c)
                for d in range(NT):
                    yield ("row_part", c, d)
                    if d and c:
                        yield ("norm_T", 3, d - 1)
    yield ("norm_T", 3, NT - 1)


def steps():
    yield ("bounds",)
    for d in range(NT):
        yield ("load_x", d)
        if d:
            yield ("norm_T", 0, d - 1)
    yield ("norm_T", 0, NT - 1)
    for d in range(NT):
        yield ("count", d)
    yield from gat_steps(0)
    yield from gat_steps(1)
    yield from rgcn_steps()
    yield ("graph_again",)
    yield from gat_steps(3)


def weight_tiles(I):
    out = {}
    for l, (heads, dh) in GAT_HEADS.items():
        w1, w2 = I[f"W1_{l}"], I[f"W2_{l}"]
        rows = 128 if l < 3 else 96
        for s in gat_steps(l):
            if s[0] == "project":
                c, w = s[2:]
                out[s] = [(w1[128 * k:128 * k + 128, c * w:c * w + w], 128, w) for k in range(6)]
            if s[0] == "project2":
                c, w = s[2:]
                out[s] = [(w2[rows * k:rows * k + rows, c * w:c * w + w], rows, w)
                          for k in range(heads * dh // rows)]
    for s in rgcn_steps():
        if s[0] == "relation":
            _, i, c, r, w = s
            f0 = RGCN_CHUNKS[i][c][0]
            out[s] = [(I[f"rel_{i}"][r, 128 * k:128 * k + 128, f0:f0 + w], 128, w) for k in range(RGCN_IN[i])]
        if s[0] == "combine":
            _, i, c, f = s
            f0 = RGCN_CHUNKS[i][c][0] + 128 * f
            out[s] = [(I[f"root_{i}"][128 * k:128 * k + 128, f0:f0 + 128], 128, 128) for k in range(RGCN_IN[i])]
        if s[0] == "combine_rows":
            f0, w = RGCN_CHUNKS[3][s[1]]
            out[s] = [(I["root_3"][128 * k:128 * k + 128, f0:f0 + w], 128, w) for k in range(RGCN_IN[3])]
    return out


def build(nc, I, out, known):
    ctx = ExitStack()
    with ctx:
        STEPS = list(steps())
        tiles_of = weight_tiles(I)
        first_tile, W = {}, []
        for s in STEPS:
            first_tile[s] = len(W)
            W += tiles_of.get(s, [])
        wend = {s: first_tile[s] + len(tiles_of.get(s, [])) for s in STEPS}

        def split_limit(s):
            if s[0] == "split":
                return first_tile[s[1]] + s[2] + 1 + AHEAD
            return wend[s] + AHEAD if s[0] in ("rows", "combine", "combine_rows") else 0

        names = ["psum_filled", "psum_free_dve", "psum_free_act", "weights_used", "weights_hi", "weights_lo",
                 "hi_ready", "lo_ready", "rows_used", "norm_stats", "norm_rows", "norm_scale", "input_hi",
                 "input_lo", "scores_step", "score_rows", "mask_rows", "relu_rows", "masked", "exp_ready", "prob_step", "prob_ready",
                 "x_bias",
                 "att_hi", "att_lo", "elu_step", "elu_relu", "elu_exp", "x2_hi", "x2_lo", "dve_step",
                 "count_step", "bounds_step", "bounds", "bounds_rows", "count_rows", "edge_sums", "graph", "pool_const", "pool_step", "x_added", "embed", "embed_hi", "mean_step"]
        names += [f"onehot{i}" for i in range(EG)] + [f"onehot_used{i}" for i in range(EG)]
        dmas = ([f"weight_in{i}" for i in range(STAGES)] + [f"x_in{i}" for i in range(2)]
                + [f"x_out{i}" for i in range(2)] + [f"att_vec{i}" for i in range(2)]
                + ["edges_in", "bias_in", "bias2_in", "small_in", "counts_out0", "counts_out1", "counts_in", "graph_out0",
                   "graph_out1", "graph_in"])
        sems = {n: ctx.enter_context(nc.semaphore(n)) for n in names + dmas}
        G = Signals(sems, known)
        up, at = G.up, G.at

        base = -(-nc.sbuf_base // 32) * 32
        def sb(name, shape, dt, off):
            off = -(-off // 32) * 32
            return nc.alloc_sbuf_tensor_at(name, shape, dt, offset=base + off)
        tile_b = 2 * NP * 4
        XB = sb("XB", [128, 7, 2, NP], F32R, 0)
        o1 = 7 * tile_b
        XA = sb("XA", [128, 9, 2, NP], F32R, o1)
        og = o1 + 9 * tile_b
        def sg(name, shape, dt, size):
            nonlocal og
            t = sb(name, shape, dt, og)
            og += -(-size // 32) * 32
            return t
        Hg = sg("Hg", [P, NT, 2, 1024], F32R, NT * 2 * 1024 * 4)
        AT = sg("AT", [P, NT, 2, NP], F32R, NT * 2 * NP * 4)
        oprob = og
        prob = sg("prob", [P, NT, NP], F32, NT * NP * 4)
        Cg = sg("Cg", [P, NT, NP], U16, NT * NP * 2)
        negm = sg("negm", [P, NT, NP], BF16, NT * NP * 2)
        asb = sg("asb", [P, 2, NP], F32, 2 * NP * 4)
        b2b = sg("b2b", [P, D], F32, D * 4)
        ab = sg("ab", [P, 2, 2, WMAX], F32, 4 * WMAX * 4)
        mx = sg("mx", [P, NT], F32, 32)
        den = sg("den", [P, NT], F32, 32)
        dene = sg("dene", [P, NT], F32, 32)
        rden = sg("rden", [P, NT], F32, 32)
        asp = sg("asp", [P, 2, 8, NT], F32, 2 * 8 * NT * 4)
        asq = sg("asq", [P, 2, NT], F32, 2 * NT * 4)
        ad8 = sg("ad8", [P, 2, NT], F32, 2 * NT * 4)
        asad = sg("asad", [P, 2, 2, NT], F32, 4 * NT * 4)
        junk = sg("junk", [P, 2, WMAX], BF16, 4 * WMAX)
        ol = o1 + 7 * tile_b
        MT = sb("MT", [P, R, NT, 2, NP], F32R, ol); ol += R * NT * 2 * NP * 4
        Hl = sb("Hl", [P, NT, R, 2, WMAX], F32R, ol); ol += NT * R * 2 * WMAX * 4
        cr_in = sb("cr_in", [P, NT, R * N], U16, 0)
        mean = sb("mean", [P, NT, N], F32, NT * R * N * 2)
        b3b = sb("b3b", [P, D], F32, 6 * tile_b)
        oc = o1
        def sc(name, shape, dt, size):
            nonlocal oc
            t = sb(name, shape, dt, oc)
            oc += -(-size // 32) * 32
            return t
        CW = R * N + 1
        iota32 = sc("iota32", [P, CW], I32, CW * 4)
        iota16 = sc("iota16", [P, CW], F16, CW * 2)
        srcs = sc("srcs", [P, EG, CW], F16, EG * CW * 2)
        dsts = sc("dsts", [P, EG, 128], F16, EG * 256)
        zero16 = sc("zero16", [1, BANK], F16, BANK * 2)
        gdst32 = sc("gdst32", [NG, EG * P], I32, EG * P * 4)
        gspan = sc("gspan", [NG, 2], F32, 8)
        gid32 = sc("gid32", [NG, 1], I32, 4)
        gid = sc("gid", [NG, 2], F32, 8)
        first32 = sc("first32", [NG, NT], I32, 4 * NT)
        first = sc("first", [NG, 2, NT], F32, 8 * NT)
        touch = sc("touch", [NG, 3, NT], F32, 12 * NT)
        reach = sc("reach", [1, 2, NT], F32, 8 * NT)
        span = sc("span", [1, 4, NT + 1], F32, 16 * NT + 16)
        bounds = sc("bounds", [1, 2, NT + 1], I32, 8 * NT + 8)
        cr = sc("cr", [P, 2, CW], U16, 2 * CW * 2)
        cn = sc("cn", [P, 2, NP], U16, 2 * NP * 2)
        edge32 = sc("edge32", [P, 3, ET], I32, 3 * ET * 4)
        edgef = sc("edgef", [P, 3, ET], F32, 3 * ET * 4)
        cnt = sc("cnt", [P, NT, R], F32, 60)
        cnt1 = sc("cnt1", [P, NT, R], F32, 60)
        got = sc("got", [P, NT, R], F32, 60)
        oa = -(-max(og, ol) // 32) * 32
        def sa(name, shape, dt, size):
            nonlocal oa
            t = sb(name, shape, dt, oa)
            oa += -(-size // 32) * 32
            return t
        stage = sa("stage", [128, STAGES, WMAX], F32, STAGES * WMAX * 4)
        pairs = sa("pairs", [128, PAIRS, 2, WMAX], F32R, PAIRS * 2 * WMAX * 4)
        ort = oa
        mn = sa("mn", [128, NP], F32, NP * 4)
        rl = sa("rl", [128, 2, NP], F32, 2 * NP * 4)
        msk = sa("msk", [P, 2, NP], F32, 2 * NP * 4)
        xl = sb("xl", [P, 2, D], F32, ort)
        xo = sb("xo", [P, 2, D], F32, ort + 2 * D * 4)
        assert 4 * D * 4 <= 5 * NP * 4
        hn = sa("hn", [P, D], F32, D * 4)
        ident = sa("ident", [128, 128], F32, 512)
        b1t = sa("b1t", [128, 16], F32, 64)
        bns = sa("bns", [P, 2, 2, 6], F32, 96)
        mv = sa("mv", [P, 2, 2], F32, 16)
        ve = sa("ve", [P, 2, 1], F32, 8)
        rstd = sa("rstd", [P, 2, 1], F32, 8)
        nb = sa("nb", [P, 2, 1], F32, 8)
        mhalf = sa("mhalf", [P, 1], F32, 4)
        inv = sa("inv", [P, NT, R], F32, 60)
        nti = sb("nti", [R, N], I32, oprob)
        ntf = sb("ntf", [R, N], F32, oprob + tile_b)
        nth = sb("nth", [R, NP], F32R, oprob + 2 * tile_b)
        emf = sb("emf", [R, TD], F32, oprob + 3 * tile_b)
        emh = sb("emh", [R, 2, TD], F32R, oprob + 3 * tile_b + 512)
        rid = sb("rid", [R, 1], F32, oprob + 3 * tile_b + 1536)
        rii = sb("rii", [R, 1], I32, oprob + 3 * tile_b + 1568)
        assert base + oa <= nc.sbuf_usable_end, (base + oa, nc.sbuf_usable_end)

        x_scr = nc.dram_tensor("x_scratch", [3, N, D], F32).ap()
        cr_scr = nc.dram_tensor("relation_counts", [N, CW], U16).ap()
        cn_scr = nc.dram_tensor("edge_counts", [N, NP], U16).ap()

        ps = ctx.enter_context(nc.psum_tensor("ps", [128, BANKS * BANK], F32))

        fill_of, place, user = {}, [], {}

        def slot(q):
            s0 = place[q] * BANK
            return ps[:, s0:min(s0 + 2 * BANK, BANKS * BANK)]

        def halves(q, rows, n=HC):
            return slot(q).rearrange("p (c n) -> p c n", c=2)[:rows, :, :n]

        def pitched(q):
            return slot(q)[:P, :NT * 128].rearrange("p (j c) -> p j c", j=NT)[:, :, :P]

        def h2(ap):
            return ap.rearrange("p (c n) -> p c n", c=2)

        def source(s):
            if s[0] == "project":
                return [(XB, k, 128) for k in range(6)]
            if s[0] == "project2":
                if s[1] == 3:
                    return [(XA, k, 96) for k in range(8)]
                return [(XA, k, 128) if k < 9 else (XB, k - 9, 128) for k in range(16)]
            return [((XB if s[1] == 2 else XA), k, 128) for k in range(RGCN_IN[s[1]])]

        def source_ready(s, k):
            if s[0] == "project":
                return ("input lo", s[1], NT - 1)
            if s[0] == "project2":
                return ("x2 lo", s[1], k) if s[1] == 3 else ("x2 lo", s[1], k // 4, k % 4)
            if s[1] == 1:
                return ("embed lo",) if k == 6 else ("input lo", 2, NT - 1)
            c = next(c for c, (f0, w) in enumerate(RGCN_CHUNKS[s[1] - 1]) if f0 <= 128 * k < f0 + w)
            return ("stage lo", s[1] - 1, c, k - RGCN_CHUNKS[s[1] - 1][c][0] // 128)

        def row_dest(s, s0, n, part, w):
            if s[0] == "project":
                c0 = s[2] * w % 1024
                return Hg[:, s0:s0 + n, part, c0:c0 + w]
            if s[0] == "project2":
                return Hg[:, s0:s0 + n, part, s[2] * w:s[2] * w + w]
            return Hl[:, s0:s0 + n, s[3], part, :w]

        def psum_rows(q, n, pitch, w):
            return slot(q)[:P, :n * pitch].rearrange("p (n c) -> p n c", n=n)[:, :, :w]

        def att_of(l, h):
            return XB if l == 3 and h % 2 else AT

        gat_projects = [s for s in STEPS if s[0] in ("project", "project2")]
        loads_x = [s for s in STEPS if s[0] in ("load_x", "output", "combine_rows")]

        def pieces(s):
            if s[0] == "project" and s[1] == 3:
                return [(4 * s[2] + i, 96 * i, 96) for i in range(4)]
            return [(s[2] if s[0] == "project2" else s[2] % 2, 0, s[3])]

        def last_piece(s):
            _, l, h = s
            heads = GAT_HEADS[l][0]
            if h == heads:
                return ("project2", l, 2, 256)
            return ("project", l, 2 * h + 1, 256) if l < 3 else ("project", l, h // 4, 384)

        heads_order = {s[1:]: i for i, s in enumerate(x for x in STEPS if x[0] == "scores")}
        soft_order = {s[1:]: i for i, s in enumerate(x for x in STEPS if x[0] == "softmax")}
        agg_order = {s[1:]: i for i, s in enumerate(x for x in STEPS if x[0] == "aggregate")}
        agg_list = list(agg_order)
        norm_order = {s[1:]: i for i, s in enumerate(x for x in STEPS if x[0] == "norm_T")}
        norm_list = list(norm_order)
        norm_of = {("load_x", d): (0, d) for d in range(NT)}
        norm_of.update({("output", l, d): (l + 1, d) for l in (0, 1) for d in range(NT)})
        norm_of.update({("row_part", 1, d): (3, d) for d in range(NT)})
        xr_keys = ([("load_x", d) for d in range(NT)] + [("output", 0, d) for d in range(NT)]
                   + [("output", 1, d) for d in range(NT)] + [("row_part", c, d) for c in range(2) for d in range(NT)]
                   + [("output", 3, d) for d in range(NT)])
        xr = {k: i for i, k in enumerate(xr_keys)}
        combine_order = {s: i for i, s in enumerate(x for x in STEPS if x[0] == "combine")}
        combine_list = list(combine_order)

        def agg_key(l, h, f):
            return (l, h, f) if l < 3 else (l, h)

        def x2_place(l, h, f):
            if l == 3:
                return XA, h
            i = 4 * h + f
            return (XA, i) if i < 9 else (XB, i - 9)

        block = ctx.enter_context(nc.Block())

        @block.tensor
        def _(pe):
            mm = nc.tensor.matmul

            end = [0]

            def acquire(*key, banks=2):
                q = len(place)
                fill_of[key] = q
                start = end[0] if end[0] + banks <= BANKS else 0
                end[0] = start + banks
                place.append(start)
                mine = range(start, start + banks)
                for last_user in sorted({user[b] for b in mine if b in user}):
                    pe.wait_ge(*at("free", last_user))
                for b in mine:
                    user[b] = q
                return q

            pe.wait_ge(*at("ident",))
            for s in STEPS:
                kind = s[0]
                if kind in ("project", "project2", "relation"):
                    w = s[-1]
                    src = source(s)
                    gs = groups(w)
                    qs = []
                    waited = None
                    for k0 in range(0, len(src), 2):
                        block_k = range(k0, min(k0 + 2, len(src)))
                        for g, (s0, ns, pitch) in enumerate(gs):
                            if k0 == 0:
                                qs.append(acquire("rows", s, g, banks=-(-ns * pitch // BANK)))
                            for k in block_k:
                                X, xi, rows = src[k]
                                n = first_tile[s] + k
                                if g == 0:
                                    if source_ready(s, k) != waited:
                                        waited = source_ready(s, k)
                                        pe.wait_ge(*at(*waited))
                                    pe.wait_ge(*at("weights lo", n))
                                for t in range(ns):
                                    o = slot(qs[g])[:P, t * pitch:t * pitch + w]
                                    for i, (a, b) in enumerate(PASSES):
                                        last = mm(o, X[:rows, xi, a, P * (s0 + t):P * (s0 + t + 1)],
                                                  pairs[:rows, n % PAIRS, b, :w],
                                                  start=k == 0 and i == 0 and t * pitch % BANK == 0,
                                                  stop=k == len(src) - 1 and i == 2, skip_group_check=True)
                                if g == len(gs) - 1 and k < block_k[-1]:
                                    last.then_inc(*up("weights_used", "weights used", n))
                            if block_k[-1] == len(src) - 1:
                                last.then_inc(*up("psum_filled", "filled", "rows", s, g))
                        if block_k[-1] == len(src) - 1:
                            G.same(("filled", "rows", s, len(gs) - 1), "weights used", n)
                        else:
                            last.then_inc(*up("weights_used", "weights used", n))
                elif kind == "scores":
                    q = acquire(*s)
                    pe.wait_ge(*at("scores col", *s[1:]))
                    hb = heads_order[s[1:]] % 2
                    for j in range(NT):
                        last = nc.tensor.transpose(slot(q)[:P, 128 * j:128 * j + P],
                                                   asad[:, hb, 0, j:j + 1].to_broadcast([P, P]), ident[:P, :P])
                    last.then_inc(*up("psum_filled", "filled", *s))
                elif kind in ("attention_T", "mean_T"):
                    M = prob if kind == "attention_T" else mean
                    d = s[-1]
                    q = acquire(*s)
                    pe.wait_ge(*at("rows ready", *s))
                    for j in range(NT):
                        last = nc.tensor.transpose(slot(q)[:P, 128 * j:128 * j + P], M[:, d, P * j:P * j + P],
                                                   ident[:P, :P])
                    last.then_inc(*up("psum_filled", "filled", *s))
                elif kind == "aggregate":
                    _, l, h, f = s
                    heads, dh = GAT_HEADS[l]
                    q = acquire(*s)
                    m = 128 if l < 3 else 96
                    c0 = h % 2 * 512 + 128 * f if l < 3 else 96 * h
                    for c in range(2):
                        if f == 0:
                            pe.wait_ge(*at("att lo", l, h, 2 + 2 * c))
                        for t in range(NT):
                            for i, (a, b) in enumerate(PASSES):
                                last = mm(halves(q, m)[:, c, :], Hg[:, t, a, c0:c0 + m],
                                          att_of(l, h)[:P, t, b, HC * c:HC * c + HC],
                                          start=t == 0 and i == 0, stop=t == NT - 1 and i == 2)
                    last.then_inc(*up("psum_filled", "filled", *s))
                elif kind == "output":
                    _, l, d = s
                    q = acquire(*s)
                    pe.wait_ge(*at("att lo", l, GAT_HEADS[l][0], d))
                    for c in range(2):
                        for t in range(NT):
                            for i, (a, b) in enumerate(PASSES):
                                last = mm(halves(q, P, 384)[:, c, :], AT[:, t, a, P * d:P * d + P],
                                          Hg[:, t, b, 384 * c:384 * c + 384],
                                          start=t == 0 and i == 0, stop=t == NT - 1 and i == 2)
                    last.then_inc(*up("psum_filled", "filled", *s))
                elif kind == "norm_T":
                    q = acquire(*s)
                    pe.wait_ge(*at("norm rows", *s[1:]))
                    for k in range(6):
                        c0 = k * P if k < 3 else BANK + (k - 3) * P
                        last = nc.tensor.transpose(slot(q)[:, c0:c0 + P], hn[:, 128 * k:128 * k + 128], ident[:P, :P])
                    last.then_inc(*up("psum_filled", "filled", *s))
                elif kind == "bounds":
                    q = acquire(*s)
                    pe.wait_ge(*at("touched"))
                    for side in range(2):
                        for d in range(NT):
                            c0 = side * BANK + NG * d
                            last = nc.tensor.transpose(slot(q)[:1, c0:c0 + NG], touch[:, 1 + side, d:d + 1],
                                                       ident[:NG, :NG])
                    last.then_inc(*up("psum_filled", "filled", *s))
                elif kind == "count":
                    d = s[1]
                    if d == 0:
                        pe.wait_ge(*at("bounds"))
                        passes = [pe.value_load(bounds[0:1, 0, i:i + 1], min_val=0, max_val=NT * NG)
                                  for i in range(NT + 1)]
                    q = acquire(*s, banks=4)
                    o = ps[:P, place[q] * BANK:(place[q] + 4) * BANK]
                    for c in range(4):
                        last = mm(o[:, BANK * c:BANK * c + BANK], zero16[:, :P], zero16[:, :], start=True,
                                  stop=True, skip_group_check=True)
                        if d == 0:
                            last.then_inc(sems[f"onehot_used{c}"], 1)
                    with pe.Fori(passes[d], passes[d + 1]) as g:
                        for i in range(EG):
                            pe.wait_ge(sems[f"onehot{i}"], g + 1)
                            for c in range(4):
                                c1 = min(BANK * c + BANK, R * N)
                                last = mm(o[:, BANK * c:c1], dsts[:, i, :P], srcs[:, i, BANK * c:c1],
                                          start=False, stop=True, skip_group_check=True)
                            last.then_inc(sems[f"onehot_used{i}"], 1)
                    mm(o[:, :2], zero16[:, :P], zero16[:, :2], start=False, stop=True,
                       skip_group_check=True).then_inc(*up("psum_filled", "filled", *s))
                elif kind == "embed":
                    q = acquire(*s)
                    pe.wait_ge(*at("embed operands",))
                    for c in range(2):
                        for a in range(2):
                            last = mm(halves(q, TD)[:, c, :], emh[:, a, :], nth[:, HC * c:HC * c + HC],
                                      start=a == 0, stop=a == 1)
                    last.then_inc(*up("psum_filled", "filled", *s))
                elif kind == "combine":
                    _, i, c, f = s
                    q = acquire(*s)
                    src = source(("relation", i))
                    for k, (X, xi, rows) in enumerate(src):
                        n = first_tile[s] + k
                        pe.wait_ge(*at("weights lo", n))
                        for half in range(2):
                            for j, (a, b) in enumerate(PASSES):
                                last = mm(halves(q, 128)[:, half, :], pairs[:, n % PAIRS, a, :128],
                                          X[:, xi, b, HC * half:HC * half + HC],
                                          start=k == 0 and j == 0, stop=False)
                        last.then_inc(*up("weights_used", "weights used", n))
                    for r in range(R):
                        if f == 0:
                            g = len(groups(RGCN_CHUNKS[i][c][1])) - 1
                            pe.wait_ge(*at("rows lo", ("relation", i, c, r, RGCN_CHUNKS[i][c][1]), g))
                        if i == 1 and c == 0 and f == 0:
                            pe.wait_ge(*at("mean lo", r, NT - 1))
                        for half in range(2):
                            for t in range(NT):
                                for j, (a, b) in enumerate(PASSES):
                                    last = mm(halves(q, 128)[:, half, :], Hl[:, t, r, a, 128 * f:128 * f + 128],
                                              MT[:, r, t, b, HC * half:HC * half + HC],
                                              start=False, stop=r == R - 1 and t == NT - 1 and j == 2)
                    last.then_inc(*up("psum_filled", "filled", *s))
                elif kind == "combine_rows":
                    c = s[1]
                    gs = groups(384)
                    qs = []
                    src = source(("relation", 3))
                    for k0 in range(0, len(src), 2):
                        for g, (s0, ns, pitch) in enumerate(gs):
                            if k0 == 0:
                                qs.append(acquire("rows", s, g, banks=-(-ns * pitch // BANK)))
                            for k in (k0, k0 + 1):
                                X, xi, rows = src[k]
                                n = first_tile[s] + k
                                if g == 0:
                                    pe.wait_ge(*at("weights lo", n))
                                for t in range(ns):
                                    for j, (a, b) in enumerate(PASSES):
                                        last = mm(slot(qs[g])[:P, t * pitch:t * pitch + 384],
                                                  X[:, xi, a, P * (s0 + t):P * (s0 + t + 1)],
                                                  pairs[:, n % PAIRS, b, :384], start=k == 0 and j == 0, stop=False)
                                if g == len(gs) - 1:
                                    last.then_inc(*up("weights_used", "weights used", n))
                    for r in range(R):
                        pe.wait_ge(*at("rows lo", ("relation", 3, c, r, 384), len(gs) - 1))
                    for g, (s0, ns, pitch) in enumerate(gs):
                        for t in range(ns):
                            for r in range(R):
                                for u in range(NT):
                                    for j, (a, b) in enumerate(PASSES):
                                        last = mm(slot(qs[g])[:P, t * pitch:t * pitch + 384],
                                                  MT[:, r, u, a, P * (s0 + t):P * (s0 + t + 1)],
                                                  Hl[:, u, r, b, :384], start=False,
                                                  stop=r == R - 1 and u == NT - 1 and j == 2)
                        last.then_inc(*up("psum_filled", "filled", "rows", s, g))

        @block.sync
        def _(sp):
            loaded = [0]

            def load_weights(upto):
                while loaded[0] < min(upto, len(W)):
                    n = loaded[0]
                    ap, rows, w = W[n]
                    if n >= STAGES:
                        sp.wait_ge(*at("weights lo", n - STAGES))
                    sp.dma_start(stage[:rows, n % STAGES, :w], ap).then_inc(
                        *up(f"weight_in{n % STAGES}", "weights in", n, by=16))
                    loaded[0] += 1

            sp.dma_start(gdst32[:, :], I["dst"]).then_inc(*up("edges_in", "targets in", by=16))
            sp.dma_start(edge32[:, :, :], I["edges"]).then_inc(*up("edges_in", "edges in", by=16))
            for s in STEPS:
                if s[0] == "count":
                    d = s[1]
                    sp.wait_ge(*at("relation counts", d))
                    sp.dma_start(cr_scr[P * d:P * d + P, :R * N], cr[:, d % 2, :R * N]).then_inc(
                        *up(f"counts_out{d % 2}", "counts out", d, by=16))
                    sp.wait_ge(*at("edge counts", d))
                    sp.dma_start(cn_scr[P * d:P * d + P, :], cn[:, d % 2, :]).then_inc(
                        *up(f"graph_out{d % 2}", "graph out", d, by=16))
                load_weights(wend[s] + AHEAD + STAGES if s in tiles_of else STAGES)
            for d in (NT - 2, NT - 1):
                sp.wait_ge(*at("graph out", d))
                sp.wait_ge(*at("counts out", d))

        @block.gpsimd
        def _(pool):
            split = [0]

            def split_lo(upto):
                while split[0] < min(upto, len(W)):
                    n = split[0]
                    _, rows, w = W[n]
                    pool.wait_ge(*at("weights hi", n))
                    nc.gpsimd.tensor_tensor(pairs[:rows, n % PAIRS, 1, :w], stage[:rows, n % STAGES, :w],
                                            pairs[:rows, n % PAIRS, 0, :w].bitcast(F32), ALU.subtract).then_inc(
                        *up("weights_lo", "weights lo", n))
                    split[0] += 1

            nc.gpsimd.memset(ident[:, :], 0.0).then_inc(*up("pool_const", "zeros"))
            pool.wait_ge(*at("zeros"))
            nc.gpsimd.affine_select(out=ident[:, :], in_=ident[:, :], compare_op=ALU.not_equal, fill=1.0, base=0,
                                    pattern=[[-1, 128]], channel_multiplier=1).then_inc(*up("pool_const", "ident"))
            nc.gpsimd.iota(iota32[:, :], pattern=[[1, CW]], base=0, channel_multiplier=0).then_inc(
                *up("pool_const", "iota32"))
            nc.gpsimd.iota(gid32[:, :], pattern=[[0, 1]], base=0, channel_multiplier=1)
            nc.gpsimd.iota(first32[:, :], pattern=[[P, NT]], base=0, channel_multiplier=0)
            nc.gpsimd.memset(zero16[:, :], 0.0).then_inc(*up("pool_const", "iota"))
            nc.gpsimd.memset(mhalf[:, :], -0.5).then_inc(*up("pool_const", "mhalf"))
            pool.wait_ge(*at("mhalf"))

            def root(n):
                b = n % 2
                pool.wait_ge(*at("norm stats", n))
                nc.gpsimd.tensor_scalar(ve[:, b, :], mv[:, b, 1:2], EPS, 1.0, ALU.add, ALU.mult).then_inc(
                    *up("pool_step", "variance", n))
                pool.wait_ge(*at("variance", n))
                nc.gpsimd.tensor_tensor(rstd[:, b, :], ve[:, b, :], mhalf[:, :], ALU.pow).then_inc(
                    *up("norm_scale", "norm scale", n))

            for s in STEPS:
                kind = s[0]
                split_lo(split_limit(s))
                if kind == "score_rows":
                    l, h, d = s[1:]
                    n = soft_order[s[1:]]
                    pool.wait_ge(*at("score rows", l, h))
                    if n >= 2:
                        pool.wait_ge(*at("masked", n - 2))
                    if h == d == 0:
                        pool.wait_ge(*at("mask", l == 3, NT - 1))
                        if l:
                            for b in range(2):
                                pool.wait_ge(*at("x stored", xr[("output", 0, NT - 1) if l == 1 else
                                                                ("row_part", 1, NT - 1)] - b))
                    nc.gpsimd.tensor_tensor(msk[:, n % 2, :N], asb[:, 1, :N], negm[:, d, :N], ALU.add).then_inc(
                        *up("mask_rows", "mask rows", n))
                elif kind == "softmax" and s[2] < GAT_HEADS[s[1]][0]:
                    l, h, d = s[1:]
                    pool.wait_ge(*at("rden", soft_order[s[1:]]))
                    nc.gpsimd.tensor_scalar(prob[:, d, :N], prob[:, d, :N], rden[:, d:d + 1], 1.0, ALU.mult,
                                            ALU.mult).then_inc(*up("prob_ready", "rows ready", "attention_T", l, h, d))
                elif kind == "output":
                    i = xr[s]
                    pool.wait_ge(*at("b2 in", s[1]))
                    pool.wait_ge(*at("x in", i))
                    nc.gpsimd.tensor_tensor(xl[:, i % 2, :], xl[:, i % 2, :], b2b[:, :], ALU.add).then_inc(
                        *up("x_bias", "x and bias", i))
                elif kind == "embed":
                    nc.gpsimd.iota(rii[:, :], pattern=[[0, 1]], base=0, channel_multiplier=1).then_inc(
                        *up("pool_step", "relation ids"))
                if s in norm_of:
                    root(norm_order[norm_of[s]])

        @block.scalar
        def _(act):
            A = nc.scalar.activation
            split = [0]

            def split_hi(upto):
                while split[0] < min(upto, len(W)):
                    n = split[0]
                    _, rows, w = W[n]
                    act.wait_ge(*at("weights in", n))
                    if n >= PAIRS:
                        act.wait_ge(*at("weights used", n - PAIRS))
                    A(pairs[:rows, n % PAIRS, 0, :w], stage[:rows, n % STAGES, :w], ACT.Copy).then_inc(
                        *up("weights_hi", "weights hi", n))
                    split[0] += 1

            def load_x(i):
                if i >= len(xr_keys):
                    return
                key = xr_keys[i]
                if i >= 2:
                    act.wait_ge(*at("x read", i - 2))
                kept = key[0] != "load_x" and key[:2] != ("output", 0)
                src = (x_scr[2] if key[:2] == ("output", 3) else
                       x_scr[0] if key[0] == "output" else x_scr[1]) if kept else I["x"]
                d = key[-1]
                c0, w = (0, D)
                if key[:2] == ("row_part", 0):
                    w = 384
                if kept:
                    act.wait_ge(*at("x stored", i - 5))
                act.dma_start(xl[:, i % 2, c0:c0 + w], src[P * d:P * d + P, c0:c0 + w]).then_inc(
                    *up(f"x_in{i % 2}", "x in", i, by=16))

            def load_vectors(i):
                s = gat_projects[i]
                if i >= 2:
                    act.wait_ge(*at("vectors read", i - 2))
                w = s[3]
                for v, name in enumerate(("a1", "a2")[s[0] == "project2"] + x for x in ("src", "dst")):
                    src = I[f"{name}_{s[1]}"][s[2] * w:s[2] * w + w]
                    act.dma_start(ab[:, i % 2, v, :w], src.partition_broadcast(P)).then_inc(
                        *up(f"att_vec{i % 2}", "vectors in", i, v, by=16))

            def store_x(i, ap, dst):
                act.dma_start(dst, ap).then_inc(*up(f"x_out{i % 2}", "x stored", i, by=16))

            def norm_rows(n, x_ap):
                b = n % 2
                act.wait_ge(*at("norm shift", n))
                if n:
                    act.wait_ge(*at("filled", "norm_T", *norm_list[n - 1]))
                act.wait_ge(*at("norm scale", n))
                A(hn[:, :], x_ap, ACT.Relu, bias=nb[:, b, :], scale=rstd[:, b, :]).then_inc(
                    *up("norm_rows", "norm rows", *norm_list[n]))

            def row_hi(s, w):
                for g, (s0, ns, pitch) in enumerate(groups(w)):
                    act.wait_ge(*at("filled", "rows", s, g))
                    A(row_dest(s, s0, ns, 0, w), psum_rows(fill_of["rows", s, g], ns, pitch, w), ACT.Copy).then_inc(
                        *up("hi_ready", "rows hi", s, g))

            def transposed_hi(s, dest, name):
                d = s[-1]
                act.wait_ge(*at("filled", *s))
                A(dest[:P, 0:NT, 0, P * d:P * d + P], pitched(fill_of[s]), ACT.Copy).then_inc(
                    *up("att_hi", name + " hi", *s[1:]))

            act.dma_start(b1t[:, :16], I["b1_0"]).then_inc(*up("bias_in", "b1 in", 0, by=16))
            load_x(0)
            for s in STEPS:
                kind = s[0]
                split_hi(split_limit(s))
                if kind == "load_x":
                    i = xr[s]
                    load_x(i + 1)
                    norm_rows(s[1], xl[:, i % 2, :])
                    G.same(("norm rows", 0, s[1]), "x read", i)
                    if s[1] == NT - 1:
                        load_vectors(0)
                        load_vectors(1)
                elif kind == "count":
                    d = s[1]
                    q = fill_of[s]
                    act.wait_ge(*at("filled", *s))
                    if d >= 2:
                        act.wait_ge(*at("counts out", d - 2))
                        act.wait_ge(*at("edge counts", d - 2))
                    for r in range(R):
                        c0 = place[q] * BANK + N * r
                        A(cr[:, d % 2, N * r:N * r + N], ps[:P, c0:c0 + N], ACT.Copy,
                          accum_out=cnt[:, d, r:r + 1]).then_inc(*up("count_rows", "relation", d, r))
                    G.same(("relation", d, R - 1), "relation counts", d)
                    G.same(("relation", d, R - 1), "free", q)
                elif kind == "norm_T":
                    l, d = s[1:]
                    X = XA if l == 2 else XB
                    act.wait_ge(*at("filled", *s))
                    A(X[:, 0:6, 0, P * d:P * d + P].rearrange("p (b k) c -> p b k c", b=2),
                      halves(fill_of[s], 128, 3 * P).rearrange("p b (k c) -> p b k c", k=3), ACT.Copy).then_inc(
                        *up("input_hi", "input hi", l, d))
                elif kind == "rows":
                    s = s[1]
                    kind = s[0]
                    if kind == "relation" and s[1:4] == (1, 0, 0):
                        act.wait_ge(*at("filled", "rows", ("project2", 1, 2, 256), 1))
                        act.wait_ge(*at("counts out", NT - 1))
                        act.wait_ge(*at("counts out", NT - 2))
                        act.dma_start(cr_in[:, :, :],
                                      cr_scr[:, :R * N].rearrange("(t p) n -> p t n", p=P)).then_inc(
                            *up("counts_in", "counts in", by=16))
                    row_hi(s, s[-1])
                    if kind != "relation":
                        i = gat_projects.index(s)
                        if i + 2 < len(gat_projects) and (gat_projects[i + 2][1] < 3 or s[1] == 3):
                            load_vectors(i + 2)
                        if kind == "project2" and s[2] == 0 and s[1] < 3:
                            act.wait_ge(*at("elu relu", agg_order[s[1], GAT_HEADS[s[1]][0] - 1, 3]))
                            bias = I[f"b1_{s[1] + 1}"]
                            act.dma_start(b1t[:, :bias.shape[1]], bias).then_inc(
                                *up("bias_in", "b1 in", s[1] + 1, by=16))
                elif kind == "scores":
                    l, h = s[1:]
                    n = heads_order[s[1:]]
                    act.wait_ge(*at("filled", *s))
                    if n:
                        prev = soft_order[(*list(heads_order)[n - 1], NT - 1)]
                        act.wait_ge(*at("mask rows", prev))
                        act.wait_ge(*at("relu rows", prev))
                    for i, scale in enumerate((1.0, SLOPE)):
                        A(asb[:, i, :N].rearrange("p (j c) -> p j c", j=NT), pitched(fill_of[s]), ACT.Copy,
                          scale=scale).then_inc(*up("score_rows", "scores", n, i))
                    G.same(("scores", n, 1), "score rows", l, h)
                    G.same(("scores", n, 1), "free", fill_of[s])
                    if h == GAT_HEADS[l][0]:
                        act.wait_ge(*at("x2 lo", *agg_key(*[k for k in agg_list if k[0] == l][-1])))
                        act.dma_start(b2b[:, :], I[f"b2_{l}"].partition_broadcast(P)).then_inc(
                            *up("bias2_in", "b2 in", l, by=16))
                        load_x(xr["output", l, 0])
                elif kind == "score_rows":
                    l, h, d = s[1:]
                    n = soft_order[s[1:]]
                    act.wait_ge(*at("score rows", l, h))
                    act.wait_ge(*at("target scores", l, h))
                    if n >= NT:
                        act.wait_ge(*at("filled", "attention_T", *list(soft_order)[n - NT]))
                    A(prob[:, d, :N], asb[:, 0, :N], ACT.Relu, bias=ad8[:, heads_order[l, h] % 2, d:d + 1],
                      scale=1 - SLOPE).then_inc(*up("relu_rows", "relu rows", n))
                elif kind == "softmax":
                    l, h, d = s[1:]
                    n = soft_order[s[1:]]
                    act.wait_ge(*at("masked", n))
                    A(prob[:, d, :N], prob[:, d, :N], ACT.Exp, bias=mx[:, d:d + 1], scale=-1.0).then_inc(
                        *up("exp_ready", "exp", n))
                elif kind == "attention_T":
                    l, h, d = s[1:]
                    if d == 0:
                        if l == 3 and h < 2:
                            act.wait_ge(*at("filled", "rows", ("project", 3, 1, 384), 2))
                        elif l == 3:
                            act.wait_ge(*at("filled", "aggregate", l, h - 2, 0))
                        elif h or l:
                            prev = ("aggregate", l, h - 1, 3) if h else ("output", 0, NT - 1)
                            act.wait_ge(*at("filled", *prev))
                    transposed_hi(s, att_of(l, h), "att")
                    if (l, h, d) == (1, 4, NT - 1):
                        act.dma_start(nti[:, :], I["node_type"].partition_broadcast(R)).then_inc(
                            *up("small_in", "types in", by=16))
                        act.dma_start(emf[:, :], I["emb"]).then_inc(*up("small_in", "emb in", by=16))
                elif kind == "mean_T":
                    transposed_hi(s, MT[:, s[1]], "mean")
                elif kind == "elu":
                    l, h, f = s[1:]
                    n = agg_order[s[1:]]
                    m = 128 if l < 3 else 96
                    q = fill_of[("aggregate", *s[1:])]
                    act.wait_ge(*at("elu min", n))
                    bcol = 4 * h + f if l < 3 else h
                    if n >= 2:
                        act.wait_ge(*at("x2 lo", *agg_key(*agg_list[n - 2])))
                    A(h2(rl[:m, n % 2, :]), halves(q, m), ACT.Relu, bias=b1t[:m, bcol:bcol + 1]).then_inc(
                        *up("elu_relu", "elu relu", n))
                    G.same(("elu relu", n), "free", q)
                    A(mn[:m, :], mn[:m, :], ACT.Exp).then_inc(*up("elu_exp", "elu exp", n))
                elif kind == "elu_high":
                    l, h, f = s[1:]
                    n = agg_order[s[1:]]
                    m = 128 if l < 3 else 96
                    act.wait_ge(*at("elu sum", n))
                    X, xi = x2_place(l, h, f)
                    A(X[:m, xi, 0, :], rl[:m, n % 2, :], ACT.Copy).then_inc(*up("x2_hi", "x2 hi", n))
                elif kind == "output":
                    l, d = s[1:]
                    i = xr[s]
                    if d + 1 < NT:
                        load_x(i + 1)
                    if l < 3:
                        n = norm_order[norm_of[s]]
                        norm_rows(n, xo[:, i % 2, :])
                        store_x(i, xo[:, i % 2, :], x_scr[l, P * d:P * d + P, :])
                    else:
                        act.wait_ge(*at("x added", i))
                        store_x(i, xo[:, i % 2, :], out[P * d:P * d + P, :])
                elif kind == "embed":
                    act.wait_ge(*at("filled", *s))
                    A(h2(XA[:TD, 6, 0, :]), halves(fill_of[s], TD), ACT.Copy).then_inc(*up("embed_hi", "embed hi"))
                elif kind == "combine":
                    _, i, c, f = s
                    act.wait_ge(*at("stage relu", *s[1:]))
                    X, xi = (XB if i == 1 else XA), RGCN_CHUNKS[i][c][0] // 128 + f
                    n = combine_order[s]
                    A(X[:, xi, 0, :], rl[:, n % 2, :], ACT.Copy).then_inc(*up("x2_hi", "stage hi", *s[1:]))
                elif kind == "combine_rows":
                    if s[1] == 0:
                        act.wait_ge(*at("stage lo", 2, 1, 2))
                        act.dma_start(b3b[:, :], I["b3_3"].partition_broadcast(P)).then_inc(
                            *up("bias2_in", "b3 in", by=16))
                        load_x(xr["row_part", 0, 0])
                elif kind == "row_part":
                    c, d = s[1:]
                    i = xr[s]
                    if (c, d) != (1, NT - 1):
                        load_x(i + 1)
                    if c == 0:
                        act.wait_ge(*at("x added", i))
                        store_x(i, xo[:, i % 2, :384], x_scr[1, P * d:P * d + P, :384])
                    else:
                        norm_rows(norm_order[(3, d)], xo[:, i % 2, :])
                        store_x(i, xo[:, i % 2, :], x_scr[2, P * d:P * d + P, :])
                elif kind == "graph_again":
                    act.wait_ge(*at("filled", "rows", ("combine_rows", 1), 2))
                    act.wait_ge(*at("graph out", NT - 2))
                    act.wait_ge(*at("graph out", NT - 1))
                    act.dma_start(Cg[:, :, :], cn_scr.rearrange("(t p) n -> p t n", p=P)).then_inc(
                        *up("graph_in", "graph in", by=16))
                    act.dma_start(b1t[:96, :8], I["b1_3"]).then_inc(*up("bias_in", "b1 in", 3, by=16))
                    load_vectors(len(gat_projects) - 5)
                    load_vectors(len(gat_projects) - 4)
            for b in range(2):
                act.wait_ge(*at("x stored", len(xr_keys) - 1 - b))

        @block.vector
        def _(dve):
            V = nc.vector
            last_tile = None
            junks = [0]

            def stats(n, x_ap):
                b = n % 2
                if n >= 2:
                    dve.wait_ge(*at("norm scale", n - 2))
                for i in range(2):
                    V.bn_stats(bns[:, b, i, :], x_ap[:, 384 * i:384 * i + 384]).then_inc(
                        *up("dve_step", "half stats", n, i))
                dve.wait_ge(*at("half stats", n, 1))
                V.bn_aggr(mv[:, b, :], bns[:, b, :, :].rearrange("p a c -> p (a c)")).then_inc(
                    *up("norm_stats", "norm stats", n))

            def shift(n):
                b = n % 2
                dve.wait_ge(*at("norm scale", n))
                if n >= 2:
                    dve.wait_ge(*at("norm rows", *norm_list[n - 2]))
                V.scalar_tensor_tensor(out=nb[:, b, :], in0=mv[:, b, 0:1], scalar=-1.0, in1=rstd[:, b, :],
                                       op0=ALU.mult, op1=ALU.mult).then_inc(*up("norm_stats", "norm shift", n))

            def minus_hi(out_ap, whole, hi_ap):
                return V.tensor_tensor(out_ap, whole, hi_ap.bitcast(F32), ALU.subtract)

            def finish_tile():
                nonlocal last_tile
                if last_tile is not None:
                    X, xi, m, b, hi, lo = last_tile
                    dve.wait_ge(*at(*hi))
                    minus_hi(X[:m, xi, 1, :], rl[:m, b, :], X[:m, xi, 0, :]).then_inc(*up("x2_lo", *lo))
                last_tile = None

            def transposed_lo(s, dest, name):
                d = s[-1]
                dve.wait_ge(*at(name + " hi", *s[1:]))
                c = slice(P * d, P * d + P)
                minus_hi(dest[:P, 0:NT, 1, c], pitched(fill_of[s]), dest[:P, 0:NT, 0, c]).then_inc(
                    *up("att_lo", name + " lo", *s[1:]))
                G.same((name + " lo", *s[1:]), "free", fill_of[s])

            def sum_relations(d):
                b = d % 2
                dve.wait_ge(*at("relation counts", d))
                if d >= 2:
                    dve.wait_ge(*at("graph out", d - 2))
                T = V.tensor_tensor
                T(cn[:, b, :N], cr[:, b, :N], cr[:, b, N:2 * N], ALU.add).then_inc(
                    *up("edge_sums", "two relations", d))
                dve.wait_ge(*at("two relations", d))
                T(cn[:, b, :N], cn[:, b, :N], cr[:, b, 2 * N:3 * N], ALU.add).then_inc(
                    *up("edge_sums", "edge counts", d))
                dve.wait_ge(*at("edge counts", d))
                V.tensor_copy(Cg[:, d, :N], cn[:, b, :N]).then_inc(*up("edge_sums", "graph copy", d))
                dve.wait_ge(*at("graph copy", d))
                dve.wait_ge(*at("ident"))
                T(Cg[:, d, P * d:P * d + P], cn[:, b, P * d:P * d + P], ident[:P, :P], ALU.add).then_inc(
                    *up("edge_sums", "graph whole", d))

            def mask(again):
                for d in range(NT):
                    dve.wait_ge(*at("graph whole", d))
                    V.tensor_scalar(negm[:, d, :N], Cg[:, d, :N], 0.0, ABSENT, ALU.is_equal, ALU.mult).then_inc(
                        *up("graph", "mask", again, d))

            V.memset(cn[:, :, N:NP], 0).then_inc(*up("graph", "cn pad"))
            V.memset(AT[:, :, :, N:NP].bitcast(F32), 0.0).then_inc(*up("graph", "AT pad"))
            for s in STEPS:
                kind = s[0]
                if kind not in ("score_rows", "softmax", "attention_T", "aggregate", "elu", "elu_high", "combine"):
                    finish_tile()
                if kind == "load_x":
                    i = xr[s]
                    dve.wait_ge(*at("x in", i))
                    stats(s[1], xl[:, i % 2, :])
                    shift(s[1])
                elif kind == "norm_T":
                    l, d = s[1:]
                    X = XA if l == 2 else XB
                    dve.wait_ge(*at("input hi", l, d))
                    c = slice(P * d, P * d + P)
                    minus_hi(X[:, 0:6, 1, c].rearrange("p (b k) c -> p b k c", b=2),
                             halves(fill_of[s], 128, 3 * P).rearrange("p b (k c) -> p b k c", k=3),
                             X[:, 0:6, 0, c].rearrange("p (b k) c -> p b k c", b=2)).then_inc(
                        *up("input_lo", "input lo", l, d))
                    G.same(("input lo", l, d), "free", fill_of[s])
                elif kind == "bounds":
                    n = iter(range(30))

                    def step(instruction):
                        key = ("bounds step", next(n))
                        instruction.then_inc(*up("bounds_step", *key))
                        dve.wait_ge(*at(*key))

                    dve.wait_ge(*at("iota"))
                    V.tensor_copy(iota16[:, :], iota32[:, :]).then_inc(*up("count_step", "iota16"))
                    V.tensor_copy(gid[:, 0:1], gid32[:, :])
                    step(V.tensor_copy(first[:, 0, :], first32[:, :]))
                    V.tensor_scalar(gid[:, 1:2], gid[:, 0:1], 1.0, None, ALU.add)
                    V.tensor_scalar(first[:, 1, :], first[:, 0, :], float(P), None, ALU.add)
                    dve.wait_ge(*at("edges in"))
                    V.tensor_reduce(gspan[:, 0:1], gdst32[:, :], AX.X, ALU.min)
                    step(V.tensor_reduce(gspan[:, 1:2], gdst32[:, :], AX.X, ALU.max))
                    step(V.tensor_scalar(touch[:, 0, :], first[:, 0, :], gspan[:, 1:2], None, ALU.is_le))
                    step(V.scalar_tensor_tensor(out=touch[:, 0, :], in0=first[:, 1, :], scalar=gspan[:, 0:1],
                                                in1=touch[:, 0, :], op0=ALU.is_gt, op1=ALU.mult))
                    V.tensor_scalar(touch[:, 2, :], touch[:, 0, :], gid[:, 1:2], None, ALU.mult)
                    step(V.tensor_scalar(touch[:, 1, :], touch[:, 0, :], gid[:, 0:1], None, ALU.mult))
                    V.scalar_tensor_tensor(out=touch[:, 1, :], in0=touch[:, 0, :], scalar=float(NG),
                                           in1=touch[:, 1, :], op0=ALU.mult, op1=ALU.subtract).then_inc(
                        *up("count_step", "touched"))
                    V.tensor_copy(edgef[:, :, :], edge32[:, :, :]).then_inc(*up("count_step", "edges float"))
                    dve.wait_ge(*at("edges float"))
                    V.scalar_tensor_tensor(out=edgef[:, 0, :], in0=edgef[:, 2, :], scalar=float(N),
                                           in1=edgef[:, 0, :], op0=ALU.mult, op1=ALU.add).then_inc(
                        *up("count_step", "edge keys"))
                    dve.wait_ge(*at("filled", *s))
                    step(V.tensor_reduce(reach[:, :, :],
                                         slot(fill_of[s])[:1, :].rearrange("p (c n) -> p c n", c=2)[
                                             :, :, :NT * NG].rearrange("p c (d g) -> p c d g", d=NT),
                                         AX.X, ALU.max))
                    step(V.tensor_scalar(span[:, 0, :NT], reach[:, 0, :], -1.0, float(NG), ALU.mult, ALU.add))
                    step(V.tensor_scalar(span[:, 0, :NT], span[:, 0, :NT], float(NG - 1), None, ALU.min))
                    step(V.scalar_tensor_tensor(out=span[:, 1, :NT], in0=span[:, 0, :NT], scalar=1.0,
                                                in1=reach[:, 1, :], op0=ALU.add, op1=ALU.max))
                    V.memset(span[:, 2, 0:1], 0.0)
                    step(V.tensor_tensor(span[:, 1, :NT], span[:, 1, :NT], span[:, 0, :NT], ALU.subtract))
                    for d in range(NT):
                        step(V.tensor_tensor(span[:, 2, d + 1:d + 2], span[:, 2, d:d + 1], span[:, 1, d:d + 1],
                                             ALU.add))
                    V.tensor_copy(bounds[:, 0, :], span[:, 2, :])
                    step(V.tensor_tensor(span[:, 3, :NT], span[:, 0, :NT], span[:, 2, :NT], ALU.subtract))
                    V.tensor_copy(bounds[:, 1, :NT], span[:, 3, :NT]).then_inc(*up("bounds", "bounds"))
                    G.same(("bounds",), "free", fill_of[s])
                elif kind == "count":
                    d = s[1]
                    if d == 0:
                        dve.wait_ge(*at("bounds"))
                        passes = [dve.value_load(bounds[0:1, 0, i:i + 1], min_val=0, max_val=NT * NG)
                                  for i in range(NT + 1)]
                        shift_of = [dve.value_load(bounds[0:1, 1, i:i + 1], min_val=-NT * NG, max_val=NG - 1)
                                    for i in range(NT)]
                        dve.wait_ge(*at("edge keys"))
                    with dve.Fori(passes[d], passes[d + 1]) as g:
                        group = nc.s_assert_within(g + shift_of[d], 0, NG - 1, skip_runtime_bounds_check_because=
                                                   "a pass's group lies between its tile's first and last")
                        for i in range(EG):
                            dve.wait_ge(sems[f"onehot_used{i}"], g + 1)
                            V.tensor_scalar(srcs[:, i, :], iota16[:, :], edgef[:, 0, bass.ds(group * EG + i, 1)],
                                            None, ALU.is_equal)
                            V.tensor_scalar(dsts[:, i, :P], iota16[:, P * d:P * d + P],
                                            edgef[:, 1, bass.ds(group * EG + i, 1)], None,
                                            ALU.is_equal).then_inc(sems[f"onehot{i}"], 1)
                    if d:
                        sum_relations(d - 1)
                    if d == NT - 1:
                        sum_relations(d)
                        mask(False)
                        V.tensor_scalar(cnt1[:, :, :], cnt[:, :, :], 1.0, None, ALU.max).then_inc(
                            *up("count_step", "degree floor"))
                        V.tensor_scalar(got[:, :, :], cnt[:, :, :], 1.0, None, ALU.min)
                        dve.wait_ge(*at("degree floor"))
                        V.reciprocal(cnt1[:, :, :], cnt1[:, :, :]).then_inc(*up("count_step", "degree inverse"))
                        dve.wait_ge(*at("degree inverse"))
                        V.tensor_tensor(inv[:, :, :], cnt1[:, :, :], got[:, :, :], ALU.mult).then_inc(
                            *up("count_step", "inverse degrees"))
                elif kind == "rows":
                    s = s[1]
                    kind = s[0]
                    w = s[-1]
                    if kind == "relation" and s[1:3] == (1, 0):
                        r = s[3]
                        if r == 0:
                            V.memset(MT[:, :, :, :, N:NP].bitcast(F32), 0.0).then_inc(*up("mean_step", "MT pad"))
                            dve.wait_ge(*at("counts in"))
                        for d in range(NT):
                            if r:
                                dve.wait_ge(*at("filled", "mean_T", r - 1, d))
                            V.tensor_scalar(mean[:, d, :], cr_in[:, d, N * r:N * r + N], inv[:, d, r:r + 1], None,
                                            ALU.mult).then_inc(*up("mean_step", "rows ready", "mean_T", r, d))
                    if kind != "relation":
                        i = gat_projects.index(s)
                        dve.wait_ge(*at("vectors in", i, 1))
                    for g, (s0, ns, pitch) in enumerate(groups(w)):
                        q = fill_of["rows", s, g]
                        dve.wait_ge(*at("rows hi", s, g))
                        last = minus_hi(row_dest(s, s0, ns, 1, w), psum_rows(q, ns, pitch, w),
                                        row_dest(s, s0, ns, 0, w))
                        last.then_inc(*up("lo_ready", "rows lo", s, g))
                        if kind == "relation":
                            G.same(("rows lo", s, g), "free", q)
                            continue
                        for t in range(ns):
                            for part, c0, pw in pieces(s):
                                for v in range(2):
                                    j = junks[0]
                                    junks[0] += 1
                                    if j >= 2:
                                        dve.wait_ge(*at("dot", j - 2))
                                    V.tensor_tensor_reduce(
                                        out=junk[:, j % 2, :pw],
                                        in0=slot(q)[:P, t * pitch + c0:t * pitch + c0 + pw],
                                        in1=ab[:, i % 2, v, c0:c0 + pw], scale=1.0, scalar=0.0, op0=ALU.mult,
                                        op1=ALU.add, accum_out=asp[:, v, part, s0 + t:s0 + t + 1]).then_inc(
                                        *up("rows_used", "dot", j))
                        G.same(("dot", junks[0] - 1), "free", q)
                    if kind != "relation":
                        G.same(("dot", junks[0] - 1), "vectors read", i)
                        G.same(("dot", junks[0] - 1), "dots", s)
                elif kind == "scores":
                    l, h = s[1:]
                    n = heads_order[s[1:]]
                    hb = n % 2
                    heads = GAT_HEADS[l][0]
                    dve.wait_ge(*at("dots", last_piece(s)))
                    if n >= 2:
                        dve.wait_ge(*at("filled", "scores", *list(heads_order)[n - 2]))
                    if h == heads:
                        V.tensor_tensor(asq[:, :, :], asp[:, :, 0, :], asp[:, :, 1, :], ALU.add).then_inc(
                            *up("scores_step", "two parts", l))
                        dve.wait_ge(*at("two parts", l))
                        V.tensor_tensor(asad[:, hb, :, :], asq[:, :, :], asp[:, :, 2, :], ALU.add).then_inc(
                            *up("scores_step", "scores col", l, h))
                    elif l < 3:
                        V.tensor_tensor(asad[:, hb, :, :], asp[:, :, 0, :], asp[:, :, 1, :], ALU.add).then_inc(
                            *up("scores_step", "scores col", l, h))
                    else:
                        V.tensor_copy(asad[:, hb, :, :], asp[:, :, h, :]).then_inc(
                            *up("scores_step", "scores col", l, h))
                    dve.wait_ge(*at("scores col", l, h))
                    if n >= 2:
                        prev = list(heads_order)[n - 2]
                        dve.wait_ge(*at("relu rows", soft_order[(*prev, NT - 1)]))
                    V.tensor_scalar(ad8[:, hb, :], asad[:, hb, 1, :], 1 - SLOPE, None, ALU.mult).then_inc(
                        *up("scores_step", "target scores", l, h))
                elif kind == "score_rows":
                    l, h, d = s[1:]
                    n = soft_order[s[1:]]
                    dve.wait_ge(*at("mask rows", n))
                    dve.wait_ge(*at("relu rows", n))
                    V.tensor_tensor_reduce(out=prob[:, d, :N], in0=prob[:, d, :N], in1=msk[:, n % 2, :N],
                                           scale=-1.0, scalar=-FLOOR, op0=ALU.add, op1=ALU.min,
                                           accum_out=mx[:, d:d + 1]).then_inc(*up("masked", "masked", n))
                elif kind == "softmax":
                    l, h, d = s[1:]
                    n = soft_order[s[1:]]
                    dve.wait_ge(*at("exp", n))
                    V.tensor_tensor_reduce(out=prob[:, d, :N], in0=prob[:, d, :N], in1=Cg[:, d, :N], scale=1.0,
                                           scalar=0.0, op0=ALU.mult, op1=ALU.add,
                                           accum_out=den[:, d:d + 1]).then_inc(*up("prob_step", "prob mass", n))
                    if h == GAT_HEADS[l][0]:
                        G.same(("prob mass", n), "rows ready", "attention_T", l, h, d)
                    dve.wait_ge(*at("prob mass", n))
                    V.tensor_scalar(dene[:, d:d + 1], den[:, d:d + 1], 1e-16, None, ALU.add).then_inc(
                        *up("prob_step", "denominator", n))
                    dve.wait_ge(*at("denominator", n))
                    V.reciprocal(rden[:, d:d + 1], dene[:, d:d + 1]).then_inc(*up("prob_step", "rden", n))
                elif kind == "attention_T":
                    transposed_lo(s, att_of(*s[1:3]), "att")
                elif kind == "mean_T":
                    transposed_lo(s, MT[:, s[1]], "mean")
                elif kind == "elu":
                    l, h, f = s[1:]
                    n = agg_order[s[1:]]
                    m = 128 if l < 3 else 96
                    q = fill_of[("aggregate", *s[1:])]
                    bcol = 4 * h + f if l < 3 else h
                    dve.wait_ge(*at("b1 in", l))
                    dve.wait_ge(*at("filled", "aggregate", *s[1:]))
                    if n:
                        dve.wait_ge(*at("elu sum", n - 1))
                    if (h, f) == (0, 0) and l:
                        for b in range(2):
                            dve.wait_ge(*at("x stored", xr[("output", 0, NT - 1) if l == 1 else
                                                           ("row_part", 1, NT - 1)] - b))
                    V.tensor_scalar(h2(mn[:m, :]), halves(q, m), b1t[:m, bcol:bcol + 1], 0.0, ALU.add,
                                    ALU.min).then_inc(*up("elu_step", "elu min", n))
                elif kind == "elu_sum":
                    l, h, f = s[1:]
                    n = agg_order[s[1:]]
                    m = 128 if l < 3 else 96
                    dve.wait_ge(*at("elu exp", n))
                    V.scalar_tensor_tensor(out=rl[:m, n % 2, :], in0=mn[:m, :], scalar=-1.0, in1=rl[:m, n % 2, :],
                                           op0=ALU.add, op1=ALU.add).then_inc(*up("elu_step", "elu sum", n))
                    last_tile = (*x2_place(l, h, f), m, n % 2, ("x2 hi", n), ("x2 lo", *agg_key(l, h, f)))
                elif kind == "output":
                    l, d = s[1:]
                    i = xr[s]
                    q = fill_of[s]
                    dve.wait_ge(*at("x and bias", i))
                    dve.wait_ge(*at("filled", *s))
                    if d >= 2:
                        dve.wait_ge(*at("x stored", i - 2))
                        if l < 3:
                            dve.wait_ge(*at("norm rows", l + 1, d - 2))
                    if d == 0:
                        dve.wait_ge(*at("masked", soft_order[l, GAT_HEADS[l][0], NT - 1]))
                    V.scalar_tensor_tensor(out=xo[:, i % 2, :].rearrange("p (c n) -> p c n", c=2),
                                           in0=halves(q, P, 384), scalar=rden[:, d:d + 1],
                                           in1=xl[:, i % 2, :].rearrange("p (c n) -> p c n", c=2), op0=ALU.mult,
                                           op1=ALU.add).then_inc(*up("x_added", "x added", i))
                    G.same(("x added", i), "free", q)
                    G.same(("x added", i), "x read", i)
                    if l < 3:
                        dve.wait_ge(*at("x added", i))
                        n = norm_order[norm_of[s]]
                        stats(n, xo[:, i % 2, :])
                        shift(n)
                elif kind == "embed":
                    dve.wait_ge(*at("emb in"))
                    V.tensor_copy(ntf[:, :], nti[:, :]).then_inc(*up("embed", "types float"))
                    V.memset(nth[:, N:NP].bitcast(F32), 0.0).then_inc(*up("embed", "types pad"))
                    dve.wait_ge(*at("relation ids"))
                    V.tensor_copy(rid[:, :], rii[:, :]).then_inc(*up("embed", "ids float"))
                    V.tensor_copy(emh[:, 0, :], emf[:, :]).then_inc(*up("embed", "emb hi"))
                    dve.wait_ge(*at("emb hi"))
                    minus_hi(emh[:, 1, :], emf[:, :], emh[:, 0, :])
                    V.tensor_scalar(nth[:, :N], ntf[:, :], rid[:, :], None, ALU.is_equal).then_inc(
                        *up("embed", "embed operands"))
                    V.memset(XA[:, 0:6, :, N:NP].bitcast(F32), 0.0).then_inc(*up("embed", "XA pad"))
                    dve.wait_ge(*at("embed hi"))
                    minus_hi(h2(XA[:TD, 6, 1, :]), halves(fill_of[s], TD), h2(XA[:TD, 6, 0, :])).then_inc(
                        *up("embed", "embed lo"))
                    G.same(("embed lo",), "free", fill_of[s])
                elif kind == "combine":
                    _, i, c, f = s
                    n = combine_order[s]
                    q = fill_of[s]
                    col = RGCN_CHUNKS[i][c][0] // 128 + f
                    bcol = col + (7 if i == 2 else 0)
                    dve.wait_ge(*at("b1 in", 2))
                    dve.wait_ge(*at("filled", *s))
                    if n < 2:
                        dve.wait_ge(*at("x stored", xr["output", 1, NT - 1 - n]))
                    else:
                        dve.wait_ge(*at("stage lo", *combine_list[n - 2][1:]))
                    V.tensor_scalar(h2(rl[:, n % 2, :]), halves(q, 128), b1t[:, bcol:bcol + 1], 0.0, ALU.add,
                                    ALU.max).then_inc(*up("elu_step", "stage relu", *s[1:]))
                    G.same(("stage relu", *s[1:]), "free", q)
                    finish_tile()
                    last_tile = (XB if i == 1 else XA, col, 128, n % 2, ("stage hi", *s[1:]), ("stage lo", *s[1:]))
                elif kind == "row_part":
                    c, d = s[1:]
                    i = xr[s]
                    g, t = d // 2, d % 2
                    q = fill_of["rows", ("combine_rows", c), g]
                    c0 = 384 * c
                    dve.wait_ge(*at("b3 in"))
                    dve.wait_ge(*at("filled", "rows", ("combine_rows", c), g))
                    if d >= 2 or c:
                        dve.wait_ge(*at("x stored", i - 2))
                    if c and d >= 2:
                        dve.wait_ge(*at("norm rows", 3, d - 2))
                    xh = xo[:, i % 2, c0:c0 + 384]
                    V.tensor_tensor(xh, slot(q)[:P, t * BANK:t * BANK + 384], b3b[:, c0:c0 + 384],
                                    ALU.add).then_inc(*up("dve_step", "part and bias", c, d))
                    if t == 1 or d == NT - 1:
                        G.same(("part and bias", c, d), "free", q)
                    dve.wait_ge(*at("part and bias", c, d))
                    dve.wait_ge(*at("x in", i))
                    last = V.scalar_tensor_tensor(out=xh, in0=xh, scalar=0.0, in1=xl[:, i % 2, c0:c0 + 384],
                                                  op0=ALU.max, op1=ALU.add)
                    if c:
                        last = V.tensor_copy(xo[:, i % 2, :384], xl[:, i % 2, :384])
                    last.then_inc(*up("x_added", "x added", i))
                    G.same(("x added", i), "x read", i)
                    if c:
                        dve.wait_ge(*at("x added", i))
                        n = norm_order[(3, d)]
                        stats(n, xo[:, i % 2, :])
                        shift(n)
                elif kind == "graph_again":
                    dve.wait_ge(*at("filled", "rows", ("combine_rows", 1), 2))
                    V.memset(AT[:, :, :, N:NP].bitcast(F32), 0.0).then_inc(*up("graph", "AT pad again"))
                    dve.wait_ge(*at("graph in"))
                    mask(True)
    return G.seen


def describe(nc, inputs):
    arrays = {}
    for name, a in inputs.items():
        arrays[name] = nc.dram_tensor(f"in_{name}", a.shape, mybir.dt.from_np(a.dtype), kind="ExternalInput").ap()
    return arrays, nc.dram_tensor("out_x", (N, D), F32, kind="ExternalOutput").ap()


def laid_out(k):
    c = np.ascontiguousarray
    edges = np.stack([k["src"], k["dst"], k["edge_type_3"]]).reshape(3, ET, P)
    out = {"x": c(k["x"]), "edges": c(edges.transpose(2, 0, 1)), "dst": c(k["dst"].reshape(NG, EG * P)), "node_type": c(k["node_type_3"]),
           "emb": c(k["L2_gnn_node_emb"])}
    names = {0: ("a1_src", "a1_dst", "a2_src", "a2_dst"), 1: ("att_src1", "att_dst1", "att_src2", "att_dst2"),
             3: ("a_src1", "a_dst1", "a_src2", "a_dst2")}
    for l, (s1, d1, s2, d2) in names.items():
        g = f"L{l}_gnn_"
        rows = 128 if l < 3 else 96
        out[f"W1_{l}"], out[f"W2_{l}"] = c(k[g + "W1"]), c(k[g + "W2"])
        out[f"a1src_{l}"], out[f"a1dst_{l}"] = c(k[g + s1].reshape(-1)), c(k[g + d1].reshape(-1))
        out[f"a2src_{l}"], out[f"a2dst_{l}"] = c(k[g + s2].reshape(-1)), c(k[g + d2].reshape(-1))
        out[f"b1_{l}"] = c(k[g + "b1"].reshape(-1, rows).T)
        out[f"b2_{l}"] = c(k[g + "b2"])
    for i in (1, 2, 3):
        out[f"rel_{i}"], out[f"root_{i}"] = c(k[f"L2_gnn_w_rel{i}"]), c(k[f"L2_gnn_w_root{i}"])
    out["b1_2"] = c(np.concatenate([k["L2_gnn_b1"].reshape(-1, 128).T, k["L2_gnn_b2"].reshape(-1, 128).T], axis=1))
    out["b3_3"] = c(k["L2_gnn_b3"])
    return out


def kernel(**inputs):
    import concourse.bacc as bacc
    from concourse.bass_utils import run_bass_kernel_spmd

    arrays = laid_out({n: np.asarray(a) for n, a in inputs.items()})
    known = {}
    for _ in range(2):
        nc = bacc.Bacc("TRN2", target_bir_lowering=False, num_devices=1, dynamic_dma_scratch_size=SCRATCH)
        I, out = describe(nc, arrays)
        known = build(nc, I, out, known)
    r = run_bass_kernel_spmd(nc, [{f"in_{n}": a for n, a in arrays.items()}], core_ids=[0])
    return r.results[0]["out_x"]
```

```python
import numpy as np
import concourse.bass as bass
from concourse import mybir
from contextlib import ExitStack

F32, F32R, F16, BF16 = mybir.dt.float32, mybir.dt.float32r, mybir.dt.float16, mybir.dt.bfloat16
U16, I32 = mybir.dt.uint16, mybir.dt.int32
ALU, ACT, AX = mybir.AluOpType, mybir.ActivationFunctionType, mybir.AxisListType

N, D, E, R, TD = 625, 768, 10000, 3, 128
NT = 5
P = N // NT
NP = 628
HC = NP // 2
ET = E // P
EG = 4
NG = ET // EG
BANK = 512
BANKS = 8
STAGED, SPLIT = 3 * 384, 5 * 384
LOADS = 4
WMAX = 384
SLOPE, EPS, ABSENT, FLOOR = 0.2, 1e-5, -1e37, -1e30
PASSES = ((0, 0), (0, 1), (1, 0))
GAT_HEADS = {0: (4, 512), 1: (4, 512), 3: (8, 96)}
RGCN_IN = {1: 7, 2: 7, 3: 6}
RGCN_CHUNKS = {1: ((0, 384), (384, 256), (640, 256)), 2: ((0, 384), (384, 384)), 3: ((0, 384), (384, 384))}
SCRATCH = 512


class Signals:

    def __init__(self, sems, known):
        self.sems, self.known, self.counts, self.seen = sems, known, dict.fromkeys(sems, 0), {}

    def up(self, name, *key, by=1):
        self.counts[name] += by
        self.seen[key] = (name, self.counts[name])
        return self.sems[name], by

    def same(self, key, *other):
        self.seen[other] = self.seen[key]

    def at(self, *key):
        name, value = self.known.get(key, (next(iter(self.sems)), 1))
        return self.sems[name], value


def groups(w):
    return ((0, 4, 256), (4, 1, 256)) if w <= 256 else ((0, 2, BANK), (2, 2, BANK), (4, 1, BANK))


def tick(l, h, t):
    if t == 0:
        yield ("mask_rows", l, h, 0)
    if 0 <= t < NT:
        yield ("score_rows", l, h, t)
    if t + 1 < NT:
        yield ("mask_rows", l, h, t + 1)
    if 1 <= t <= NT:
        yield ("softmax", l, h, t - 1)
    if 3 <= t < NT + 3:
        yield ("attention_T", l, h, t - 3)


def gat_steps(l):
    heads, dh = GAT_HEADS[l]
    if l == 3:
        yield ("project", l, 0, 384)
        yield ("rows", ("project", l, 0, 384))
        yield from (("spread", l, 0), ("scores", l, 0), ("mask_rows", l, 0, 0))
        yield ("project", l, 1, 384)
        yield ("split", ("project", l, 1, 384), 1)
        for t in range(heads * NT + 3):
            h, d = t // NT, t % NT
            if h < heads:
                yield ("score_rows", l, h, d)
                if d == 2 and h + 1 < heads:
                    yield ("spread", l, h + 1)
                if d == NT - 1 and h + 1 < heads:
                    yield ("scores", l, h + 1)
            if t + 1 < heads * NT:
                yield ("mask_rows", l, (t + 1) // NT, (t + 1) % NT)
            if h > 1 and d == 2:
                yield ("elu_sum", l, h - 2, 0)
            if 0 < t <= heads * NT:
                yield ("softmax", l, (t - 1) // NT, (t - 1) % NT)
            if h > 1 and d == 2:
                yield ("elu_high", l, h - 2, 0)
            if t == 2:
                yield ("rows", ("project", l, 1, 384))
            if t >= 3:
                yield ("attention_T", l, (t - 3) // NT, (t - 3) % NT)
            if h and d == 4:
                yield ("aggregate", l, h - 1, 0)
            if h > 1 and d == 0:
                yield ("aggregate_rest", l, h - 2, 0)
            if h > 1 and d == 1:
                yield ("elu", l, h - 2, 0)
        h = heads - 1
        yield from (("aggregate", l, h, 0), ("aggregate_rest", l, h, 0), ("elu", l, h, 0), ("elu_sum", l, h, 0), ("elu_high", l, h, 0))
    else:
        for h in range(heads + 1):
            new = [("project", l, 2 * h + i, 256) for i in range(2)]
            old = h - 1
            if h < heads and h != 1:
                yield new[0]
            if h > 1:
                yield from (("elu_sum", l, h - 2, 3), ("elu_high", l, h - 2, 3))
            if 1 < h < heads:
                yield ("split", new[0], 1)
            if h:
                yield ("softmax", l, old, 4)
            if h < heads and h != 1:
                yield ("rows", new[0])
            if h:
                for d in range(3, NT):
                    yield ("attention_T", l, old, d)
            if h < heads:
                yield new[1]
                if h == 0:
                    yield ("project", l, 2, 256)
                yield ("rows", new[1])
            for f in range(4):
                if h and f != 1:
                    yield ("aggregate", l, old, f)
                if h and f == 0:
                    yield ("aggregate", l, old, 1)
                if h < heads:
                    if f == 0:
                        yield from (("spread", l, h), ("scores", l, h))
                        if h:
                            yield ("elu", l, old, 0)
                        yield ("mask_rows", l, h, 0)
                    else:
                        yield from (("score_rows", l, h, f), ("mask_rows", l, h, f + 1))
                if h and f:
                    yield ("elu_sum", l, old, f - 1)
                if h < heads and f:
                    yield ("softmax", l, h, f - 1)
                if h and f:
                    yield ("elu_high", l, old, f - 1)
                if h and (f or h == heads):
                    yield ("elu", l, old, f)
                if h == 0 and f == 3:
                    yield ("rows", ("project", l, 2, 256))
                if 0 < h < heads - 1 and f == 1:
                    yield ("split", ("project", l, 2 * h + 2, 256), 0)
                if h < heads and f == 0:
                    yield from (("score_rows", l, h, 0), ("mask_rows", l, h, 1))
            if h < heads:
                yield ("attention_T", l, h, 0)
                yield ("attention_T", l, h, 1)
                yield from (("score_rows", l, h, 4), ("softmax", l, h, 3), ("attention_T", l, h, 2))
        yield from (("elu_sum", l, heads - 1, 3), ("elu_high", l, heads - 1, 3))
    h = heads
    for c in range(3):
        yield ("project2", l, c, 256)
        yield ("rows", ("project2", l, c, 256))
    yield from (("spread", l, h), ("scores", l, h))
    for t in range(NT + 3):
        yield from tick(l, h, t)
        if l == 1 and t == 5:
            yield ("split", ("relation", 1, 0, 0, 384), 0)
        if t >= 4:
            yield ("output", l, t - 4)
            if t > 4 and l != 3:
                yield ("norm_T", l + 1, t - 5)
    yield ("output", l, NT - 1)
    if l != 3:
        yield ("norm_T", l + 1, NT - 2)
        yield ("norm_T", l + 1, NT - 1)


def rgcn_steps():
    yield ("embed",)
    for i in (1, 2, 3):
        for c, (f0, w) in enumerate(RGCN_CHUNKS[i]):
            for r in range(R):
                yield ("relation", i, c, r, w)
                yield ("rows", ("relation", i, c, r, w))
                if i == 1 and c == 0:
                    for d in range(NT):
                        yield ("mean_T", r, d)
            if i < 3:
                for f in range(w // 128):
                    yield ("combine", i, c, f)
            else:
                yield ("combine_rows", c)
                for d in range(NT):
                    yield ("combine_tile", c, d)
                    if c and d in (1, 2):
                        yield ("norm_T", 3, d - 1)
                    yield ("row_part", c, d)
                    if c and d > 2:
                        yield ("norm_T", 3, d - 1)
    yield ("norm_T", 3, NT - 1)


def steps():
    yield ("bounds",)
    for d in range(NT + 2):
        if d < NT:
            yield ("load_x", d)
        if d > 1:
            yield ("norm_T", 0, d - 2)
    for d in range(NT):
        yield ("count", d)
    yield from gat_steps(0)
    yield from gat_steps(1)
    yield from rgcn_steps()
    yield ("graph_again",)
    yield from gat_steps(3)


def weight_tiles(I):
    out = {}
    for l, (heads, dh) in GAT_HEADS.items():
        w1, w2 = I[f"W1_{l}"], I[f"W2_{l}"]
        rows = 128 if l < 3 else 96
        for s in gat_steps(l):
            if s[0] == "project":
                c, w = s[2:]
                out[s] = [(w1[128 * k:128 * k + 128, c * w:c * w + w], 128, w) for k in range(6)]
            if s[0] == "project2":
                c, w = s[2:]
                out[s] = [(w2[rows * k:rows * k + rows, c * w:c * w + w], rows, w)
                          for k in range(heads * dh // rows)]
    for s in rgcn_steps():
        if s[0] == "relation":
            _, i, c, r, w = s
            f0 = RGCN_CHUNKS[i][c][0]
            out[s] = [(I[f"rel_{i}"][r, 128 * k:128 * k + 128, f0:f0 + w], 128, w) for k in range(RGCN_IN[i])]
        if s[0] == "combine":
            _, i, c, f = s
            f0 = RGCN_CHUNKS[i][c][0] + 128 * f
            out[s] = [(I[f"root_{i}"][128 * k:128 * k + 128, f0:f0 + 128], 128, 128) for k in range(RGCN_IN[i])]
        if s[0] == "combine_rows":
            f0, w = RGCN_CHUNKS[3][s[1]]
            out[s] = [(I["root_3"][128 * k:128 * k + 128, f0:f0 + w], 128, w) for k in range(RGCN_IN[3])]
    return out


def build(nc, I, out, known):
    ctx = ExitStack()
    with ctx:
        STEPS = list(steps())
        tiles_of = weight_tiles(I)
        first_tile, W = {}, []
        for s in STEPS:
            first_tile[s] = len(W)
            W += tiles_of.get(s, [])
        wend = {s: first_tile[s] + len(tiles_of.get(s, [])) for s in STEPS}

        def ring(columns):
            wide = next(first_tile[s] for s in STEPS if s[0] == "relation")
            at_col, before = [], []
            for n in range(len(W)):
                size = 256 if n < wide else WMAX
                i = (n if n < wide else n - wide) % (columns // size)
                at_col.append(i * size)
                over = [m for m in range(max(0, n - 16), n)
                        if at_col[m] < i * size + size and i * size < at_col[m] + (256 if m < wide else WMAX)]
                before.append(over[-1] if over else None)
            return at_col, before

        stage_col, stage_before = ring(STAGED)
        pair_col, pair_before = ring(SPLIT)

        def staged(n):
            _, rows, w = W[n]
            return stage[:rows, stage_col[n]:stage_col[n] + w]

        def pair(n, part, w=None):
            _, rows, width = W[n]
            return pairs[:rows, part, pair_col[n]:pair_col[n] + (w or width)]

        def split_limit(s):
            if s[0] == "split":
                used = first_tile[s[1]] + s[2]
            elif s[0] in ("combine", "combine_rows"):
                used = wend[s]
            elif s[0] == "rows":
                used = wend[s[1]]
                if s[1] == ("project2", 1, 2, 256):
                    return used
            else:
                return 0
            return next((n for n in range(used, len(W)) if (pair_before[n] or 0) >= used), len(W))

        names = ["psum_filled", "psum_free_dve", "psum_free_act", "weights_used", "weights_hi",
                 "weights_lo", "hi_ready", "lo_ready", "rows_used", "norm_stats", "norm_rows",
                 "norm_scale", "input_hi", "input_lo", "scores_step", "score_rows", "mask_rows",
                 "relu_rows", "masked", "exp_ready", "prob_step", "prob_ready", "x_bias", "att_hi",
                 "att_lo", "elu_step", "elu_relu", "elu_exp", "x2_hi", "x2_lo", "dve_step", "count_step",
                 "bounds_step", "bounds", "count_rows", "edge_sums", "graph", "pool_const", "pool_step",
                 "x_added", "embed", "embed_hi", "mean_step"]
        names += [f"onehot{i}" for i in range(EG)] + [f"onehot_used{i}" for i in range(EG)]
        names += [f"x_first{d}" for d in range(NT)]
        dmas = ([f"weight_in{i}" for i in range(LOADS)] + [f"x_in{i}" for i in range(2)]
                + [f"x_out{i}" for i in range(2)] + [f"att_vec{i}" for i in range(2)]
                + ["edges_in", "bias_in", "bias2_in", "small_in", "counts_out0", "counts_out1", "counts_in", "graph_out0",
                   "graph_out1", "graph_in"])
        sems = {n: ctx.enter_context(nc.semaphore(n)) for n in names + dmas}
        G = Signals(sems, known)
        up, at = G.up, G.at

        base = -(-nc.sbuf_base // 32) * 32
        def sb(name, shape, dt, off):
            off = -(-off // 32) * 32
            return nc.alloc_sbuf_tensor_at(name, shape, dt, offset=base + off)
        tile_b = 2 * NP * 4
        XB = sb("XB", [128, 7, 2, NP], F32R, 0)
        o1 = 7 * tile_b
        XA = sb("XA", [128, 9, 2, NP], F32R, o1)
        og = o1 + 9 * tile_b
        def sg(name, shape, dt, size):
            nonlocal og
            t = sb(name, shape, dt, og)
            og += -(-size // 32) * 32
            return t
        Hg = sg("Hg", [P, NT, 2, 1024], F32R, NT * 2 * 1024 * 4)
        AT = sg("AT", [P, NT, 2, NP], F32R, NT * 2 * NP * 4)
        oprob = og
        prob = sg("prob", [P, NT, NP], F32, NT * NP * 4)
        Cg = sg("Cg", [P, NT, NP], U16, NT * NP * 2)
        negm = sg("negm", [P, NT, NP], BF16, NT * NP * 2)
        asb = sg("asb", [P, 2, NP], F32, 2 * NP * 4)
        b2b = sg("b2b", [P, D], F32, D * 4)
        ab = sg("ab", [P, 2, 2, WMAX], F32, 4 * WMAX * 4)
        mx = sg("mx", [P, NT], F32, 32)
        den = sg("den", [P, NT], F32, 32)
        rden = sg("rden", [P, NT], F32, 32)
        asp = sg("asp", [P, 2, 8, NT], F32, 2 * 8 * NT * 4)
        asq = sg("asq", [P, 2, NT], F32, 2 * NT * 4)
        ad8 = sg("ad8", [P, 2, NT], F32, 2 * NT * 4)
        asad = sg("asad", [P, 2, 2, NT], F32, 4 * NT * 4)
        full = sg("full", [P, 4, 256], F32, 4096)
        junk = sg("junk", [P, 2, WMAX], BF16, 4 * WMAX)
        ol = o1 + 7 * tile_b
        MT = sb("MT", [P, R, NT, 2, NP], F32R, ol); ol += R * NT * 2 * NP * 4
        Hl = sb("Hl", [P, NT, R, 2, WMAX], F32R, ol); ol += NT * R * 2 * WMAX * 4
        cr_in = sb("cr_in", [P, NT, R * N], U16, 0)
        mean = sb("mean", [P, NT, N], F32, NT * R * N * 2)
        b3b = sb("b3b", [P, D], F32, 6 * tile_b)
        oc = o1
        def sc(name, shape, dt, size):
            nonlocal oc
            t = sb(name, shape, dt, oc)
            oc += -(-size // 32) * 32
            return t
        CW = R * N + 1
        iota32 = sc("iota32", [P, CW], I32, CW * 4)
        iota16 = sc("iota16", [P, CW], F16, CW * 2)
        srcs = sc("srcs", [P, EG, CW], F16, EG * CW * 2)
        dsts = sc("dsts", [P, EG, 128], F16, EG * 256)
        zero16 = sc("zero16", [1, BANK], F16, BANK * 2)
        gdst32 = sc("gdst32", [NG, EG * P], I32, EG * P * 4)
        gspan = sc("gspan", [NG, 2], F32, 8)
        gid32 = sc("gid32", [NG, 1], I32, 4)
        gid = sc("gid", [NG, 2], F32, 8)
        first32 = sc("first32", [NG, NT], I32, 4 * NT)
        first = sc("first", [NG, 2, NT], F32, 8 * NT)
        touch = sc("touch", [NG, 3, NT], F32, 12 * NT)
        reach = sc("reach", [1, 2, NT], F32, 8 * NT)
        span = sc("span", [1, 4, NT + 1], F32, 16 * NT + 16)
        bounds = sc("bounds", [1, 2, NT + 1], I32, 8 * NT + 8)
        cr = sc("cr", [P, 2, CW], U16, 2 * CW * 2)
        cn = sc("cn", [P, 2, NP], U16, 2 * NP * 2)
        edge32 = sc("edge32", [P, 3, ET], I32, 3 * ET * 4)
        edgef = sc("edgef", [P, 3, ET], F32, 3 * ET * 4)
        cnt = sc("cnt", [P, NT, R], F32, 60)
        cnt1 = sc("cnt1", [P, NT, R], F32, 60)
        got = sc("got", [P, NT, R], F32, 60)
        oc = o1 + 9 * tile_b + 5 * 1024
        x_first = sc("x_first", [P, NT, D], F32, NT * D * 4)
        h_first = sc("h_first", [P, NT, D], F32, NT * D * 4)
        assert oc <= o1 + 9 * tile_b + NT * 2 * 1024 * 4
        oa = -(-max(og, ol) // 32) * 32
        def sa(name, shape, dt, size):
            nonlocal oa
            t = sb(name, shape, dt, oa)
            oa += -(-size // 32) * 32
            return t
        stage = sa("stage", [128, STAGED], F32, STAGED * 4)
        pairs = sa("pairs", [128, 2, SPLIT], F32R, 2 * SPLIT * 4)
        ort = oa
        mn = sa("mn", [128, NP], F32, NP * 4)
        rl = sa("rl", [128, 2, NP], F32, 2 * NP * 4)
        msk = sa("msk", [P, 2, NP], F32, 2 * NP * 4)
        xl = sb("xl", [P, 2, D], F32, ort)
        xo = sb("xo", [P, 2, D], F32, ort + 2 * D * 4)
        assert 4 * D * 4 <= 5 * NP * 4
        hn = sa("hn", [P, D], F32, D * 4)
        ident = sa("ident", [128, 128], F32, 512)
        b1t = sa("b1t", [128, 16], F32, 64)
        bns = sa("bns", [P, 2, 2, 6], F32, 96)
        mv = sa("mv", [P, 2, 2], F32, 16)
        ve = sa("ve", [P, 2, 1], F32, 8)
        rstd = sa("rstd", [P, 2, 1], F32, 8)
        nb = sa("nb", [P, 2, 1], F32, 8)
        mhalf = sa("mhalf", [P, 1], F32, 4)
        inv = sa("inv", [P, NT, R], F32, 60)
        nti = sb("nti", [R, N], I32, oprob)
        ntf = sb("ntf", [R, N], F32, oprob + tile_b)
        nth = sb("nth", [R, NP], F32R, oprob + 2 * tile_b)
        emf = sb("emf", [R, TD], F32, oprob + 3 * tile_b)
        emh = sb("emh", [R, 2, TD], F32R, oprob + 3 * tile_b + 512)
        rid = sb("rid", [R, 1], F32, oprob + 3 * tile_b + 1536)
        rii = sb("rii", [R, 1], I32, oprob + 3 * tile_b + 1568)
        assert base + oa <= nc.sbuf_usable_end, (base + oa, nc.sbuf_usable_end)

        x_scr = nc.dram_tensor("x_scratch", [3, N, D], F32).ap()
        cr_scr = nc.dram_tensor("relation_counts", [N, CW], U16).ap()
        cn_scr = nc.dram_tensor("edge_counts", [N, NP], U16).ap()

        ps = ctx.enter_context(nc.psum_tensor("ps", [128, BANKS * BANK], F32))

        fill_of, place, user = {}, [], {}

        def slot(q):
            s0 = place[q] * BANK
            return ps[:, s0:min(s0 + 2 * BANK, BANKS * BANK)]

        def halves(q, rows, n=HC):
            return slot(q).rearrange("p (c n) -> p c n", c=2)[:rows, :, :n]

        def pitched(q):
            return slot(q)[:P, :NT * 128].rearrange("p (j c) -> p j c", j=NT)[:, :, :P]

        def h2(ap):
            return ap.rearrange("p (c n) -> p c n", c=2)

        def source(s):
            if s[0] == "project":
                return [(XB, k, 128) for k in range(6)]
            if s[0] == "project2":
                if s[1] == 3:
                    return [(XA, k, 96) for k in range(8)]
                return [(XA, k, 128) if k < 9 else (XB, k - 9, 128) for k in range(16)]
            return [((XB if s[1] == 2 else XA), k, 128) for k in range(RGCN_IN[s[1]])]

        def source_ready(s, k):
            if s[0] == "project":
                return ("input lo", s[1], NT - 1)
            if s[0] == "project2":
                return ("x2 lo", s[1], k) if s[1] == 3 else ("x2 lo", s[1], k // 4, k % 4)
            if s[1] == 1:
                return ("embed lo",) if k == 6 else ("input lo", 2, NT - 1)
            c = next(c for c, (f0, w) in enumerate(RGCN_CHUNKS[s[1] - 1]) if f0 <= 128 * k < f0 + w)
            return ("stage lo", s[1] - 1, c, k - RGCN_CHUNKS[s[1] - 1][c][0] // 128)

        def row_dest(s, s0, n, part, w):
            if s[0] == "project":
                c0 = s[2] * w % 1024
                return Hg[:, s0:s0 + n, part, c0:c0 + w]
            if s[0] == "project2":
                return Hg[:, s0:s0 + n, part, s[2] * w:s[2] * w + w]
            return Hl[:, s0:s0 + n, s[3], part, :w]

        def copied(s, g):
            return s[0] == "project" and s[-1] == 256 and g == 0

        def psum_rows(q, n, pitch, w):
            return slot(q)[:P, :n * pitch].rearrange("p (n c) -> p n c", n=n)[:, :, :w]

        def att_of(l, h):
            return XB if l == 3 and h % 2 else AT

        gat_projects = [s for s in STEPS if s[0] in ("project", "project2")]
        narrow_projects = [s for s in gat_projects if s[0] == "project" and s[-1] == 256]

        def pieces(s):
            if s[0] == "project" and s[1] == 3:
                return [(4 * s[2] + i, 96 * i, 96) for i in range(4)]
            return [(s[2] if s[0] == "project2" else s[2] % 2, 0, s[3])]

        def last_piece(s):
            _, l, h = s
            heads = GAT_HEADS[l][0]
            if h == heads:
                return ("project2", l, 2, 256)
            return ("project", l, 2 * h + 1, 256) if l < 3 else ("project", l, h // 4, 384)

        heads_order = {s[1:]: i for i, s in enumerate(x for x in STEPS if x[0] == "scores")}
        soft_order = {s[1:]: i for i, s in enumerate(x for x in STEPS if x[0] == "softmax")}
        agg_order = {s[1:]: i for i, s in enumerate(x for x in STEPS if x[0] == "aggregate")}
        agg_list = list(agg_order)
        norm_order = {s[1:]: i for i, s in enumerate(x for x in STEPS if x[0] == "norm_T")}
        norm_list = list(norm_order)
        norm_of = {("load_x", d): (0, d) for d in range(NT)}
        norm_of.update({("output", l, d): (l + 1, d) for l in (0, 1) for d in range(NT)})
        norm_of.update({("row_part", 1, d): (3, d) for d in range(NT)})
        xr_keys = ([("load_x", d) for d in range(NT)] + [("output", 0, d) for d in range(NT)]
                   + [("output", 1, d) for d in range(NT)] + [("row_part", c, d) for c in range(2) for d in range(NT)]
                   + [("output", 3, d) for d in range(NT)])
        xr = {k: i for i, k in enumerate(xr_keys)}
        combine_order = {s: i for i, s in enumerate(x for x in STEPS if x[0] == "combine")}
        combine_list = list(combine_order)

        def agg_key(l, h, f):
            return (l, h, f) if l < 3 else (l, h)

        def x2_place(l, h, f):
            if l == 3:
                return XA, h
            i = 4 * h + f
            return (XA, i) if i < 9 else (XB, i - 9)

        block = ctx.enter_context(nc.Block())

        @block.tensor
        def _(pe):
            mm = nc.tensor.matmul

            end = [0]

            def acquire(*key, banks=2):
                q = len(place)
                fill_of[key] = q
                start = end[0] if end[0] + banks <= BANKS else 0
                end[0] = start + banks
                place.append(start)
                mine = range(start, start + banks)
                for last_user in sorted({user[b] for b in mine if b in user}):
                    pe.wait_ge(*at("free", last_user))
                for b in mine:
                    user[b] = q
                return q

            pe.wait_ge(*at("ident",))
            for s in STEPS:
                kind = s[0]
                if kind in ("project", "project2", "relation"):
                    w = s[-1]
                    src = source(s)
                    gs = groups(w)
                    qs = []
                    waited = None
                    for k0 in range(0, len(src), 2):
                        block_k = range(k0, min(k0 + 2, len(src)))
                        for g, (s0, ns, pitch) in enumerate(gs):
                            if k0 == 0:
                                qs.append(acquire("rows", s, g, banks=-(-ns * pitch // BANK)))
                            for k in block_k:
                                X, xi, rows = src[k]
                                n = first_tile[s] + k
                                if g == 0:
                                    if source_ready(s, k) != waited:
                                        waited = source_ready(s, k)
                                        pe.wait_ge(*at(*waited))
                                    pe.wait_ge(*at("weights lo", n))
                                for t in range(ns):
                                    o = slot(qs[g])[:P, t * pitch:t * pitch + w]
                                    for i, (a, b) in enumerate(PASSES):
                                        last = mm(o, X[:rows, xi, a, P * (s0 + t):P * (s0 + t + 1)],
                                                  pair(n, b),
                                                  start=k == 0 and i == 0 and t * pitch % BANK == 0,
                                                  stop=k == len(src) - 1 and i == 2, skip_group_check=True)
                                if g == len(gs) - 1 and k < block_k[-1]:
                                    last.then_inc(*up("weights_used", "weights used", n))
                            if block_k[-1] == len(src) - 1:
                                last.then_inc(*up("psum_filled", "filled", "rows", s, g))
                        if block_k[-1] == len(src) - 1:
                            G.same(("filled", "rows", s, len(gs) - 1), "weights used", n)
                        else:
                            last.then_inc(*up("weights_used", "weights used", n))
                elif kind == "spread":
                    q = acquire(*s)
                    pe.wait_ge(*at("scores col", *s[1:]))
                    hb = heads_order[s[1:]] % 2
                    for j in range(NT):
                        last = nc.tensor.transpose(slot(q)[:P, 128 * j:128 * j + P],
                                                   asad[:, hb, 0, j:j + 1].to_broadcast([P, P]), ident[:P, :P])
                    last.then_inc(*up("psum_filled", "filled", *s))
                elif kind in ("attention_T", "mean_T"):
                    M = prob if kind == "attention_T" else mean
                    d = s[-1]
                    q = acquire(*s)
                    pe.wait_ge(*at("rows ready", *s))
                    for j in range(NT):
                        last = nc.tensor.transpose(slot(q)[:P, 128 * j:128 * j + P], M[:, d, P * j:P * j + P],
                                                   ident[:P, :P])
                    last.then_inc(*up("psum_filled", "filled", *s))
                elif kind in ("aggregate", "aggregate_rest"):
                    _, l, h, f = s
                    first_half = kind == "aggregate"
                    key = ("aggregate", l, h, f)
                    q = acquire(*key) if first_half else fill_of[key]
                    m = 128 if l < 3 else 96
                    c0 = h % 2 * 512 + 128 * f if l < 3 else 96 * h
                    for c in ((0, 1) if l < 3 else (0,) if first_half else (1,)):
                        if f == 0:
                            pe.wait_ge(*at("att lo", l, h, 2 + 2 * c))
                        for t in range(NT):
                            for i, (a, b) in enumerate(PASSES):
                                last = mm(halves(q, m)[:, c, :], Hg[:, t, a, c0:c0 + m],
                                          att_of(l, h)[:P, t, b, HC * c:HC * c + HC],
                                          start=t == 0 and i == 0, stop=t == NT - 1 and i == 2)
                    if l < 3 or not first_half:
                        last.then_inc(*up("psum_filled", "filled", *key))
                elif kind == "output":
                    _, l, d = s
                    q = acquire(*s)
                    pe.wait_ge(*at("att lo", l, GAT_HEADS[l][0], d))
                    for c in range(2):
                        for t in range(NT):
                            for i, (a, b) in enumerate(PASSES):
                                last = mm(halves(q, P, 384)[:, c, :], AT[:, t, a, P * d:P * d + P],
                                          Hg[:, t, b, 384 * c:384 * c + 384],
                                          start=t == 0 and i == 0, stop=t == NT - 1 and i == 2)
                    last.then_inc(*up("psum_filled", "filled", *s))
                elif kind == "norm_T":
                    q = acquire(*s)
                    pe.wait_ge(*at("norm rows", *s[1:]))
                    rows = hn if s[1] else h_first[:, s[2]]
                    for k in range(6):
                        c0 = k * P if k < 3 else BANK + (k - 3) * P
                        last = nc.tensor.transpose(slot(q)[:, c0:c0 + P], rows[:, 128 * k:128 * k + 128], ident[:P, :P])
                    last.then_inc(*up("psum_filled", "filled", *s))
                elif kind == "bounds":
                    q = acquire(*s)
                    pe.wait_ge(*at("touched"))
                    for side in range(2):
                        for d in range(NT):
                            c0 = side * BANK + NG * d
                            last = nc.tensor.transpose(slot(q)[:1, c0:c0 + NG], touch[:, 1 + side, d:d + 1],
                                                       ident[:NG, :NG])
                    last.then_inc(*up("psum_filled", "filled", *s))
                elif kind == "count":
                    d = s[1]
                    if d == 0:
                        pe.wait_ge(*at("bounds"))
                        passes = [pe.value_load(bounds[0:1, 0, i:i + 1], min_val=0, max_val=NT * NG)
                                  for i in range(NT + 1)]
                    q = acquire(*s, banks=4)
                    o = ps[:P, place[q] * BANK:(place[q] + 4) * BANK]
                    for c in range(4):
                        last = mm(o[:, BANK * c:BANK * c + BANK], zero16[:, :P], zero16[:, :], start=True,
                                  stop=True, skip_group_check=True)
                        if d == 0:
                            last.then_inc(sems[f"onehot_used{c}"], 1)
                    with pe.Fori(passes[d], passes[d + 1]) as g:
                        for i in range(EG):
                            pe.wait_ge(sems[f"onehot{i}"], g + 1)
                            for c in range(4):
                                c1 = min(BANK * c + BANK, R * N)
                                last = mm(o[:, BANK * c:c1], dsts[:, i, :P], srcs[:, i, BANK * c:c1],
                                          start=False, stop=True, skip_group_check=True)
                            last.then_inc(sems[f"onehot_used{i}"], 1)
                    mm(o[:, :2], zero16[:, :P], zero16[:, :2], start=False, stop=True,
                       skip_group_check=True).then_inc(*up("psum_filled", "filled", *s))
                elif kind == "embed":
                    q = acquire(*s)
                    pe.wait_ge(*at("embed operands",))
                    for c in range(2):
                        for a in range(2):
                            last = mm(halves(q, TD)[:, c, :], emh[:, a, :], nth[:, HC * c:HC * c + HC],
                                      start=a == 0, stop=a == 1)
                    last.then_inc(*up("psum_filled", "filled", *s))
                elif kind == "combine":
                    _, i, c, f = s
                    q = acquire(*s)
                    src = source(("relation", i))
                    for k, (X, xi, rows) in enumerate(src):
                        n = first_tile[s] + k
                        pe.wait_ge(*at("weights lo", n))
                        for half in range(2):
                            for j, (a, b) in enumerate(PASSES):
                                last = mm(halves(q, 128)[:, half, :], pair(n, a),
                                          X[:, xi, b, HC * half:HC * half + HC],
                                          start=k == 0 and j == 0, stop=False)
                        last.then_inc(*up("weights_used", "weights used", n))
                    for r in range(R):
                        if f == 0:
                            g = len(groups(RGCN_CHUNKS[i][c][1])) - 1
                            pe.wait_ge(*at("rows lo", ("relation", i, c, r, RGCN_CHUNKS[i][c][1]), g))
                        if i == 1 and c == 0 and f == 0:
                            pe.wait_ge(*at("mean lo", r, NT - 1))
                        for half in range(2):
                            for t in range(NT):
                                for j, (a, b) in enumerate(PASSES):
                                    last = mm(halves(q, 128)[:, half, :], Hl[:, t, r, a, 128 * f:128 * f + 128],
                                              MT[:, r, t, b, HC * half:HC * half + HC],
                                              start=False, stop=r == R - 1 and t == NT - 1 and j == 2)
                    last.then_inc(*up("psum_filled", "filled", *s))
                elif kind == "combine_rows":
                    c = s[1]
                    gs = groups(384)
                    qs = []
                    src = source(("relation", 3))
                    for k0 in range(0, len(src), 2):
                        for g, (s0, ns, pitch) in enumerate(gs):
                            if k0 == 0:
                                qs.append(acquire("rows", s, g, banks=-(-ns * pitch // BANK)))
                            for k in (k0, k0 + 1):
                                X, xi, rows = src[k]
                                n = first_tile[s] + k
                                if g == 0:
                                    pe.wait_ge(*at("weights lo", n))
                                for t in range(ns):
                                    for j, (a, b) in enumerate(PASSES):
                                        last = mm(slot(qs[g])[:P, t * pitch:t * pitch + 384],
                                                  X[:, xi, a, P * (s0 + t):P * (s0 + t + 1)],
                                                  pair(n, b), start=k == 0 and j == 0, stop=False)
                                if g == len(gs) - 1:
                                    last.then_inc(*up("weights_used", "weights used", n))
                elif kind == "combine_tile":
                    c, d = s[1:]
                    g, t = d // 2, d % 2
                    if d == 0:
                        for r in range(R):
                            pe.wait_ge(*at("rows lo", ("relation", 3, c, r, 384), 2))
                    o = slot(fill_of["rows", ("combine_rows", c), g])[:P, t * BANK:t * BANK + 384]
                    for r in range(R):
                        for u in range(NT):
                            for j, (a, b) in enumerate(PASSES):
                                last = mm(o, MT[:, r, u, a, P * d:P * d + P], Hl[:, u, r, b, :384], start=False,
                                          stop=r == R - 1 and u == NT - 1 and j == 2)
                    last.then_inc(*up("psum_filled", "filled", *s))

        @block.sync
        def _(sp):
            loaded = [0]

            def load_weights(upto):
                while loaded[0] < min(upto, len(W)):
                    n = loaded[0]
                    ap = W[n][0]
                    if stage_before[n] is not None:
                        sp.wait_ge(*at("weights lo", stage_before[n]))
                    sp.dma_start(staged(n), ap).then_inc(
                        *up(f"weight_in{n % LOADS}", "weights in", n, by=16))
                    loaded[0] += 1

            sp.dma_start(gdst32[:, :], I["dst"]).then_inc(*up("edges_in", "targets in", by=16))
            sp.dma_start(edge32[:, :, :], I["edges"]).then_inc(*up("edges_in", "edges in", by=16))
            for s in STEPS:
                if s[0] == "count":
                    d = s[1]
                    sp.wait_ge(*at("relation counts", d))
                    sp.dma_start(cr_scr[P * d:P * d + P, :R * N], cr[:, d % 2, :R * N]).then_inc(
                        *up(f"counts_out{d % 2}", "counts out", d, by=16))
                    sp.wait_ge(*at("edge counts", d))
                    sp.dma_start(cn_scr[P * d:P * d + P, :], cn[:, d % 2, :]).then_inc(
                        *up(f"graph_out{d % 2}", "graph out", d, by=16))
                if s[0] == "count":
                    load_weights(LOADS)
                elif s in tiles_of:
                    load_weights(wend[s] + 12)
            for d in (NT - 2, NT - 1):
                sp.wait_ge(*at("graph out", d))
                sp.wait_ge(*at("counts out", d))

        @block.gpsimd
        def _(pool):
            split = [0]

            def split_lo(upto):
                while split[0] < min(upto, len(W)):
                    n = split[0]
                    pool.wait_ge(*at("weights hi", n))
                    nc.gpsimd.tensor_tensor(pair(n, 1), staged(n), pair(n, 0).bitcast(F32), ALU.subtract).then_inc(
                        *up("weights_lo", "weights lo", n))
                    split[0] += 1

            nc.gpsimd.memset(ident[:, :], 0.0).then_inc(*up("pool_const", "zeros"))
            pool.wait_ge(*at("zeros"))
            nc.gpsimd.affine_select(out=ident[:, :], in_=ident[:, :], compare_op=ALU.not_equal, fill=1.0, base=0,
                                    pattern=[[-1, 128]], channel_multiplier=1).then_inc(*up("pool_const", "ident"))
            nc.gpsimd.iota(iota32[:, :], pattern=[[1, CW]], base=0, channel_multiplier=0).then_inc(
                *up("pool_const", "iota32"))
            nc.gpsimd.iota(gid32[:, :], pattern=[[0, 1]], base=0, channel_multiplier=1)
            nc.gpsimd.iota(first32[:, :], pattern=[[P, NT]], base=0, channel_multiplier=0)
            nc.gpsimd.memset(zero16[:, :], 0.0).then_inc(*up("pool_const", "iota"))
            nc.gpsimd.memset(mhalf[:, :], -0.5).then_inc(*up("pool_const", "mhalf"))
            pool.wait_ge(*at("mhalf"))

            def root(n):
                b = n % 2
                pool.wait_ge(*at("norm stats", n))
                nc.gpsimd.tensor_scalar(ve[:, b, :], mv[:, b, 1:2], EPS, 1.0, ALU.add, ALU.mult).then_inc(
                    *up("pool_step", "variance", n))
                pool.wait_ge(*at("variance", n))
                if n >= 2:
                    pool.wait_ge(*at("norm rows", *norm_list[n - 2]))
                nc.gpsimd.tensor_scalar(nb[:, b, :], mv[:, b, 0:1], -1.0, 1.0, ALU.mult, ALU.mult).then_inc(
                    *up("pool_step", "minus mean", n))
                nc.gpsimd.tensor_tensor(rstd[:, b, :], ve[:, b, :], mhalf[:, :], ALU.pow).then_inc(
                    *up("norm_scale", "norm scale", n))
                pool.wait_ge(*at("minus mean", n))
                pool.wait_ge(*at("norm scale", n))
                nc.gpsimd.tensor_tensor(nb[:, b, :], nb[:, b, :], rstd[:, b, :], ALU.mult).then_inc(
                    *up("norm_scale", "norm shift", n))

            for s in STEPS:
                kind = s[0]
                split_lo(split_limit(s))
                if kind == "mask_rows":
                    l, h, d = s[1:]
                    n = soft_order[s[1:]]
                    pool.wait_ge(*at("score rows", l, h))
                    if n >= 2:
                        pool.wait_ge(*at("masked", n - 2))
                    if h == d == 0:
                        pool.wait_ge(*at("mask", l == 3, NT - 1))
                        if l:
                            for b in range(2):
                                pool.wait_ge(*at("x stored", xr[("output", 0, NT - 1) if l == 1 else
                                                                ("row_part", 1, NT - 1)] - b))
                    nc.gpsimd.tensor_tensor(msk[:, n % 2, :N], asb[:, 1, :N], negm[:, d, :N], ALU.add).then_inc(
                        *up("mask_rows", "mask rows", n))
                elif kind == "softmax" and s[2] < GAT_HEADS[s[1]][0]:
                    l, h, d = s[1:]
                    pool.wait_ge(*at("rden", soft_order[s[1:]]))
                    nc.gpsimd.tensor_scalar(prob[:, d, :N], prob[:, d, :N], rden[:, d:d + 1], 1.0, ALU.mult,
                                            ALU.mult).then_inc(*up("prob_ready", "rows ready", "attention_T", l, h, d))
                elif kind == "output":
                    i = xr[s]
                    pool.wait_ge(*at("b2 in", s[1]))
                    pool.wait_ge(*at("x in", i))
                    nc.gpsimd.tensor_tensor(xl[:, i % 2, :], xl[:, i % 2, :], b2b[:, :], ALU.add).then_inc(
                        *up("x_bias", "x and bias", i))
                elif kind == "embed":
                    nc.gpsimd.iota(rii[:, :], pattern=[[0, 1]], base=0, channel_multiplier=1).then_inc(
                        *up("pool_step", "relation ids"))
                if s in norm_of:
                    root(norm_order[norm_of[s]])

        @block.scalar
        def _(act):
            A = nc.scalar.activation
            split = [0]

            def split_hi(upto):
                while split[0] < min(upto, len(W)):
                    n = split[0]
                    act.wait_ge(*at("weights in", n))
                    if pair_before[n] is not None:
                        act.wait_ge(*at("weights used", pair_before[n]))
                    A(pair(n, 0), staged(n), ACT.Copy).then_inc(
                        *up("weights_hi", "weights hi", n))
                    split[0] += 1

            def load_x(i):
                if i >= len(xr_keys):
                    return
                key = xr_keys[i]
                if i >= 2:
                    act.wait_ge(*at("x read", i - 2))
                kept = key[0] != "load_x" and key[:2] != ("output", 0)
                src = (x_scr[2] if key[:2] == ("output", 3) else
                       x_scr[0] if key[0] == "output" else x_scr[1]) if kept else I["x"]
                d = key[-1]
                c0, w = (0, D)
                if key[:2] == ("row_part", 0):
                    w = 384
                if kept:
                    act.wait_ge(*at("x stored", i - 5))
                act.dma_start(xl[:, i % 2, c0:c0 + w], src[P * d:P * d + P, c0:c0 + w]).then_inc(
                    *up(f"x_in{i % 2}", "x in", i, by=16))

            def load_vectors(i):
                s = gat_projects[i]
                if i >= 2:
                    act.wait_ge(*at("vectors read", i - 2))
                w = s[3]
                for v, name in enumerate(("a1", "a2")[s[0] == "project2"] + x for x in ("src", "dst")):
                    src = I[f"{name}_{s[1]}"][s[2] * w:s[2] * w + w]
                    act.dma_start(ab[:, i % 2, v, :w], src.partition_broadcast(P)).then_inc(
                        *up(f"att_vec{i % 2}", "vectors in", i, v, by=16))

            def store_x(i, ap, dst):
                act.dma_start(dst, ap).then_inc(*up(f"x_out{i % 2}", "x stored", i, by=16))

            def norm_rows(n, x_ap):
                b = n % 2
                act.wait_ge(*at("norm shift", n))
                l, d = norm_list[n]
                if l:
                    act.wait_ge(*at("filled", "norm_T", *norm_list[n - 1]))
                A(hn[:, :] if l else h_first[:, d], x_ap, ACT.Relu, bias=nb[:, b, :], scale=rstd[:, b, :]).then_inc(
                    *up("norm_rows", "norm rows", *norm_list[n]))

            def row_hi(s, w):
                for g, (s0, ns, pitch) in enumerate(groups(w)):
                    act.wait_ge(*at("filled", "rows", s, g))
                    q = fill_of["rows", s, g]
                    A(row_dest(s, s0, ns, 0, w), psum_rows(q, ns, pitch, w), ACT.Copy).then_inc(
                        *up("hi_ready", "rows hi", s, g))
                    if copied(s, g):
                        i = narrow_projects.index(s)
                        if i:
                            act.wait_ge(*at("full read", i - 1))
                        A(full[:, :, :], psum_rows(q, ns, pitch, w), ACT.Copy).then_inc(
                            *up("hi_ready", "rows full", s))
                        G.same(("rows full", s), "free", q)

            def transposed_hi(s, dest, name):
                d = s[-1]
                act.wait_ge(*at("filled", *s))
                A(dest[:P, 0:NT, 0, P * d:P * d + P], pitched(fill_of[s]), ACT.Copy).then_inc(
                    *up("att_hi", name + " hi", *s[1:]))

            act.dma_start(b1t[:, :16], I["b1_0"]).then_inc(*up("bias_in", "b1 in", 0, by=16))
            for d in range(NT):
                act.dma_start(x_first[:, d], I["x"][P * d:P * d + P, :]).then_inc(
                    *up(f"x_first{d}", "x in", d, by=16))
            for s in STEPS:
                kind = s[0]
                split_hi(split_limit(s))
                if kind == "load_x":
                    i = xr[s]
                    norm_rows(s[1], x_first[:, s[1]])
                    G.same(("norm rows", 0, s[1]), "x read", i)
                    if s[1] == NT - 1:
                        load_vectors(0)
                        load_vectors(1)
                elif kind == "count":
                    d = s[1]
                    q = fill_of[s]
                    act.wait_ge(*at("filled", *s))
                    if d >= 2:
                        act.wait_ge(*at("counts out", d - 2))
                        act.wait_ge(*at("edge counts", d - 2))
                    for r in range(R):
                        c0 = place[q] * BANK + N * r
                        A(cr[:, d % 2, N * r:N * r + N], ps[:P, c0:c0 + N], ACT.Copy,
                          accum_out=cnt[:, d, r:r + 1]).then_inc(*up("count_rows", "relation", d, r))
                    G.same(("relation", d, R - 1), "relation counts", d)
                    G.same(("relation", d, R - 1), "free", q)
                elif kind == "norm_T":
                    l, d = s[1:]
                    X = XA if l == 2 else XB
                    act.wait_ge(*at("filled", *s))
                    A(X[:, 0:6, 0, P * d:P * d + P].rearrange("p (b k) c -> p b k c", b=2),
                      halves(fill_of[s], 128, 3 * P).rearrange("p b (k c) -> p b k c", k=3), ACT.Copy).then_inc(
                        *up("input_hi", "input hi", l, d))
                elif kind == "rows":
                    s = s[1]
                    kind = s[0]
                    row_hi(s, s[-1])
                    if kind != "relation":
                        i = gat_projects.index(s)
                        if i + 2 < len(gat_projects) and (gat_projects[i + 2][1] < 3 or s[1] == 3):
                            load_vectors(i + 2)
                        if kind == "project2" and s[2] == 0 and s[1] < 3:
                            act.wait_ge(*at("elu relu", agg_order[s[1], GAT_HEADS[s[1]][0] - 1, 3]))
                            bias = I[f"b1_{s[1] + 1}"]
                            act.dma_start(b1t[:, :bias.shape[1]], bias).then_inc(
                                *up("bias_in", "b1 in", s[1] + 1, by=16))
                elif kind == "scores":
                    l, h = s[1:]
                    n = heads_order[s[1:]]
                    act.wait_ge(*at("filled", "spread", l, h))
                    if n:
                        prev = soft_order[(*list(heads_order)[n - 1], NT - 1)]
                        act.wait_ge(*at("mask rows", prev))
                        act.wait_ge(*at("relu rows", prev))
                    for i, scale in enumerate((1.0, SLOPE)):
                        A(asb[:, i, :N].rearrange("p (j c) -> p j c", j=NT), pitched(fill_of["spread", l, h]), ACT.Copy,
                          scale=scale).then_inc(*up("score_rows", "scores", n, i))
                    G.same(("scores", n, 1), "score rows", l, h)
                    G.same(("scores", n, 1), "free", fill_of["spread", l, h])
                    if h == GAT_HEADS[l][0]:
                        act.wait_ge(*at("x2 lo", *agg_key(*[k for k in agg_list if k[0] == l][-1])))
                        act.dma_start(b2b[:, :], I[f"b2_{l}"].partition_broadcast(P)).then_inc(
                            *up("bias2_in", "b2 in", l, by=16))
                        load_x(xr["output", l, 0])
                elif kind == "mask_rows":
                    l, h, d = s[1:]
                    n = soft_order[s[1:]]
                    act.wait_ge(*at("score rows", l, h))
                    act.wait_ge(*at("target scores", l, h))
                    if n >= NT:
                        act.wait_ge(*at("filled", "attention_T", *list(soft_order)[n - NT]))
                    A(prob[:, d, :N], asb[:, 0, :N], ACT.Relu, bias=ad8[:, heads_order[l, h] % 2, d:d + 1],
                      scale=1 - SLOPE).then_inc(*up("relu_rows", "relu rows", n))
                elif kind == "softmax":
                    l, h, d = s[1:]
                    n = soft_order[s[1:]]
                    act.wait_ge(*at("masked", n))
                    A(prob[:, d, :N], prob[:, d, :N], ACT.Exp, bias=mx[:, d:d + 1], scale=-1.0).then_inc(
                        *up("exp_ready", "exp", n))
                elif kind == "attention_T":
                    l, h, d = s[1:]
                    if d == 0:
                        if l == 3 and h < 2:
                            act.wait_ge(*at("filled", "rows", ("project", 3, 1, 384), 2))
                        elif l == 3:
                            act.wait_ge(*at("filled", "aggregate", l, h - 2, 0))
                        elif h or l:
                            prev = ("aggregate", l, h - 1, 3) if h else ("output", 0, NT - 1)
                            act.wait_ge(*at("filled", *prev))
                    transposed_hi(s, att_of(l, h), "att")
                    if (l, h, d) == (1, 4, NT - 1):
                        act.dma_start(nti[:, :], I["node_type"].partition_broadcast(R)).then_inc(
                            *up("small_in", "types in", by=16))
                        act.dma_start(emf[:, :], I["emb"]).then_inc(*up("small_in", "emb in", by=16))
                elif kind == "mean_T":
                    transposed_hi(s, MT[:, s[1]], "mean")
                elif kind == "elu":
                    l, h, f = s[1:]
                    n = agg_order[s[1:]]
                    m = 128 if l < 3 else 96
                    q = fill_of[("aggregate", *s[1:])]
                    act.wait_ge(*at("elu min", n))
                    bcol = 4 * h + f if l < 3 else h
                    if n >= 2:
                        act.wait_ge(*at("x2 lo", *agg_key(*agg_list[n - 2])))
                    A(h2(rl[:m, n % 2, :]), halves(q, m), ACT.Relu, bias=b1t[:m, bcol:bcol + 1]).then_inc(
                        *up("elu_relu", "elu relu", n))
                    G.same(("elu relu", n), "free", q)
                    A(mn[:m, :], mn[:m, :], ACT.Exp).then_inc(*up("elu_exp", "elu exp", n))
                elif kind == "elu_high":
                    l, h, f = s[1:]
                    n = agg_order[s[1:]]
                    m = 128 if l < 3 else 96
                    act.wait_ge(*at("elu sum", n))
                    X, xi = x2_place(l, h, f)
                    A(X[:m, xi, 0, :], rl[:m, n % 2, :], ACT.Copy).then_inc(*up("x2_hi", "x2 hi", n))
                elif kind == "output":
                    l, d = s[1:]
                    i = xr[s]
                    if (l, d) == (1, 0):
                        act.wait_ge(*at("filled", "rows", ("project2", 1, 2, 256), 1))
                        act.wait_ge(*at("counts out", NT - 1))
                        act.wait_ge(*at("counts out", NT - 2))
                        act.dma_start(cr_in[:, :, :],
                                      cr_scr[:, :R * N].rearrange("(t p) n -> p t n", p=P)).then_inc(
                            *up("counts_in", "counts in", by=16))
                    if d + 1 < NT:
                        load_x(i + 1)
                    if l < 3:
                        n = norm_order[norm_of[s]]
                        norm_rows(n, xo[:, i % 2, :])
                        store_x(i, xo[:, i % 2, :], x_scr[l, P * d:P * d + P, :])
                    else:
                        act.wait_ge(*at("x added", i))
                        store_x(i, xo[:, i % 2, :], out[P * d:P * d + P, :])
                elif kind == "embed":
                    act.wait_ge(*at("filled", *s))
                    A(h2(XA[:TD, 6, 0, :]), halves(fill_of[s], TD), ACT.Copy).then_inc(*up("embed_hi", "embed hi"))
                elif kind == "combine":
                    _, i, c, f = s
                    act.wait_ge(*at("stage relu", *s[1:]))
                    X, xi = (XB if i == 1 else XA), RGCN_CHUNKS[i][c][0] // 128 + f
                    n = combine_order[s]
                    A(X[:, xi, 0, :], rl[:, n % 2, :], ACT.Copy).then_inc(*up("x2_hi", "stage hi", *s[1:]))
                elif kind == "combine_rows":
                    if s[1] == 0:
                        act.wait_ge(*at("stage lo", 2, 1, 2))
                        act.dma_start(b3b[:, :], I["b3_3"].partition_broadcast(P)).then_inc(
                            *up("bias2_in", "b3 in", by=16))
                        load_x(xr["row_part", 0, 0])
                elif kind == "row_part":
                    c, d = s[1:]
                    i = xr[s]
                    if (c, d) != (1, NT - 1):
                        load_x(i + 1)
                    if c == 0:
                        act.wait_ge(*at("x added", i))
                        store_x(i, xo[:, i % 2, :384], x_scr[1, P * d:P * d + P, :384])
                    else:
                        norm_rows(norm_order[(3, d)], xo[:, i % 2, :])
                        store_x(i, xo[:, i % 2, :], x_scr[2, P * d:P * d + P, :])
                elif kind == "graph_again":
                    act.wait_ge(*at("filled", "combine_tile", 1, NT - 1))
                    act.wait_ge(*at("graph out", NT - 2))
                    act.wait_ge(*at("graph out", NT - 1))
                    act.dma_start(Cg[:, :, :], cn_scr.rearrange("(t p) n -> p t n", p=P)).then_inc(
                        *up("graph_in", "graph in", by=16))
                    act.dma_start(b1t[:96, :8], I["b1_3"]).then_inc(*up("bias_in", "b1 in", 3, by=16))
                    load_vectors(len(gat_projects) - 5)
                    load_vectors(len(gat_projects) - 4)
            for b in range(2):
                act.wait_ge(*at("x stored", len(xr_keys) - 1 - b))

        @block.vector
        def _(dve):
            V = nc.vector
            last_tile = None
            junks = [0]

            def stats(n, x_ap):
                b = n % 2
                if n >= 2:
                    dve.wait_ge(*at("norm scale", n - 2))
                for i in range(2):
                    V.bn_stats(bns[:, b, i, :], x_ap[:, 384 * i:384 * i + 384]).then_inc(
                        *up("dve_step", "half stats", n, i))
                dve.wait_ge(*at("half stats", n, 1))
                V.bn_aggr(mv[:, b, :], bns[:, b, :, :].rearrange("p a c -> p (a c)")).then_inc(
                    *up("norm_stats", "norm stats", n))

            def minus_hi(out_ap, whole, hi_ap):
                return V.tensor_tensor(out_ap, whole, hi_ap.bitcast(F32), ALU.subtract)

            def finish_tile():
                nonlocal last_tile
                if last_tile is not None:
                    X, xi, m, b, hi, lo = last_tile
                    dve.wait_ge(*at(*hi))
                    minus_hi(X[:m, xi, 1, :], rl[:m, b, :], X[:m, xi, 0, :]).then_inc(*up("x2_lo", *lo))
                last_tile = None

            def transposed_lo(s, dest, name):
                d = s[-1]
                dve.wait_ge(*at(name + " hi", *s[1:]))
                c = slice(P * d, P * d + P)
                minus_hi(dest[:P, 0:NT, 1, c], pitched(fill_of[s]), dest[:P, 0:NT, 0, c]).then_inc(
                    *up("att_lo", name + " lo", *s[1:]))
                G.same((name + " lo", *s[1:]), "free", fill_of[s])

            def sum_relations(d):
                b = d % 2
                dve.wait_ge(*at("relation counts", d))
                if d >= 2:
                    dve.wait_ge(*at("graph out", d - 2))
                T = V.tensor_tensor
                T(cn[:, b, :N], cr[:, b, :N], cr[:, b, N:2 * N], ALU.add).then_inc(
                    *up("edge_sums", "two relations", d))
                dve.wait_ge(*at("two relations", d))
                T(cn[:, b, :N], cn[:, b, :N], cr[:, b, 2 * N:3 * N], ALU.add).then_inc(
                    *up("edge_sums", "edge counts", d))
                dve.wait_ge(*at("edge counts", d))
                V.tensor_copy(Cg[:, d, :N], cn[:, b, :N]).then_inc(*up("edge_sums", "graph copy", d))
                dve.wait_ge(*at("graph copy", d))
                dve.wait_ge(*at("ident"))
                T(Cg[:, d, P * d:P * d + P], cn[:, b, P * d:P * d + P], ident[:P, :P], ALU.add).then_inc(
                    *up("edge_sums", "graph whole", d))

            def mean_rows(r):
                if r == 0:
                    V.memset(MT[:, :, :, :, N:NP].bitcast(F32), 0.0).then_inc(*up("mean_step", "MT pad"))
                    dve.wait_ge(*at("counts in"))
                for d in range(NT):
                    if r:
                        dve.wait_ge(*at("filled", "mean_T", r - 1, d))
                    V.tensor_scalar(mean[:, d, :], cr_in[:, d, N * r:N * r + N], inv[:, d, r:r + 1], None,
                                    ALU.mult).then_inc(*up("mean_step", "rows ready", "mean_T", r, d))

            def mask(again):
                for d in range(NT):
                    dve.wait_ge(*at("graph whole", d))
                    V.tensor_scalar(negm[:, d, :N], Cg[:, d, :N], 0.0, ABSENT, ALU.is_equal, ALU.mult).then_inc(
                        *up("graph", "mask", again, d))

            V.memset(cn[:, :, N:NP], 0).then_inc(*up("graph", "cn pad"))
            V.memset(AT[:, :, :, N:NP].bitcast(F32), 0.0).then_inc(*up("graph", "AT pad"))
            for s in STEPS:
                kind = s[0]
                if kind not in ("mask_rows", "score_rows", "softmax", "attention_T", "aggregate", "elu", "elu_high", "combine"):
                    finish_tile()
                if kind == "load_x":
                    i = xr[s]
                    dve.wait_ge(*at("x in", i))
                    stats(s[1], x_first[:, s[1]])
                elif kind == "norm_T":
                    l, d = s[1:]
                    X = XA if l == 2 else XB
                    dve.wait_ge(*at("input hi", l, d))
                    c = slice(P * d, P * d + P)
                    minus_hi(X[:, 0:6, 1, c].rearrange("p (b k) c -> p b k c", b=2),
                             halves(fill_of[s], 128, 3 * P).rearrange("p b (k c) -> p b k c", k=3),
                             X[:, 0:6, 0, c].rearrange("p (b k) c -> p b k c", b=2)).then_inc(
                        *up("input_lo", "input lo", l, d))
                    G.same(("input lo", l, d), "free", fill_of[s])
                elif kind == "bounds":
                    n = iter(range(30))

                    def step(instruction):
                        key = ("bounds step", next(n))
                        instruction.then_inc(*up("bounds_step", *key))
                        dve.wait_ge(*at(*key))

                    dve.wait_ge(*at("iota"))
                    V.tensor_copy(iota16[:, :], iota32[:, :]).then_inc(*up("count_step", "iota16"))
                    V.tensor_copy(gid[:, 0:1], gid32[:, :])
                    step(V.tensor_copy(first[:, 0, :], first32[:, :]))
                    V.tensor_scalar(gid[:, 1:2], gid[:, 0:1], 1.0, None, ALU.add)
                    V.tensor_scalar(first[:, 1, :], first[:, 0, :], float(P), None, ALU.add)
                    dve.wait_ge(*at("edges in"))
                    V.tensor_reduce(gspan[:, 0:1], gdst32[:, :], AX.X, ALU.min)
                    step(V.tensor_reduce(gspan[:, 1:2], gdst32[:, :], AX.X, ALU.max))
                    step(V.tensor_scalar(touch[:, 0, :], first[:, 0, :], gspan[:, 1:2], None, ALU.is_le))
                    step(V.scalar_tensor_tensor(out=touch[:, 0, :], in0=first[:, 1, :], scalar=gspan[:, 0:1],
                                                in1=touch[:, 0, :], op0=ALU.is_gt, op1=ALU.mult))
                    V.tensor_scalar(touch[:, 2, :], touch[:, 0, :], gid[:, 1:2], None, ALU.mult)
                    step(V.tensor_scalar(touch[:, 1, :], touch[:, 0, :], gid[:, 0:1], None, ALU.mult))
                    V.scalar_tensor_tensor(out=touch[:, 1, :], in0=touch[:, 0, :], scalar=float(NG),
                                           in1=touch[:, 1, :], op0=ALU.mult, op1=ALU.subtract).then_inc(
                        *up("count_step", "touched"))
                    V.tensor_copy(edgef[:, :, :], edge32[:, :, :]).then_inc(*up("count_step", "edges float"))
                    dve.wait_ge(*at("edges float"))
                    V.scalar_tensor_tensor(out=edgef[:, 0, :], in0=edgef[:, 2, :], scalar=float(N),
                                           in1=edgef[:, 0, :], op0=ALU.mult, op1=ALU.add).then_inc(
                        *up("count_step", "edge keys"))
                    dve.wait_ge(*at("filled", *s))
                    step(V.tensor_reduce(reach[:, :, :],
                                         slot(fill_of[s])[:1, :].rearrange("p (c n) -> p c n", c=2)[
                                             :, :, :NT * NG].rearrange("p c (d g) -> p c d g", d=NT),
                                         AX.X, ALU.max))
                    step(V.tensor_scalar(span[:, 0, :NT], reach[:, 0, :], -1.0, float(NG), ALU.mult, ALU.add))
                    step(V.tensor_scalar(span[:, 0, :NT], span[:, 0, :NT], float(NG - 1), None, ALU.min))
                    step(V.scalar_tensor_tensor(out=span[:, 1, :NT], in0=span[:, 0, :NT], scalar=1.0,
                                                in1=reach[:, 1, :], op0=ALU.add, op1=ALU.max))
                    V.memset(span[:, 2, 0:1], 0.0)
                    step(V.tensor_tensor(span[:, 1, :NT], span[:, 1, :NT], span[:, 0, :NT], ALU.subtract))
                    for d in range(NT):
                        step(V.tensor_tensor(span[:, 2, d + 1:d + 2], span[:, 2, d:d + 1], span[:, 1, d:d + 1],
                                             ALU.add))
                    V.tensor_copy(bounds[:, 0, :], span[:, 2, :])
                    step(V.tensor_tensor(span[:, 3, :NT], span[:, 0, :NT], span[:, 2, :NT], ALU.subtract))
                    V.tensor_copy(bounds[:, 1, :NT], span[:, 3, :NT]).then_inc(*up("bounds", "bounds"))
                    G.same(("bounds",), "free", fill_of[s])
                elif kind == "count":
                    d = s[1]
                    if d == 0:
                        dve.wait_ge(*at("bounds"))
                        passes = [dve.value_load(bounds[0:1, 0, i:i + 1], min_val=0, max_val=NT * NG)
                                  for i in range(NT + 1)]
                        shift_of = [dve.value_load(bounds[0:1, 1, i:i + 1], min_val=-NT * NG, max_val=NG - 1)
                                    for i in range(NT)]
                        dve.wait_ge(*at("edge keys"))
                    with dve.Fori(passes[d], passes[d + 1]) as g:
                        group = nc.s_assert_within(g + shift_of[d], 0, NG - 1, skip_runtime_bounds_check_because=
                                                   "a pass's group lies between its tile's first and last")
                        for i in range(EG):
                            dve.wait_ge(sems[f"onehot_used{i}"], g + 1)
                            V.tensor_scalar(srcs[:, i, :], iota16[:, :], edgef[:, 0, bass.ds(group * EG + i, 1)],
                                            None, ALU.is_equal)
                            V.tensor_scalar(dsts[:, i, :P], iota16[:, P * d:P * d + P],
                                            edgef[:, 1, bass.ds(group * EG + i, 1)], None,
                                            ALU.is_equal).then_inc(sems[f"onehot{i}"], 1)
                    if d:
                        sum_relations(d - 1)
                    if d == NT - 1:
                        sum_relations(d)
                        mask(False)
                        V.tensor_scalar(cnt1[:, :, :], cnt[:, :, :], 1.0, None, ALU.max).then_inc(
                            *up("count_step", "degree floor"))
                        V.tensor_scalar(got[:, :, :], cnt[:, :, :], 1.0, None, ALU.min)
                        dve.wait_ge(*at("degree floor"))
                        V.reciprocal(cnt1[:, :, :], cnt1[:, :, :]).then_inc(*up("count_step", "degree inverse"))
                        dve.wait_ge(*at("degree inverse"))
                        V.tensor_tensor(inv[:, :, :], cnt1[:, :, :], got[:, :, :], ALU.mult).then_inc(
                            *up("count_step", "inverse degrees"))
                elif kind == "rows":
                    s = s[1]
                    kind = s[0]
                    w = s[-1]
                    if kind == "relation" and s[1:3] == (1, 0) and s[3]:
                        mean_rows(s[3])
                    if kind != "relation":
                        i = gat_projects.index(s)
                        dve.wait_ge(*at("vectors in", i, 1))
                    for g, (s0, ns, pitch) in enumerate(groups(w)):
                        q = fill_of["rows", s, g]
                        rows = psum_rows(q, ns, pitch, w)
                        if kind != "relation" and copied(s, g):
                            dve.wait_ge(*at("rows full", s))
                            rows = full[:, :, :]
                        else:
                            dve.wait_ge(*at("rows hi", s, g))
                        last = minus_hi(row_dest(s, s0, ns, 1, w), rows, row_dest(s, s0, ns, 0, w))
                        last.then_inc(*up("lo_ready", "rows lo", s, g))
                        if kind == "relation":
                            G.same(("rows lo", s, g), "free", q)
                            continue
                        for t in range(ns):
                            for part, c0, pw in pieces(s):
                                for v in range(2):
                                    j = junks[0]
                                    junks[0] += 1
                                    if j >= 2:
                                        dve.wait_ge(*at("dot", j - 2))
                                    V.tensor_tensor_reduce(
                                        out=junk[:, j % 2, :pw], in0=rows[:, t, c0:c0 + pw],
                                        in1=ab[:, i % 2, v, c0:c0 + pw], scale=1.0, scalar=0.0, op0=ALU.mult,
                                        op1=ALU.add, accum_out=asp[:, v, part, s0 + t:s0 + t + 1]).then_inc(
                                        *up("rows_used", "dot", j))
                        if copied(s, g):
                            G.same(("dot", junks[0] - 1), "full read", narrow_projects.index(s))
                        else:
                            G.same(("dot", junks[0] - 1), "free", q)
                    if kind != "relation":
                        G.same(("dot", junks[0] - 1), "vectors read", i)
                        G.same(("dot", junks[0] - 1), "dots", s)
                elif kind == "spread":
                    l, h = s[1:]
                    n = heads_order[s[1:]]
                    hb = n % 2
                    heads = GAT_HEADS[l][0]
                    dve.wait_ge(*at("dots", last_piece(s)))
                    if n >= 2:
                        dve.wait_ge(*at("filled", "spread", *list(heads_order)[n - 2]))
                    if h == heads:
                        V.tensor_tensor(asq[:, :, :], asp[:, :, 0, :], asp[:, :, 1, :], ALU.add).then_inc(
                            *up("scores_step", "two parts", l))
                        dve.wait_ge(*at("two parts", l))
                        V.tensor_tensor(asad[:, hb, :, :], asq[:, :, :], asp[:, :, 2, :], ALU.add).then_inc(
                            *up("scores_step", "scores col", l, h))
                    elif l < 3:
                        V.tensor_tensor(asad[:, hb, :, :], asp[:, :, 0, :], asp[:, :, 1, :], ALU.add).then_inc(
                            *up("scores_step", "scores col", l, h))
                    else:
                        V.tensor_copy(asad[:, hb, :, :], asp[:, :, h, :]).then_inc(
                            *up("scores_step", "scores col", l, h))
                    dve.wait_ge(*at("scores col", l, h))
                    if n >= 2:
                        prev = list(heads_order)[n - 2]
                        dve.wait_ge(*at("relu rows", soft_order[(*prev, NT - 1)]))
                    V.tensor_scalar(ad8[:, hb, :], asad[:, hb, 1, :], 1 - SLOPE, None, ALU.mult).then_inc(
                        *up("scores_step", "target scores", l, h))
                elif kind == "score_rows":
                    l, h, d = s[1:]
                    n = soft_order[s[1:]]
                    dve.wait_ge(*at("mask rows", n))
                    dve.wait_ge(*at("relu rows", n))
                    V.tensor_tensor_reduce(out=prob[:, d, :N], in0=prob[:, d, :N], in1=msk[:, n % 2, :N],
                                           scale=-1.0, scalar=-FLOOR, op0=ALU.add, op1=ALU.min,
                                           accum_out=mx[:, d:d + 1]).then_inc(*up("masked", "masked", n))
                elif kind == "softmax":
                    l, h, d = s[1:]
                    n = soft_order[s[1:]]
                    dve.wait_ge(*at("exp", n))
                    V.tensor_tensor_reduce(out=prob[:, d, :N], in0=prob[:, d, :N], in1=Cg[:, d, :N], scale=1.0,
                                           scalar=1e-16, op0=ALU.mult, op1=ALU.add,
                                           accum_out=den[:, d:d + 1]).then_inc(*up("prob_step", "prob mass", n))
                    if h == GAT_HEADS[l][0]:
                        G.same(("prob mass", n), "rows ready", "attention_T", l, h, d)
                    dve.wait_ge(*at("prob mass", n))
                    V.reciprocal(rden[:, d:d + 1], den[:, d:d + 1]).then_inc(*up("prob_step", "rden", n))
                elif kind == "attention_T":
                    transposed_lo(s, att_of(*s[1:3]), "att")
                elif kind == "mean_T":
                    transposed_lo(s, MT[:, s[1]], "mean")
                elif kind == "elu":
                    l, h, f = s[1:]
                    n = agg_order[s[1:]]
                    m = 128 if l < 3 else 96
                    q = fill_of[("aggregate", *s[1:])]
                    bcol = 4 * h + f if l < 3 else h
                    dve.wait_ge(*at("b1 in", l))
                    dve.wait_ge(*at("filled", "aggregate", *s[1:]))
                    if n:
                        dve.wait_ge(*at("elu sum", n - 1))
                    if (h, f) == (0, 0) and l:
                        for b in range(2):
                            dve.wait_ge(*at("x stored", xr[("output", 0, NT - 1) if l == 1 else
                                                           ("row_part", 1, NT - 1)] - b))
                    V.tensor_scalar(h2(mn[:m, :]), halves(q, m), b1t[:m, bcol:bcol + 1], 0.0, ALU.add,
                                    ALU.min).then_inc(*up("elu_step", "elu min", n))
                elif kind == "elu_sum":
                    l, h, f = s[1:]
                    n = agg_order[s[1:]]
                    m = 128 if l < 3 else 96
                    dve.wait_ge(*at("elu exp", n))
                    V.scalar_tensor_tensor(out=rl[:m, n % 2, :], in0=mn[:m, :], scalar=-1.0, in1=rl[:m, n % 2, :],
                                           op0=ALU.add, op1=ALU.add).then_inc(*up("elu_step", "elu sum", n))
                    last_tile = (*x2_place(l, h, f), m, n % 2, ("x2 hi", n), ("x2 lo", *agg_key(l, h, f)))
                elif kind == "output":
                    l, d = s[1:]
                    i = xr[s]
                    q = fill_of[s]
                    dve.wait_ge(*at("x and bias", i))
                    dve.wait_ge(*at("filled", *s))
                    if d >= 2:
                        dve.wait_ge(*at("x stored", i - 2))
                        if l < 3:
                            dve.wait_ge(*at("norm rows", l + 1, d - 2))
                    if d == 0:
                        dve.wait_ge(*at("masked", soft_order[l, GAT_HEADS[l][0], NT - 1]))
                    V.scalar_tensor_tensor(out=xo[:, i % 2, :].rearrange("p (c n) -> p c n", c=2),
                                           in0=halves(q, P, 384), scalar=rden[:, d:d + 1],
                                           in1=xl[:, i % 2, :].rearrange("p (c n) -> p c n", c=2), op0=ALU.mult,
                                           op1=ALU.add).then_inc(*up("x_added", "x added", i))
                    G.same(("x added", i), "free", q)
                    G.same(("x added", i), "x read", i)
                    if l < 3:
                        dve.wait_ge(*at("x added", i))
                        n = norm_order[norm_of[s]]
                        stats(n, xo[:, i % 2, :])
                elif kind == "embed":
                    dve.wait_ge(*at("emb in"))
                    V.tensor_copy(ntf[:, :], nti[:, :]).then_inc(*up("embed", "types float"))
                    V.memset(nth[:, N:NP].bitcast(F32), 0.0).then_inc(*up("embed", "types pad"))
                    dve.wait_ge(*at("relation ids"))
                    V.tensor_copy(rid[:, :], rii[:, :]).then_inc(*up("embed", "ids float"))
                    V.tensor_copy(emh[:, 0, :], emf[:, :]).then_inc(*up("embed", "emb hi"))
                    dve.wait_ge(*at("emb hi"))
                    minus_hi(emh[:, 1, :], emf[:, :], emh[:, 0, :])
                    V.tensor_scalar(nth[:, :N], ntf[:, :], rid[:, :], None, ALU.is_equal).then_inc(
                        *up("embed", "embed operands"))
                    V.memset(XA[:, 0:6, :, N:NP].bitcast(F32), 0.0).then_inc(*up("embed", "XA pad"))
                    dve.wait_ge(*at("embed hi"))
                    minus_hi(h2(XA[:TD, 6, 1, :]), halves(fill_of[s], TD), h2(XA[:TD, 6, 0, :])).then_inc(
                        *up("embed", "embed lo"))
                    G.same(("embed lo",), "free", fill_of[s])
                    mean_rows(0)
                elif kind == "combine":
                    _, i, c, f = s
                    n = combine_order[s]
                    q = fill_of[s]
                    col = RGCN_CHUNKS[i][c][0] // 128 + f
                    bcol = col + (7 if i == 2 else 0)
                    dve.wait_ge(*at("b1 in", 2))
                    dve.wait_ge(*at("filled", *s))
                    if n < 2:
                        dve.wait_ge(*at("x stored", xr["output", 1, NT - 1 - n]))
                    else:
                        dve.wait_ge(*at("stage lo", *combine_list[n - 2][1:]))
                    V.tensor_scalar(h2(rl[:, n % 2, :]), halves(q, 128), b1t[:, bcol:bcol + 1], 0.0, ALU.add,
                                    ALU.max).then_inc(*up("elu_step", "stage relu", *s[1:]))
                    G.same(("stage relu", *s[1:]), "free", q)
                    finish_tile()
                    last_tile = (XB if i == 1 else XA, col, 128, n % 2, ("stage hi", *s[1:]), ("stage lo", *s[1:]))
                elif kind == "row_part":
                    c, d = s[1:]
                    i = xr[s]
                    g, t = d // 2, d % 2
                    q = fill_of["rows", ("combine_rows", c), g]
                    c0 = 384 * c
                    dve.wait_ge(*at("b3 in"))
                    dve.wait_ge(*at("filled", "combine_tile", c, d))
                    if d >= 2 or c:
                        dve.wait_ge(*at("x stored", i - 2))
                    if c and d >= 2:
                        dve.wait_ge(*at("norm rows", 3, d - 2))
                    xh = xo[:, i % 2, c0:c0 + 384]
                    V.tensor_tensor(xh, slot(q)[:P, t * BANK:t * BANK + 384], b3b[:, c0:c0 + 384],
                                    ALU.add).then_inc(*up("dve_step", "part and bias", c, d))
                    if t == 1 or d == NT - 1:
                        G.same(("part and bias", c, d), "free", q)
                    dve.wait_ge(*at("part and bias", c, d))
                    dve.wait_ge(*at("x in", i))
                    last = V.scalar_tensor_tensor(out=xh, in0=xh, scalar=0.0, in1=xl[:, i % 2, c0:c0 + 384],
                                                  op0=ALU.max, op1=ALU.add)
                    if c:
                        last = V.tensor_copy(xo[:, i % 2, :384], xl[:, i % 2, :384])
                    last.then_inc(*up("x_added", "x added", i))
                    G.same(("x added", i), "x read", i)
                    if c:
                        dve.wait_ge(*at("x added", i))
                        n = norm_order[(3, d)]
                        stats(n, xo[:, i % 2, :])
                elif kind == "graph_again":
                    dve.wait_ge(*at("filled", "combine_tile", 1, NT - 1))
                    V.memset(AT[:, :, :, N:NP].bitcast(F32), 0.0).then_inc(*up("graph", "AT pad again"))
                    dve.wait_ge(*at("graph in"))
                    mask(True)
    return G.seen


def describe(nc, inputs):
    arrays = {}
    for name, a in inputs.items():
        arrays[name] = nc.dram_tensor(f"in_{name}", a.shape, mybir.dt.from_np(a.dtype), kind="ExternalInput").ap()
    return arrays, nc.dram_tensor("out_x", (N, D), F32, kind="ExternalOutput").ap()


def laid_out(k):
    c = np.ascontiguousarray
    edges = np.stack([k["src"], k["dst"], k["edge_type_3"]]).reshape(3, ET, P)
    out = {"x": c(k["x"]), "edges": c(edges.transpose(2, 0, 1)), "dst": c(k["dst"].reshape(NG, EG * P)),
           "node_type": c(k["node_type_3"]),
           "emb": c(k["L2_gnn_node_emb"])}
    names = {0: ("a1_src", "a1_dst", "a2_src", "a2_dst"), 1: ("att_src1", "att_dst1", "att_src2", "att_dst2"),
             3: ("a_src1", "a_dst1", "a_src2", "a_dst2")}
    for l, (s1, d1, s2, d2) in names.items():
        g = f"L{l}_gnn_"
        rows = 128 if l < 3 else 96
        out[f"W1_{l}"], out[f"W2_{l}"] = c(k[g + "W1"]), c(k[g + "W2"])
        out[f"a1src_{l}"], out[f"a1dst_{l}"] = c(k[g + s1].reshape(-1)), c(k[g + d1].reshape(-1))
        out[f"a2src_{l}"], out[f"a2dst_{l}"] = c(k[g + s2].reshape(-1)), c(k[g + d2].reshape(-1))
        out[f"b1_{l}"] = c(k[g + "b1"].reshape(-1, rows).T)
        out[f"b2_{l}"] = c(k[g + "b2"])
    for i in (1, 2, 3):
        out[f"rel_{i}"], out[f"root_{i}"] = c(k[f"L2_gnn_w_rel{i}"]), c(k[f"L2_gnn_w_root{i}"])
    out["b1_2"] = c(np.concatenate([k["L2_gnn_b1"].reshape(-1, 128).T, k["L2_gnn_b2"].reshape(-1, 128).T], axis=1))
    out["b3_3"] = c(k["L2_gnn_b3"])
    return out


def kernel(**inputs):
    import concourse.bacc as bacc
    from concourse.bass_utils import run_bass_kernel_spmd

    arrays = laid_out({n: np.asarray(a) for n, a in inputs.items()})
    known = {}
    for _ in range(2):
        nc = bacc.Bacc("TRN2", target_bir_lowering=False, num_devices=1, dynamic_dma_scratch_size=SCRATCH)
        I, out = describe(nc, arrays)
        known = build(nc, I, out, known)
    r = run_bass_kernel_spmd(nc, [{f"in_{n}": a for n, a in arrays.items()}], core_ids=[0])
    return r.results[0]["out_x"]
```
